# Optimizing a Trainium2 kernel written in Bass

```python
import numpy as np
import jax
import jax.numpy as jnp

def _softmax(x, axis=-1):
    return jax.nn.softmax(x, axis=axis)

def _gelu(x):
    return jax.nn.gelu(x, approximate=True)

def _silu(x):
    return jax.nn.silu(x)

def _sigmoid(x):
    return jax.nn.sigmoid(x)

def _layernorm(x, axis=-1, eps=1e-05):
    m = jnp.mean(x, axis=axis, keepdims=True)
    v = jnp.var(x, axis=axis, keepdims=True)
    return (x - m) / jnp.sqrt(v + eps)

def _scatter_add(tgt, idx, src, axis=0):
    return tgt.at[idx].add(src)

def _segment_sum(src, seg, n):
    return jax.ops.segment_sum(src, seg, n)
kernel_name = 'mk_seq_postln_d2_jaxref_r8_ebc5c9'

def setup_inputs(seed: int=0):
    np.random.seed(seed)
    _w = jnp.asarray

    def _L0_attn_setup():
        import jax, jax.numpy as jnp
        import numpy as np
        B, L = (4, 256)
        D_MODEL, D_STATE, D_CONV, EXPAND = (128, 64, 4, 2)
        D_INNER = D_MODEL * EXPAND
        key = jax.random.key(seed)
        ks = jax.random.split(key, 10)
        s = 0.02
        return {'x': jax.random.normal(ks[0], (B, L, D_MODEL), jnp.float32), 'W_in': jax.random.normal(ks[1], (D_INNER, D_MODEL), jnp.float32) * s, 'b_in': jnp.zeros((D_INNER,), jnp.float32), 'conv_w': jax.random.normal(ks[2], (D_INNER, 1, D_CONV), jnp.float32) * s, 'conv_b': jnp.zeros((D_INNER,), jnp.float32), 'W_x': jax.random.normal(ks[3], (D_STATE, D_INNER), jnp.float32) * s, 'b_x': jnp.zeros((D_STATE,), jnp.float32), 'W_dt': jax.random.normal(ks[4], (D_STATE, D_INNER), jnp.float32) * s, 'b_dt': jnp.zeros((D_STATE,), jnp.float32), 'A_log': jax.random.normal(ks[5], (D_STATE,), jnp.float32) * 0.5, 'D_mat': jax.random.normal(ks[6], (D_STATE, D_INNER), jnp.float32) * s, 'W_out': jax.random.normal(ks[7], (D_MODEL, D_INNER), jnp.float32) * s, 'b_out': jnp.zeros((D_MODEL,), jnp.float32)}
    _L0_attn_in = _L0_attn_setup()

    def _L0_ffn_setup():
        import jax, jax.numpy as jnp
        import numpy as np
        H = 128
        I = 512
        E = 8
        K = 2
        B, S = (2, 256)

        def _moe_linear(x, router_w, expert_w):
            n_exp = router_w.shape[0]
            logits = x @ router_w.T
            vals, idx = jax.lax.top_k(logits, K)
            probs = jax.nn.softmax(vals, axis=-1)
            onehot = jax.nn.one_hot(idx, n_exp, dtype=x.dtype)
            combine = jnp.einsum('tk,tke->te', probs, onehot)
            out = jnp.zeros((x.shape[0], expert_w.shape[1]), x.dtype)
            for e in range(n_exp):
                out = out + combine[:, e:e + 1] * (x @ expert_w[e].T)
            return out
        key = jax.random.key(seed)
        ks = jax.random.split(key, 7)
        init = lambda k, shape, fan_in: jax.random.normal(k, shape, jnp.float32) / np.float32(np.sqrt(fan_in))
        return {'x': jax.random.normal(ks[0], (B, S, H), jnp.float32), 'router_gate': init(ks[1], (E, H), H), 'w_gate': init(ks[2], (E, I, H), H), 'router_up': init(ks[3], (E, H), H), 'w_up': init(ks[4], (E, I, H), H), 'router_down': init(ks[5], (E, I), I), 'w_down': init(ks[6], (E, H, I), I)}
    _L0_ffn_in = _L0_ffn_setup()

    def _L1_attn_setup():
        import jax, jax.numpy as jnp
        import numpy as np
        D_MODEL, D_STATE, D_CONV, EXPAND = (128, 16, 4, 2)
        D_INNER = EXPAND * D_MODEL
        B, L = (2, 512)
        LN_EPS = 1e-05

        def _layernorm(x, gamma, beta):
            mu = jnp.mean(x, axis=-1, keepdims=True)
            var = jnp.mean(jnp.square(x - mu), axis=-1, keepdims=True)
            return (x - mu) * jax.lax.rsqrt(var + LN_EPS) * gamma + beta

        def _causal_depthwise_conv(xp, conv_w, conv_b):
            lhs = jnp.pad(xp.transpose(0, 2, 1), ((0, 0), (0, 0), (D_CONV - 1, 0)))
            out = jax.lax.conv_general_dilated(lhs, conv_w, window_strides=(1,), padding='VALID', dimension_numbers=('NCH', 'OIH', 'NCH'), feature_group_count=D_INNER)
            return out.transpose(0, 2, 1) + conv_b
        key = jax.random.key(seed)
        ks = jax.random.split(key, 6)
        x = jax.random.normal(ks[0], (B, L, D_MODEL), dtype=jnp.float32)
        ln_gamma = jnp.ones((D_MODEL,), jnp.float32)
        ln_beta = jnp.zeros((D_MODEL,), jnp.float32)
        W_in = jax.random.normal(ks[1], (2 * D_INNER, D_MODEL), jnp.float32) / np.sqrt(D_MODEL).astype(np.float32)
        conv_w = jax.random.normal(ks[2], (D_INNER, 1, D_CONV), jnp.float32) * 0.1
        conv_b = jnp.zeros((D_INNER,), jnp.float32)
        W_out = jax.random.normal(ks[3], (D_MODEL, D_INNER), jnp.float32) / np.sqrt(D_INNER).astype(np.float32)
        A = jnp.eye(D_STATE, dtype=jnp.float32)
        Bm = jax.random.normal(ks[4], (D_STATE, D_INNER), jnp.float32) * 0.01
        Cm = jax.random.normal(ks[5], (D_STATE, D_INNER), jnp.float32) * 0.01
        return dict(x=x, ln_gamma=ln_gamma, ln_beta=ln_beta, W_in=W_in, conv_w=conv_w, conv_b=conv_b, W_out=W_out, A=A, Bm=Bm, Cm=Cm)
    _L1_attn_in = _L1_attn_setup()

    def _L1_ffn_setup():
        import jax, jax.numpy as jnp
        import numpy as np
        DIM = 128
        DEPTH = 6
        HEADS = 16
        DIM_HEAD = 64
        WINDOW = 32
        INNER = HEADS * DIM_HEAD
        DIM_INNER = int(DIM * 4 * 2 / 3)
        QK_SCALE = 8.0

        def shift_tokens(t):
            a, s = jnp.split(t, 2, -1)
            s = jnp.pad(s, ((0, 0), (1, 0), (0, 0)))[:, :-1]
            return jnp.concatenate([a, s], -1)

        def l2norm(t):
            return t / jnp.maximum(jnp.linalg.norm(t, axis=-1, keepdims=True), 1e-12)

        def rotate_half(x):
            x1, x2 = jnp.split(x, 2, -1)
            return jnp.concatenate([-x2, x1], -1)

        def rotary_tables(n):
            half = jnp.arange(0, DIM_HEAD, 2, dtype=jnp.float32)
            inv_freq = 1.0 / 10000.0 ** (half / DIM_HEAD)
            t = jnp.arange(n, dtype=jnp.float32)
            freqs = t[:, None] * inv_freq[None, :]
            freqs = jnp.concatenate([freqs, freqs], -1)
            base_scale = (half + 0.4 * DIM_HEAD) / (1.4 * DIM_HEAD)
            power = (t - n // 2) / (WINDOW // 2)
            scale = base_scale[None, :] ** power[:, None]
            scale = jnp.concatenate([scale, scale], -1)
            return (freqs, scale)

        def local_attention(q, k, v):
            b, h, n, d = q.shape
            w = WINDOW
            nw = n // w
            bq = q.reshape(b, h, nw, w, d)
            bk = k.reshape(b, h, nw, w, d)
            bv = v.reshape(b, h, nw, w, d)

            def look(t):
                p = jnp.pad(t, ((0, 0), (0, 0), (1, 0), (0, 0), (0, 0)))
                return jnp.concatenate([p[:, :, :nw], p[:, :, 1:]], axis=3)
            bk2, bv2 = (look(bk), look(bv))
            seq = jnp.arange(n).reshape(nw, w)
            seq_p = jnp.pad(seq, ((1, 0), (0, 0)), constant_values=-1)
            jt = jnp.concatenate([seq_p[:nw], seq_p[1:]], axis=1)
            it = seq[:, :, None]
            jb = jt[:, None, :]
            mask = (it < jb) | (it > jb + w) | (jb == -1)
            sim = jnp.einsum('bhwie,bhwje->bhwij', bq, bk2) * QK_SCALE
            sim = jnp.where(mask, -jnp.finfo(sim.dtype).max, sim)
            attn = jax.nn.softmax(sim, -1)
            out = jnp.einsum('bhwij,bhwje->bhwie', attn, bv2)
            return out.reshape(b, h, n, d)

        def attn_layer(x, Wqkv, qs, ksc, Wo):
            b, n, _ = x.shape
            qkv = x @ Wqkv
            q, k, v = jnp.split(qkv, 3, -1)
            sh = lambda t: t.reshape(b, n, HEADS, DIM_HEAD).transpose(0, 2, 1, 3)
            q, k, v = (sh(q), sh(k), sh(v))
            q = l2norm(q) * qs
            k = l2norm(k) * ksc
            freqs, scale = rotary_tables(n)
            cos, sin = (jnp.cos(freqs), jnp.sin(freqs))
            q = q * cos * scale + rotate_half(q) * sin * scale
            inv = 1.0 / scale
            k = k * cos * inv + rotate_half(k) * sin * inv
            out = local_attention(q, k, v)
            out = out.transpose(0, 2, 1, 3).reshape(b, n, INNER)
            return out @ Wo

        def ffn_layer(x, g, bln, W1, b1, W2, b2):
            mu = x.mean(-1, keepdims=True)
            var = ((x - mu) ** 2).mean(-1, keepdims=True)
            xn = (x - mu) / jnp.sqrt(var + 1e-05) * g + bln
            hg = xn @ W1 + b1
            a, gate = jnp.split(hg, 2, -1)
            return a * jax.nn.gelu(gate, approximate=False) @ W2 + b2
        key = jax.random.key(seed)
        ks = jax.random.split(key, 8)
        B, N = (2, 256)
        init = lambda k, shape: jax.random.normal(k, shape, jnp.float32) * 0.02
        return {'x': jax.random.normal(ks[0], (B, N, DIM), jnp.float32), 'Wqkv': init(ks[1], (DEPTH, DIM, 3 * INNER)), 'q_scale': jnp.ones((DEPTH, DIM_HEAD), jnp.float32), 'k_scale': jnp.ones((DEPTH, DIM_HEAD), jnp.float32), 'Wo': init(ks[2], (DEPTH, INNER, DIM)), 'ln_g': jnp.ones((DEPTH, DIM), jnp.float32), 'ln_b': jnp.zeros((DEPTH, DIM), jnp.float32), 'W1': init(ks[3], (DEPTH, DIM, 2 * DIM_INNER)), 'b1': jnp.zeros((DEPTH, 2 * DIM_INNER), jnp.float32), 'W2': init(ks[4], (DEPTH, DIM_INNER, DIM)), 'b2': jnp.zeros((DEPTH, DIM), jnp.float32)}
    _L1_ffn_in = _L1_ffn_setup()
    _d = {'L0_attn_x': _L0_attn_in['x'], 'L0_attn_W_in': _L0_attn_in['W_in'], 'L0_attn_b_in': _L0_attn_in['b_in'], 'L0_attn_conv_w': _L0_attn_in['conv_w'], 'L0_attn_conv_b': _L0_attn_in['conv_b'], 'L0_attn_W_x': _L0_attn_in['W_x'], 'L0_attn_b_x': _L0_attn_in['b_x'], 'L0_attn_W_dt': _L0_attn_in['W_dt'], 'L0_attn_b_dt': _L0_attn_in['b_dt'], 'L0_attn_A_log': _L0_attn_in['A_log'], 'L0_attn_D_mat': _L0_attn_in['D_mat'], 'L0_attn_W_out': _L0_attn_in['W_out'], 'L0_attn_b_out': _L0_attn_in['b_out'], 'L0_ffn_router_gate': _L0_ffn_in['router_gate'], 'L0_ffn_w_gate': _L0_ffn_in['w_gate'], 'L0_ffn_router_up': _L0_ffn_in['router_up'], 'L0_ffn_w_up': _L0_ffn_in['w_up'], 'L0_ffn_router_down': _L0_ffn_in['router_down'], 'L0_ffn_w_down': _L0_ffn_in['w_down'], 'L1_attn_ln_gamma': _L1_attn_in['ln_gamma'], 'L1_attn_ln_beta': _L1_attn_in['ln_beta'], 'L1_attn_W_in': _L1_attn_in['W_in'], 'L1_attn_conv_w': _L1_attn_in['conv_w'], 'L1_attn_conv_b': _L1_attn_in['conv_b'], 'L1_attn_W_out': _L1_attn_in['W_out'], 'L1_attn_A': _L1_attn_in['A'], 'L1_attn_Bm': _L1_attn_in['Bm'], 'L1_attn_Cm': _L1_attn_in['Cm'], 'L1_ffn_Wqkv': _L1_ffn_in['Wqkv'], 'L1_ffn_q_scale': _L1_ffn_in['q_scale'], 'L1_ffn_k_scale': _L1_ffn_in['k_scale'], 'L1_ffn_Wo': _L1_ffn_in['Wo'], 'L1_ffn_ln_g': _L1_ffn_in['ln_g'], 'L1_ffn_ln_b': _L1_ffn_in['ln_b'], 'L1_ffn_W1': _L1_ffn_in['W1'], 'L1_ffn_b1': _L1_ffn_in['b1'], 'L1_ffn_W2': _L1_ffn_in['W2'], 'L1_ffn_b2': _L1_ffn_in['b2']}
    _x0 = _d['L0_attn_x']
    _d['L0_attn_x'] = jax.random.normal(jax.random.fold_in(jax.random.key(seed), 1), (16, 256, 128), dtype=_x0.dtype)
    del _x0
    return _d

def reference(L0_attn_x, L0_attn_W_in, L0_attn_b_in, L0_attn_conv_w, L0_attn_conv_b, L0_attn_W_x, L0_attn_b_x, L0_attn_W_dt, L0_attn_b_dt, L0_attn_A_log, L0_attn_D_mat, L0_attn_W_out, L0_attn_b_out, L0_ffn_router_gate, L0_ffn_w_gate, L0_ffn_router_up, L0_ffn_w_up, L0_ffn_router_down, L0_ffn_w_down, L1_attn_ln_gamma, L1_attn_ln_beta, L1_attn_W_in, L1_attn_conv_w, L1_attn_conv_b, L1_attn_W_out, L1_attn_A, L1_attn_Bm, L1_attn_Cm, L1_ffn_Wqkv, L1_ffn_q_scale, L1_ffn_k_scale, L1_ffn_Wo, L1_ffn_ln_g, L1_ffn_ln_b, L1_ffn_W1, L1_ffn_b1, L1_ffn_W2, L1_ffn_b2):

    def _L0_attn_ref(x, W_in, b_in, conv_w, conv_b, W_x, b_x, W_dt, b_dt, A_log, D_mat, W_out, b_out):
        import jax, jax.numpy as jnp
        import numpy as np
        B, L = (4, 256)
        D_MODEL, D_STATE, D_CONV, EXPAND = (128, 64, 4, 2)
        D_INNER = D_MODEL * EXPAND
        Bb, Ll, _ = x.shape
        K = conv_w.shape[-1]
        h = x @ W_in.T + b_in
        h = h.transpose(0, 2, 1)
        h = jax.lax.conv_general_dilated(h, conv_w, window_strides=(1,), padding=[(K - 1, 0)], dimension_numbers=('NCH', 'OIH', 'NCH'), feature_group_count=h.shape[1]) + conv_b[None, :, None]
        h = h.transpose(0, 2, 1)
        x_ssm = h @ W_x.T + b_x
        dt = jax.nn.softplus(h @ W_dt.T + b_dt)
        A = -jnp.exp(A_log)[None, None, :]
        dA = jnp.exp(A * dt)
        dBx = (1.0 - dA) / A * x_ssm

        def step(z, inp):
            da, dbx = inp
            z = da * z + dbx
            return (z, z)
        z0 = jnp.zeros((Bb, dA.shape[-1]), x.dtype)
        _, zs = jax.lax.scan(step, z0, (dA.transpose(1, 0, 2), dBx.transpose(1, 0, 2)))
        z = zs.transpose(1, 0, 2)
        y = jnp.einsum('bls,si->bli', z, D_mat)
        return y @ W_out.T + b_out

    def _L0_ffn_ref(x, router_gate, w_gate, router_up, w_up, router_down, w_down):
        import jax, jax.numpy as jnp
        import numpy as np
        H = 128
        I = 512
        E = 8
        K = 2
        B, S = (2, 256)

        def _moe_linear(x, router_w, expert_w):
            n_exp = router_w.shape[0]
            logits = x @ router_w.T
            vals, idx = jax.lax.top_k(logits, K)
            probs = jax.nn.softmax(vals, axis=-1)
            onehot = jax.nn.one_hot(idx, n_exp, dtype=x.dtype)
            combine = jnp.einsum('tk,tke->te', probs, onehot)
            out = jnp.zeros((x.shape[0], expert_w.shape[1]), x.dtype)
            for e in range(n_exp):
                out = out + combine[:, e:e + 1] * (x @ expert_w[e].T)
            return out
        b, s, h = x.shape
        xt = x.reshape(b * s, h)
        g = _moe_linear(xt, router_gate, w_gate)
        u = _moe_linear(xt, router_up, w_up)
        inter = jax.nn.silu(g) * u
        d = _moe_linear(inter, router_down, w_down)
        return d.reshape(b, s, h)

    def _L1_attn_ref(x, ln_gamma, ln_beta, W_in, conv_w, conv_b, W_out, A, Bm, Cm):
        import jax, jax.numpy as jnp
        import numpy as np
        D_MODEL, D_STATE, D_CONV, EXPAND = (128, 16, 4, 2)
        D_INNER = EXPAND * D_MODEL
        B, L = (2, 512)
        LN_EPS = 1e-05

        def _layernorm(x, gamma, beta):
            mu = jnp.mean(x, axis=-1, keepdims=True)
            var = jnp.mean(jnp.square(x - mu), axis=-1, keepdims=True)
            return (x - mu) * jax.lax.rsqrt(var + LN_EPS) * gamma + beta

        def _causal_depthwise_conv(xp, conv_w, conv_b):
            lhs = jnp.pad(xp.transpose(0, 2, 1), ((0, 0), (0, 0), (D_CONV - 1, 0)))
            out = jax.lax.conv_general_dilated(lhs, conv_w, window_strides=(1,), padding='VALID', dimension_numbers=('NCH', 'OIH', 'NCH'), feature_group_count=D_INNER)
            return out.transpose(0, 2, 1) + conv_b
        xn = _layernorm(x, ln_gamma, ln_beta)
        xz = jnp.einsum('bld,ed->ble', xn, W_in)
        x_part, z = jnp.split(xz, 2, axis=-1)
        x_conv = jax.nn.silu(_causal_depthwise_conv(x_part, conv_w, conv_b))
        u_seq = x_part.transpose(1, 0, 2)
        xc_seq = x_conv.transpose(1, 0, 2)
        z_seq = z.transpose(1, 0, 2)

        def step(state, inp):
            u_t, xc_t, z_t = inp
            state = state @ A.T + u_t @ Bm.T
            out = (xc_t + state @ Cm) * jax.nn.sigmoid(z_t)
            return (state, out)
        state0 = jnp.zeros((x.shape[0], D_STATE), x.dtype)
        _, ys = jax.lax.scan(step, state0, (u_seq, xc_seq, z_seq))
        y = ys.transpose(1, 0, 2)
        residual = jnp.einsum('bli,di->bld', y, W_out)
        return x + residual

    def _L1_ffn_ref(x, Wqkv, q_scale, k_scale, Wo, ln_g, ln_b, W1, b1, W2, b2):
        import jax, jax.numpy as jnp
        import numpy as np
        DIM = 128
        DEPTH = 6
        HEADS = 16
        DIM_HEAD = 64
        WINDOW = 32
        INNER = HEADS * DIM_HEAD
        DIM_INNER = int(DIM * 4 * 2 / 3)
        QK_SCALE = 8.0

        def shift_tokens(t):
            a, s = jnp.split(t, 2, -1)
            s = jnp.pad(s, ((0, 0), (1, 0), (0, 0)))[:, :-1]
            return jnp.concatenate([a, s], -1)

        def l2norm(t):
            return t / jnp.maximum(jnp.linalg.norm(t, axis=-1, keepdims=True), 1e-12)

        def rotate_half(x):
            x1, x2 = jnp.split(x, 2, -1)
            return jnp.concatenate([-x2, x1], -1)

        def rotary_tables(n):
            half = jnp.arange(0, DIM_HEAD, 2, dtype=jnp.float32)
            inv_freq = 1.0 / 10000.0 ** (half / DIM_HEAD)
            t = jnp.arange(n, dtype=jnp.float32)
            freqs = t[:, None] * inv_freq[None, :]
            freqs = jnp.concatenate([freqs, freqs], -1)
            base_scale = (half + 0.4 * DIM_HEAD) / (1.4 * DIM_HEAD)
            power = (t - n // 2) / (WINDOW // 2)
            scale = base_scale[None, :] ** power[:, None]
            scale = jnp.concatenate([scale, scale], -1)
            return (freqs, scale)

        def local_attention(q, k, v):
            b, h, n, d = q.shape
            w = WINDOW
            nw = n // w
            bq = q.reshape(b, h, nw, w, d)
            bk = k.reshape(b, h, nw, w, d)
            bv = v.reshape(b, h, nw, w, d)

            def look(t):
                p = jnp.pad(t, ((0, 0), (0, 0), (1, 0), (0, 0), (0, 0)))
                return jnp.concatenate([p[:, :, :nw], p[:, :, 1:]], axis=3)
            bk2, bv2 = (look(bk), look(bv))
            seq = jnp.arange(n).reshape(nw, w)
            seq_p = jnp.pad(seq, ((1, 0), (0, 0)), constant_values=-1)
            jt = jnp.concatenate([seq_p[:nw], seq_p[1:]], axis=1)
            it = seq[:, :, None]
            jb = jt[:, None, :]
            mask = (it < jb) | (it > jb + w) | (jb == -1)
            sim = jnp.einsum('bhwie,bhwje->bhwij', bq, bk2) * QK_SCALE
            sim = jnp.where(mask, -jnp.finfo(sim.dtype).max, sim)
            attn = jax.nn.softmax(sim, -1)
            out = jnp.einsum('bhwij,bhwje->bhwie', attn, bv2)
            return out.reshape(b, h, n, d)

        def attn_layer(x, Wqkv, qs, ksc, Wo):
            b, n, _ = x.shape
            qkv = x @ Wqkv
            q, k, v = jnp.split(qkv, 3, -1)
            sh = lambda t: t.reshape(b, n, HEADS, DIM_HEAD).transpose(0, 2, 1, 3)
            q, k, v = (sh(q), sh(k), sh(v))
            q = l2norm(q) * qs
            k = l2norm(k) * ksc
            freqs, scale = rotary_tables(n)
            cos, sin = (jnp.cos(freqs), jnp.sin(freqs))
            q = q * cos * scale + rotate_half(q) * sin * scale
            inv = 1.0 / scale
            k = k * cos * inv + rotate_half(k) * sin * inv
            out = local_attention(q, k, v)
            out = out.transpose(0, 2, 1, 3).reshape(b, n, INNER)
            return out @ Wo

        def ffn_layer(x, g, bln, W1, b1, W2, b2):
            mu = x.mean(-1, keepdims=True)
            var = ((x - mu) ** 2).mean(-1, keepdims=True)
            xn = (x - mu) / jnp.sqrt(var + 1e-05) * g + bln
            hg = xn @ W1 + b1
            a, gate = jnp.split(hg, 2, -1)
            return a * jax.nn.gelu(gate, approximate=False) @ W2 + b2
        for i in range(DEPTH):
            x = attn_layer(shift_tokens(x), Wqkv[i], q_scale[i], k_scale[i], Wo[i]) + x
            x = ffn_layer(shift_tokens(x), ln_g[i], ln_b[i], W1[i], b1[i], W2[i], b2[i]) + x
        return x
    x = L0_attn_x
    x = _layernorm(x + _L0_attn_ref(x, L0_attn_W_in, L0_attn_b_in, L0_attn_conv_w, L0_attn_conv_b, L0_attn_W_x, L0_attn_b_x, L0_attn_W_dt, L0_attn_b_dt, L0_attn_A_log, L0_attn_D_mat, L0_attn_W_out, L0_attn_b_out), axis=-1)
    x = _layernorm(x + _L0_ffn_ref(x, L0_ffn_router_gate, L0_ffn_w_gate, L0_ffn_router_up, L0_ffn_w_up, L0_ffn_router_down, L0_ffn_w_down), axis=-1)
    x = _layernorm(x + _L1_attn_ref(x, L1_attn_ln_gamma, L1_attn_ln_beta, L1_attn_W_in, L1_attn_conv_w, L1_attn_conv_b, L1_attn_W_out, L1_attn_A, L1_attn_Bm, L1_attn_Cm), axis=-1)
    x = _layernorm(x + _L1_ffn_ref(x, L1_ffn_Wqkv, L1_ffn_q_scale, L1_ffn_k_scale, L1_ffn_Wo, L1_ffn_ln_g, L1_ffn_ln_b, L1_ffn_W1, L1_ffn_b1, L1_ffn_W2, L1_ffn_b2), axis=-1)
    return x

_drawn_inputs = setup_inputs


def setup_inputs(seed=0):
    import zlib

    import numpy as np

    out = dict(_drawn_inputs(seed))
    spreads = {'L0_attn_b_in': (0.0, 0.8),
     'L0_attn_conv_b': (0.0, 0.492),
     'L0_attn_b_x': (0.0, 0.1),
     'L0_attn_b_dt': (0.0, 0.8),
     'L0_attn_b_out': (0.0, 0.1),
     'L1_attn_ln_gamma': (1.0, 0.6),
     'L1_attn_ln_beta': (0.0, 0.27),
     'L1_attn_conv_b': (0.0, 0.585),
     'L1_ffn_q_scale': (1.0, 0.6),
     'L1_ffn_k_scale': (1.0, 0.6),
     'L1_ffn_ln_g': (1.0, 0.6),
     'L1_ffn_ln_b': (0.0, 0.8),
     'L1_ffn_b1': (0.0, 0.8),
     'L1_ffn_b2': (0.0, 0.1)}
    factors = {'L0_attn_W_in': 8.0,
     'L0_attn_conv_w': 8.0,
     'L0_attn_W_x': 3.522,
     'L0_attn_W_dt': 8.0,
     'L1_ffn_W1': 3.676,
     'L1_ffn_W2': 3.608}
    for name, (base, spread) in spreads.items():
        noise = np.random.default_rng([zlib.crc32(name.encode()), seed]).standard_normal(out[name].shape)
        drawn = base * np.exp(spread * noise) if base else spread * noise
        out[name] = jnp.asarray(drawn.astype(out[name].dtype))
    for name, factor in factors.items():
        out[name] = (out[name] * factor).astype(out[name].dtype)
    return out
```

```python
from contextlib import ExitStack

import numpy as np
import concourse.bass as bass
from concourse import mybir

F32 = mybir.dt.float32
BF16 = mybir.dt.bfloat16
I32 = mybir.dt.int32
U32 = mybir.dt.uint32
ALU = mybir.AluOpType
ACT = mybir.ActivationFunctionType
AX = mybir.AxisListType

NSEQ, L, D, P = 16, 256, 128, 128
T = L // P
DI = 256
CI = DI // P
TAPS = 4
S0, S1 = 64, 16
NE, FI = 8, 512
CF = FI // P
DEPTH, HEADS, HD, WIN = 6, 16, 64, 32
NW = L // WIN
NG = 4
KEYS = 2 * WIN
HALF = D // 2
HC = 3
EPS = 1e-5
RS = 14
MAGIC = float(0x5F3759DF)


class Steps:

    def __init__(self, ctx, nc, name, steps):
        self.sem = ctx.enter_context(nc.semaphore(name))
        self.index, k = {}, 0
        for s in steps.split():
            s, _, m = s.partition("*")
            k += int(m or 1)
            self.index[s] = k
        self.per = k

    def passed(self, n):
        return n * self.per

    def at(self, step, n, back=0):
        return n * self.per + (self.index[step] - back)


def later(n):
    return not isinstance(n, int) or n > 0


def each_sequence(eng, body):
    body(0)
    with eng.Fori(1, NSEQ) as s:
        body(s)


def at_rest(eng):
    eng.nop(nofuse=True)


def newton_rsqrt(eng, st, n, step, y, var, h, t):
    k = RS
    def own():
        eng.wait_ge(st.sem, st.at(step, n, k))
        at_rest(eng)
    eng.tensor_scalar(h, var, -0.5, 0.0, ALU.mult, ALU.add).then_inc(st.sem, 1)
    eng.tensor_tensor(t, y, y, ALU.mult).then_inc(st.sem, 1)
    k -= 2
    for r in range(3):
        own()
        eng.tensor_tensor(t, t, h, ALU.mult).then_inc(st.sem, 1)
        k -= 1
        own()
        eng.tensor_scalar(t, t, 1.0, 1.5, ALU.mult, ALU.add).then_inc(st.sem, 1)
        k -= 1
        own()
        eng.tensor_tensor(y, y, t, ALU.mult).then_inc(st.sem, 1)
        k -= 1
        own()
        if r < 2:
            eng.tensor_tensor(t, y, y, ALU.mult).then_inc(st.sem, 1)
            k -= 1
    eng.tensor_copy(h, t).then_inc(st.sem, 1)
    k -= 1
    assert k == 0


def layernorm_stats(v, st, n, src, stats, mv, step_in):
    for t in range(T):
        v.bn_stats(stats[:, t, :], src(t)).then_inc(st.sem, 1)
    v.wait_ge(st.sem, st.at(step_in + "bn", n))
    at_rest(v)
    for t in range(T):
        v.bn_aggr(mv[:, t, :], stats[:, t, :]).then_inc(st.sem, 1)


def rsqrt_seed(v, st, n, pre, var, bits):
    v.tensor_scalar(bits, var, 1, None, ALU.logical_shift_right).then_inc(st.sem, 1)
    v.wait_ge(st.sem, st.at(pre + "sh", n))
    v.tensor_scalar(bits, bits, -1.0, MAGIC, ALU.mult, ALU.add).then_inc(st.sem, 1)


def program(nc, I, out):
    top = ExitStack()
    with top:
        X = top.enter_context(nc.sbuf_tensor("X", [P, NSEQ, T, D], F32))
        ident = top.enter_context(nc.sbuf_tensor("ident", [P, P], F32))
        ssm_phase(nc, I, X, ident)
        moe_phase(nc, I, X, ident)
        ssm2_phase(nc, I, X, ident)
        transformer_phase(nc, I, X, ident, out)


def tools(nc):
    ctx = ExitStack()

    def sb(name, shape, dt=F32):
        return ctx.enter_context(nc.sbuf_tensor(name, shape, dt))

    def ps(name, shape, dt=F32):
        return ctx.enter_context(nc.psum_tensor(name, shape, dt))
    return ctx, sb, ps


def ssm_phase(nc, I, X, ident):
    ctx, sb, ps = tools(nc)
    with ctx:
        win = sb("a_win", [P, CI, D])
        wxd = sb("a_wxd", [P, CI, 2 * S0])
        cw = sb("a_cw", [P, CI, TAPS])
        bias_in = sb("a_bias_in", [P, CI, 2])
        svec = sb("a_svec", [S0, 3])
        dmt = sb("a_dmt", [P, CI, S0])
        wot = sb("a_wot", [P, CI, D])
        bout = sb("a_bout", [1, D])
        ind = sb("a_ind", [TAPS + 1, L])
        ones = sb("a_ones", [1, P])
        scaled = sb("a_scaled", [P, CI, TAPS, 2 * S0])
        bsc = sb("a_bsc", [P, CI, TAPS + 1])
        fused = sb("a_fused", [P, TAPS, 2 * S0])
        beta = sb("a_beta", [TAPS + 1, 2 * S0])
        wzo = sb("a_wzo", [S0, D])
        aneg = sb("a_aneg", [S0, 2])
        ealog = sb("a_ealog", [S0, 1])
        xst = sb("a_xst", [P, 2, L])
        xpad = sb("a_xpad", [P, 2, TAPS - 1 + L])
        pre = sb("a_pre", [S0, 4, L])
        dt_ = sb("a_dt", [S0, L])
        dA = sb("a_dA", [S0, L])
        wx = sb("a_wx", [S0, L])
        om = sb("a_om", [S0, L])
        dbx = sb("a_dbx", [S0, L])
        z = sb("a_z", [S0, 2, L])
        res = sb("a_res", [P, T, D])
        stats = sb("a_stats", [P, T, 6])
        mv = sb("a_mv", [P, T, 2])
        ve = sb("a_ve", [P, T])
        y = sb("a_y", [P, T])
        h = sb("a_h", [P, T])
        tt = sb("a_t", [P, T])
        pf = ps("a_pf", [P, 512])
        pb = ps("a_pb", [TAPS + 1, 512])
        px = ps("a_px", [P, 512])
        pu = ps("a_pu", [S0, 512])
        pz = ps("a_pz", [P, 512])
        loaded = ctx.enter_context(nc.semaphore("a_loaded"))
        xl = ctx.enter_context(nc.semaphore("a_xl"))
        pset = ctx.enter_context(nc.semaphore("a_pset"))
        vset = ctx.enter_context(nc.semaphore("a_vset"))
        aset = ctx.enter_context(nc.semaphore("a_aset"))
        gset = ctx.enter_context(nc.semaphore("a_gset"))
        pe = Steps(ctx, nc, "a_pe", "xt u y")
        va = Steps(ctx, nc, "a_va", "pre rel wx om dbx scan res bn*2 ag*2 ve sh sd out*2")
        aa = Steps(ctx, nc, "a_aa", "xpad abs exp ln dA")
        ga = Steps(ctx, nc, "a_ga", f"stage rs*{RS}")
        LOADS = 11
        block = ctx.enter_context(nc.Block())

        @block.sync
        def _(e):
            for dst, src in [(ident[:, :], I["ident"]), (win[:, :, :], I["a_win"]), (wxd[:, :, :], I["a_wxd"]),
                             (cw[:, :, :], I["a_cw"]), (bias_in[:, :, :], I["a_bias_in"]), (svec[:, :], I["a_svec"]),
                             (dmt[:, :, :], I["a_dmt"]), (wot[:, :, :], I["a_wot"]), (bout[:, :], I["a_bout"]),
                             (ind[:, :], I["ind"]), (ones[:, :], I["ones"])]:
                e.dma_start(dst, src).then_inc(loaded, 16)
            e.dma_start(X[:, :, :, :], I["x"]).then_inc(xl, 16)

        @block.gpsimd
        def _(e):
            e.memset(xpad[:, :, 0:TAPS - 1], 0.0).then_inc(gset, 1)
            e.wait_ge(xl, 16)
            def sequence(s):
                if later(s):
                    e.wait_ge(pe.sem, pe.passed(s))
                at_rest(e)
                e.tensor_copy(xst[:, 0, :], X[:, s, :, :].rearrange("p t d -> p (t d)")).then_inc(ga.sem, 1)
                e.wait_ge(va.sem, va.at("sd", s))
                at_rest(e)
                newton_rsqrt(e, ga, s, "rs", y[:, :], ve[:, :], h[:, :], tt[:, :])
            each_sequence(e, sequence)

        @block.vector
        def _(e):
            e.wait_ge(loaded, 16 * LOADS)
            for c in range(CI):
                for k in range(TAPS):
                    e.tensor_scalar(scaled[:, c, k, :], wxd[:, c, :], cw[:, c, k:k + 1], None, ALU.mult).then_inc(vset, 1)
                e.tensor_scalar(bsc[:, c, 0:TAPS], cw[:, c, :], bias_in[:, c, 0:1], None, ALU.mult).then_inc(vset, 1)
                e.tensor_copy(bsc[:, c, TAPS:TAPS + 1], bias_in[:, c, 1:2]).then_inc(vset, 1)
            e.wait_ge(pset, 1)
            e.tensor_copy(fused[:, :, :], pf[:, :].rearrange("p (k m) -> p k m", k=TAPS)).then_inc(vset, 1)
            e.tensor_copy(beta[:, :], pb[:, 0:2 * S0]).then_inc(vset, 1)
            e.wait_ge(pset, 2)
            e.tensor_copy(wzo[:, :], pf[0:S0, 0:D]).then_inc(vset, 1)
            e.wait_ge(aset, 1)
            e.tensor_scalar(aneg[:, 0:1], ealog[:, :], -1.0, None, ALU.mult).then_inc(vset, 1)
            e.wait_ge(vset, CI * (TAPS + 2) + 4)
            e.reciprocal(aneg[:, 1:2], aneg[:, 0:1]).then_inc(vset, 1)
            e.wait_ge(vset, CI * (TAPS + 2) + 5)
            def sequence(s):
                e.wait_ge(pe.sem, pe.at("u", s))
                if later(s):
                    e.wait_ge(aa.sem, aa.passed(s))
                e.tensor_scalar(pre[:, 0, :], pu[:, 0:L], svec[:, 0:1], None, ALU.add).then_inc(va.sem, 1)
                e.wait_ge(aa.sem, aa.at("ln", s))
                e.scalar_tensor_tensor(dt_[:, :], pre[:, 0, :], 0.0, pre[:, 3, :], ALU.max, ALU.add).then_inc(va.sem, 1)
                e.tensor_scalar(wx[:, :], pu[:, L:2 * L], svec[:, 1:2], aneg[:, 1:2], ALU.add, ALU.mult).then_inc(va.sem, 1)
                e.wait_ge(aa.sem, aa.at("dA", s))
                e.tensor_scalar(om[:, :], dA[:, :], -1.0, 1.0, ALU.mult, ALU.add).then_inc(va.sem, 1)
                e.wait_ge(va.sem, va.at("om", s))
                e.tensor_tensor(dbx[:, :], om[:, :], wx[:, :], ALU.mult).then_inc(va.sem, 1)
                e.wait_ge(va.sem, va.at("dbx", s))
                e.tensor_tensor_scan(z[:, 0, :], dA[:, :], dbx[:, :], 0.0, ALU.mult, ALU.add).then_inc(va.sem, 1)
                e.wait_ge(pe.sem, pe.at("y", s))
                e.tensor_tensor(res[:, :, :], X[:, s, :, :], pz[:, 0:L].rearrange("p (t d) -> p t d", t=T), ALU.add)\
                    .then_inc(va.sem, 1)
                e.wait_ge(va.sem, va.at("res", s))
                layernorm_stats(e, va, s, lambda t: res[:, t, :], stats, mv, "")
                e.wait_ge(va.sem, va.at("ag", s))
                e.tensor_scalar(ve[:, :], mv[:, :, 1], EPS, None, ALU.add).then_inc(va.sem, 1)
                e.wait_ge(va.sem, va.at("ve", s))
                rsqrt_seed(e, va, s, "", ve[:, :].bitcast(I32), y[:, :].bitcast(I32))
                e.wait_ge(ga.sem, ga.at("rs", s))
                for t in range(T):
                    e.tensor_scalar(X[:, s, t, :], res[:, t, :], mv[:, t, 0:1], y[:, t:t + 1], ALU.subtract, ALU.mult)\
                        .then_inc(va.sem, 1)
            each_sequence(e, sequence)

        @block.scalar
        def _(e):
            e.wait_ge(loaded, 16 * LOADS)
            e.activation(ealog[:, :], svec[:, 2:3], ACT.Exp).then_inc(aset, 1)
            e.wait_ge(gset, 1)
            e.wait_ge(vset, CI * (TAPS + 2) + 5)
            def sequence(s):
                e.wait_ge(pe.sem, pe.at("xt", s))
                e.activation(xpad[:, 0, TAPS - 1:], px[:, 0:L], ACT.Copy).then_inc(aa.sem, 1)
                e.wait_ge(va.sem, va.at("pre", s))
                e.activation(pre[:, 1, :], pre[:, 0, :], ACT.Abs).then_inc(aa.sem, 1)
                e.wait_ge(aa.sem, aa.at("abs", s))
                e.activation(pre[:, 2, :], pre[:, 1, :], ACT.Exp, scale=-1.0).then_inc(aa.sem, 1)
                e.wait_ge(aa.sem, aa.at("exp", s))
                e.activation(pre[:, 3, :], pre[:, 2, :], ACT.Ln, bias=1.0).then_inc(aa.sem, 1)
                e.wait_ge(va.sem, va.at("rel", s))
                e.activation(dA[:, :], dt_[:, :], ACT.Exp, scale=aneg[:, 0:1]).then_inc(aa.sem, 1)
            each_sequence(e, sequence)

        @block.tensor
        def _(e):
            e.wait_ge(loaded, 16 * LOADS)
            e.wait_ge(vset, CI * (TAPS + 2))
            for k in range(TAPS):
                for c in range(CI):
                    e.matmul(pf[:, k * P:(k + 1) * P], win[:, c, :], scaled[:, c, k, :], start=c == 0, stop=c == CI - 1)
            for c in range(CI):
                m = e.matmul(pb[:, 0:2 * S0], bsc[:, c, :], wxd[:, c, :], start=c == 0, stop=c == CI - 1)
            m.then_inc(pset, 1)
            e.wait_ge(vset, CI * (TAPS + 2) + 2)
            for c in range(CI):
                m = e.matmul(pf[0:S0, 0:D], dmt[:, c, :], wot[:, c, :], start=c == 0, stop=c == CI - 1)
            m.then_inc(pset, 1)
            e.wait_ge(vset, CI * (TAPS + 2) + 3)
            def sequence(s):
                e.wait_ge(ga.sem, ga.at("stage", s))
                if later(s):
                    e.wait_ge(aa.sem, aa.passed(s))
                for t in range(T):
                    m = e.transpose(px[:, t * P:(t + 1) * P], xst[:, 0, t * P:(t + 1) * P], ident[:, :])
                m.then_inc(pe.sem, 1)
                e.wait_ge(aa.sem, aa.at("xpad", s))
                for a in range(2):
                    o = pu[:, a * L:(a + 1) * L]
                    for k in range(TAPS):
                        e.matmul(o, fused[:, k, a * S0:(a + 1) * S0], xpad[:, 0, k:k + L], start=k == 0, stop=False)
                    m = e.matmul(o, beta[:, a * S0:(a + 1) * S0], ind[:, :], start=False, stop=True)
                m.then_inc(pe.sem, 1)
                e.wait_ge(va.sem, va.at("scan", s))
                for t in range(T):
                    o = pz[:, t * P:(t + 1) * P]
                    e.matmul(o, z[:, 0, t * P:(t + 1) * P], wzo[:, :], start=True, stop=False)
                    m = e.matmul(o, ones[:, :], bout[:, :], start=False, stop=True)
                m.then_inc(pe.sem, 1)
            each_sequence(e, sequence)


def moe_phase(nc, I, X, ident):
    ctx, sb, ps = tools(nc)
    with ctx:
        wg = sb("b_wg", [P, NE, FI])
        wu = sb("b_wu", [P, NE, FI])
        wd = sb("b_wd", [P, CF, NE * D])
        rgu = sb("b_rgu", [P, 2 * NE])
        rd = sb("b_rd", [P, CF, NE])
        iota = sb("b_iota", [P, NE])
        xst = sb("b_xst", [P, L])
        xT = sb("b_xT", [P, L])
        lg = sb("b_lg", [P, 3 * T, NE])
        mx = sb("b_mx", [P, 3 * T, 8])
        ix = sb("b_ix", [P, 3 * T, 8], U32)
        ixf = sb("b_ixf", [P, 3 * T, 8])
        df = sb("b_df", [P, 3 * T])
        ex = sb("b_ex", [P, 3 * T])
        sm = sb("b_sm", [P, 3 * T])
        pr = sb("b_pr", [P, 2, 3 * T])
        oh = sb("b_oh", [P, 3 * T, NE])
        o2 = sb("b_o2", [P, 3 * T, NE])
        cb = sb("b_cb", [P, 3 * T, NE])
        xc = sb("b_xc", [P, T, 2 * NE, D])
        xcT = sb("b_xcT", [P, 2 * NE, L])
        sig = sb("b_sig", [P, CF, L])
        it = sb("b_it", [P, CF, L])
        acc = sb("b_acc", [P, T, D])
        stats = sb("b_stats", [P, T, 6])
        mv = sb("b_mv", [P, T, 2])
        ve = sb("b_ve", [P, T])
        y = sb("b_y", [P, T])
        h = sb("b_h", [P, T])
        tt = sb("b_t", [P, T])
        pg = ps("b_pg", [P, CF, L])
        pu = ps("b_pu", [P, CF, L])
        pd = ps("b_pd", [P, NE, D])
        pm = [ps("b_pm0", [P, 512]), ps("b_pm1", [P, 512])]
        loaded = ctx.enter_context(nc.semaphore("b_loaded"))
        pe = Steps(ctx, nc, "b_pe", "xt lg ct*16 g u ld d*2")
        route = "mx{0}*{1} ix{0}*{1} xf{0} df{0} sm{0} p0{0} p1{0} oh{0}*{1} o2{0}*{1} cb{0}"
        va = Steps(ctx, nc, "b_va", "lc " + route.format("g", 2 * T) + f" xc*{T * 2 * NE} gu ldc "
                   + route.format("d", T) + f" acc*{T * NE} bn*2 ag*2 ve sh sd out*2")
        aa = Steps(ctx, nc, "b_aa", "xT exg ctc*16 sig exd")
        ga = Steps(ctx, nc, "b_ga", f"stage rs*{RS}")
        LOADS = 6
        block = ctx.enter_context(nc.Block())

        @block.sync
        def _(e):
            for dst, src in [(rgu[:, :], I["b_rgu"]), (iota[:, :], I["iota"]), (rd[:, :, :], I["b_rd"]),
                             (wg[:, :, :], I["b_wg"]), (wu[:, :, :], I["b_wu"]), (wd[:, :, :], I["b_wd"])]:
                e.dma_start(dst, src).then_inc(loaded, 16)

        @block.gpsimd
        def _(e):
            def sequence(s):
                if later(s):
                    e.wait_ge(pe.sem, pe.passed(s))
                if later(s):
                    e.wait_ge(va.sem, va.passed(s))
                at_rest(e)
                e.tensor_copy(xst[:, :], X[:, s, :, :].rearrange("p t d -> p (t d)")).then_inc(ga.sem, 1)
                e.wait_ge(va.sem, va.at("sd", s))
                at_rest(e)
                newton_rsqrt(e, ga, s, "rs", y[:, :], ve[:, :], h[:, :], tt[:, :])
            each_sequence(e, sequence)

        def top2(e, s, q, a, b):
            at_rest(e)
            for j in range(a, b):
                e.max(mx[:, j, :], lg[:, j, :]).then_inc(va.sem, 1)
            e.wait_ge(va.sem, va.at("mx" + q, s))
            at_rest(e)
            for j in range(a, b):
                e.max_index(ix[:, j, :], mx[:, j, :], lg[:, j, :]).then_inc(va.sem, 1)
            e.wait_ge(va.sem, va.at("ix" + q, s))
            e.tensor_copy(ixf[:, a:b, :], ix[:, a:b, :]).then_inc(va.sem, 1)
            e.tensor_tensor(df[:, a:b], mx[:, a:b, 1], mx[:, a:b, 0], ALU.subtract).then_inc(va.sem, 1)
            e.wait_ge(aa.sem, aa.at("ex" + q, s))
            e.tensor_scalar(sm[:, a:b], ex[:, a:b], 1.0, None, ALU.add).then_inc(va.sem, 1)
            e.wait_ge(va.sem, va.at("sm" + q, s))
            e.reciprocal(pr[:, 0, a:b], sm[:, a:b]).then_inc(va.sem, 1)
            e.wait_ge(va.sem, va.at("p0" + q, s))
            e.tensor_tensor(pr[:, 1, a:b], pr[:, 0, a:b], ex[:, a:b], ALU.mult).then_inc(va.sem, 1)
            e.wait_ge(va.sem, va.at("p1" + q, s))
            for j in range(a, b):
                e.tensor_scalar(oh[:, j, :], iota[:, :], ixf[:, j, 0:1], pr[:, 0, j:j + 1], ALU.is_equal, ALU.mult)\
                    .then_inc(va.sem, 1)
            for j in range(a, b):
                e.tensor_scalar(o2[:, j, :], iota[:, :], ixf[:, j, 1:2], pr[:, 1, j:j + 1], ALU.is_equal, ALU.mult)\
                    .then_inc(va.sem, 1)
            e.wait_ge(va.sem, va.at("o2" + q, s))
            e.tensor_tensor(cb[:, a:b, :], oh[:, a:b, :], o2[:, a:b, :], ALU.add).then_inc(va.sem, 1)
            e.wait_ge(va.sem, va.at("cb" + q, s))

        @block.vector
        def _(e):
            e.wait_ge(loaded, 16 * LOADS)
            def sequence(s):
                e.wait_ge(pe.sem, pe.at("lg", s))
                e.tensor_copy(lg[:, 0:2 * T, :], pm[1][:, 0:2 * T * NE].rearrange("p (j n) -> p j n", n=NE)).then_inc(va.sem, 1)
                e.wait_ge(va.sem, va.at("lc", s))
                top2(e, s, "g", 0, 2 * T)
                for t in range(T):
                    for r in range(2):
                        for n in range(NE):
                            if t == 0 and r == 0 and n == 0:
                                if later(s):
                                    e.wait_ge(pe.sem, pe.passed(s))
                            j = 2 * t + r
                            e.tensor_scalar(xc[:, t, r * NE + n, :], xst[:, t * D:(t + 1) * D], cb[:, j, n:n + 1],
                                            None, ALU.mult).then_inc(va.sem, 1)
                e.wait_ge(aa.sem, aa.at("sig", s))
                e.wait_ge(pe.sem, pe.at("u", s))
                e.tensor_tensor(it[:, :, :], pu[:, :, :], sig[:, :, :], ALU.mult).then_inc(va.sem, 1)
                e.wait_ge(pe.sem, pe.at("ld", s))
                e.tensor_copy(lg[:, 2 * T:3 * T, :], pm[1][:, 0:T * NE].rearrange("p (j n) -> p j n", n=NE)).then_inc(va.sem, 1)
                e.wait_ge(va.sem, va.at("ldc", s))
                top2(e, s, "d", 2 * T, 3 * T)
                for t in range(T):
                    e.wait_ge(pe.sem, pe.at("d", s, T - 1 - t))
                    for n in range(NE):
                        src = xst[:, t * D:(t + 1) * D] if n == 0 else acc[:, t, :]
                        if n:
                            e.wait_ge(va.sem, va.at("acc", s, T * NE - t * NE - n))
                        e.scalar_tensor_tensor(acc[:, t, :], pd[:, n, :], cb[:, 2 * T + t, n:n + 1], src,
                                               ALU.mult, ALU.add).then_inc(va.sem, 1)
                e.wait_ge(va.sem, va.at("acc", s))
                layernorm_stats(e, va, s, lambda t: acc[:, t, :], stats, mv, "")
                e.wait_ge(va.sem, va.at("ag", s))
                e.tensor_scalar(ve[:, :], mv[:, :, 1], EPS, None, ALU.add).then_inc(va.sem, 1)
                e.wait_ge(va.sem, va.at("ve", s))
                rsqrt_seed(e, va, s, "", ve[:, :].bitcast(I32), y[:, :].bitcast(I32))
                e.wait_ge(ga.sem, ga.at("rs", s))
                for t in range(T):
                    e.tensor_scalar(X[:, s, t, :], acc[:, t, :], mv[:, t, 0:1], y[:, t:t + 1], ALU.subtract, ALU.mult)\
                        .then_inc(va.sem, 1)
            each_sequence(e, sequence)

        @block.scalar
        def _(e):
            def sequence(s):
                e.wait_ge(pe.sem, pe.at("xt", s))
                e.activation(xT[:, :], pm[0][:, 0:L], ACT.Copy).then_inc(aa.sem, 1)
                e.wait_ge(va.sem, va.at("dfg", s))
                e.activation(ex[:, 0:2 * T], df[:, 0:2 * T], ACT.Exp).then_inc(aa.sem, 1)
                for n in range(2 * NE):
                    e.wait_ge(pe.sem, pe.at("ct", s, 2 * NE - 1 - n))
                    e.activation(xcT[:, n, :], pm[n % 2][:, 0:L], ACT.Copy).then_inc(aa.sem, 1)
                e.wait_ge(pe.sem, pe.at("g", s))
                e.activation(sig[:, :, :], pg[:, :, :], ACT.Silu).then_inc(aa.sem, 1)
                e.wait_ge(va.sem, va.at("dfd", s))
                e.activation(ex[:, 2 * T:3 * T], df[:, 2 * T:3 * T], ACT.Exp).then_inc(aa.sem, 1)
            each_sequence(e, sequence)

        @block.tensor
        def _(e):
            e.wait_ge(loaded, 16 * LOADS)
            def sequence(s):
                e.wait_ge(ga.sem, ga.at("stage", s))
                for t in range(T):
                    m = e.transpose(pm[0][:, t * P:(t + 1) * P], xst[:, t * P:(t + 1) * P], ident[:, :])
                m.then_inc(pe.sem, 1)
                e.wait_ge(aa.sem, aa.at("xT", s))
                for t in range(T):
                    m = e.matmul(pm[1][:, t * 2 * NE:(t + 1) * 2 * NE], xT[:, t * P:(t + 1) * P], rgu[:, :], start=True, stop=True)
                m.then_inc(pe.sem, 1)
                for n in range(2 * NE):
                    e.wait_ge(va.sem, va.at("xc", s))
                    if n >= 2:
                        e.wait_ge(aa.sem, aa.at("ctc", s, 2 * NE + 1 - n))
                    for t in range(T):
                        m = e.transpose(pm[n % 2][:, t * P:(t + 1) * P], xc[:, t, n, :], ident[:, :])
                    m.then_inc(pe.sem, 1)
                for r, (w, o) in enumerate(((wg, pg), (wu, pu))):
                    e.wait_ge(aa.sem, aa.at("ctc", s, NE * (1 - r)))
                    for j in range(CF):
                        for n in range(NE):
                            m = e.matmul(o[:, j, :], w[:, n, j * P:(j + 1) * P], xcT[:, r * NE + n, :], start=n == 0, stop=n == NE - 1)
                    m.then_inc(pe.sem, 1)
                e.wait_ge(va.sem, va.at("gu", s))
                for t in range(T):
                    for j in range(CF):
                        m = e.matmul(pm[1][:, t * NE:(t + 1) * NE], it[:, j, t * P:(t + 1) * P], rd[:, j, :], start=j == 0, stop=j == CF - 1)
                m.then_inc(pe.sem, 1)
                for t in range(T):
                    if t:
                        e.wait_ge(va.sem, va.at("acc", s, (T - t) * NE))
                    for b in range(2):
                        for j in range(CF):
                            m = e.matmul(pd[:, 4 * b:4 * b + 4, :].rearrange("p n d -> p (n d)"), it[:, j, t * P:(t + 1) * P],
                                         wd[:, j, b * 512:(b + 1) * 512], start=j == 0, stop=j == CF - 1)
                    m.then_inc(pe.sem, 1)
            each_sequence(e, sequence)


def ssm2_phase(nc, I, X, ident):
    ctx, sb, ps = tools(nc)
    NK = 8
    with ctx:
        winT = sb("c_winT", [P, 2 * DI])
        winu = sb("c_winu", [P, CI, D])
        cwb = sb("c_cwb", [P, TAPS, DI])
        cvb = sb("c_cvb", [P, CI])
        gb = sb("c_gb", [P, 2])
        wot = sb("c_wot", [P, CI, D])
        am = sb("c_am", [S1, NK, 2, S1])
        bmT = sb("c_bmT", [P, CI, S1])
        cm = sb("c_cm", [S1, DI])
        wc = sb("c_wc", [P, TAPS, DI])
        bw = sb("c_bw", [P, S1])
        xh = sb("c_xh", [P, T, D])
        xn = sb("c_xn", [P, TAPS - 1 + L])
        sg = sb("c_sg", [P, CI, L])
        sz = sb("c_sz", [P, CI, L])
        st = [sb("c_st0", [S1, L]), sb("c_st1", [S1, L])]
        yT = sb("c_yT", [P, CI, L])
        res = sb("c_res", [P, T, D])
        stats = sb("c_stats", [P, T, 6])
        mv = sb("c_mv", [P, 2, T, 2])
        ve = sb("c_ve", [P, 2, T])
        y = sb("c_y", [P, 2, T])
        h = sb("c_h", [P, T])
        tt = sb("c_t", [P, T])
        px = ps("c_px", [P, 512])
        pc = ps("c_pc", [P, CI, L])
        pz = ps("c_pz", [P, CI, L])
        pst = [ps("c_ps0", [S1, 512]), ps("c_ps1", [S1, 512])]
        pk = ps("c_pk", [P, CI, L])
        po = ps("c_po", [P, 512])
        loaded = ctx.enter_context(nc.semaphore("c_loaded"))
        vset = ctx.enter_context(nc.semaphore("c_vset"))
        pset = ctx.enter_context(nc.semaphore("c_pset"))
        gset = ctx.enter_context(nc.semaphore("c_gset"))
        pe = Steps(ctx, nc, "c_pe", f"xt v conv z dbl*{NK} k y")
        va = Steps(ctx, nc, "c_va", f"Ibn*2 Iag*2 Ive Ish Isd xh*2 v0 hd*{NK} ad*{NK} kc ky res bn*2 ag*2 ve sh sd out*2"
                   .replace(f"hd*{NK} ad*{NK}", " ".join(f"hd{k} ad{k}" for k in range(NK))))
        aa = Steps(ctx, nc, "c_aa", "xn sg*2 sz")
        ga = Steps(ctx, nc, "c_ga", f"Irs*{RS} rs*{RS}")
        LOADS = 9
        block = ctx.enter_context(nc.Block())

        @block.sync
        def _(e):
            for dst, src in [(winT[:, :], I["c_winT"]), (winu[:, :, :], I["c_winu"]),
                             (cwb[:, :, :], I["c_cw"].to_broadcast([P, TAPS, DI])),
                             (cvb[:, :], I["c_cvb"]), (gb[:, :], I["c_gb"]), (wot[:, :, :], I["c_wot"]),
                             (am[:, 0, :, :], I["c_am"]), (bmT[:, :, :], I["c_bmT"]), (cm[:, :], I["c_cm"])]:
                e.dma_start(dst, src).then_inc(loaded, 16)

        @block.gpsimd
        def _(e):
            e.memset(xn[:, 0:TAPS - 1], 0.0).then_inc(gset, 1)
            def sequence(s):
                e.wait_ge(va.sem, va.at("Isd", s))
                at_rest(e)
                newton_rsqrt(e, ga, s, "Irs", y[:, 0, :], ve[:, 0, :], h[:, :], tt[:, :])
                e.wait_ge(va.sem, va.at("sd", s))
                e.wait_ge(ga.sem, ga.at("Irs", s))
                at_rest(e)
                newton_rsqrt(e, ga, s, "rs", y[:, 1, :], ve[:, 1, :], h[:, :], tt[:, :])
            each_sequence(e, sequence)

        @block.vector
        def _(e):
            e.wait_ge(loaded, 16 * LOADS)
            for k in range(TAPS):
                e.tensor_tensor(wc[:, k, :], winT[:, 0:DI], cwb[:, k, :], ALU.mult).then_inc(vset, 1)
            e.wait_ge(pset, 1)
            e.tensor_copy(bw[:, :], po[:, 0:S1]).then_inc(vset, 1)
            for k in range(1, NK):
                e.wait_ge(pset, k + 1)
                e.tensor_copy(am[:, k, :, :], pst[0][:, 0:2 * S1].rearrange("p (a b) -> p a b", a=2)).then_inc(vset, 1)
            e.wait_ge(vset, TAPS + NK)
            def sequence(s):
                layernorm_stats(e, va, s, lambda t: X[:, s, t, :], stats, mv[:, 0, :, :], "I")
                e.wait_ge(va.sem, va.at("Iag", s))
                e.tensor_scalar(ve[:, 0, :], mv[:, 0, :, 1], EPS, None, ALU.add).then_inc(va.sem, 1)
                e.wait_ge(va.sem, va.at("Ive", s))
                rsqrt_seed(e, va, s, "I", ve[:, 0, :].bitcast(I32), y[:, 0, :].bitcast(I32))
                e.wait_ge(ga.sem, ga.at("Irs", s))
                for t in range(T):
                    e.tensor_scalar(xh[:, t, :], X[:, s, t, :], mv[:, 0, t, 0:1], y[:, 0, t:t + 1], ALU.subtract, ALU.mult)\
                        .then_inc(va.sem, 1)
                e.wait_ge(pe.sem, pe.at("v", s))
                e.tensor_copy(st[0][:, :], po[0:S1, 0:L]).then_inc(va.sem, 1)
                for k in range(NK):
                    a, b, d = st[k % 2], st[(k + 1) % 2], 1 << k
                    e.wait_ge(va.sem, va.at(f"ad{k - 1}" if k else "v0", s))
                    e.tensor_copy(b[:, 0:d], a[:, 0:d]).then_inc(va.sem, 1)
                    e.wait_ge(pe.sem, pe.at("dbl", s, NK - 1 - k))
                    e.tensor_tensor(b[:, d:L], pst[k % 2][:, 0:L - d], a[:, d:L], ALU.add).then_inc(va.sem, 1)
                e.wait_ge(aa.sem, aa.at("sg", s))
                e.wait_ge(pe.sem, pe.at("k", s))
                e.tensor_tensor(yT[:, :, :], pk[:, :, :], sg[:, :, :], ALU.add).then_inc(va.sem, 1)
                e.wait_ge(va.sem, va.at("kc", s))
                e.wait_ge(aa.sem, aa.at("sz", s))
                e.tensor_tensor(yT[:, :, :], yT[:, :, :], sz[:, :, :], ALU.mult).then_inc(va.sem, 1)
                e.wait_ge(pe.sem, pe.at("y", s))
                e.scalar_tensor_tensor(res[:, :, :], X[:, s, :, :], 2.0, po[:, 0:L].rearrange("p (t d) -> p t d", t=T),
                                       ALU.mult, ALU.add).then_inc(va.sem, 1)
                e.wait_ge(va.sem, va.at("res", s))
                layernorm_stats(e, va, s, lambda t: res[:, t, :], stats, mv[:, 1, :, :], "")
                e.wait_ge(va.sem, va.at("ag", s))
                e.tensor_scalar(ve[:, 1, :], mv[:, 1, :, 1], EPS, None, ALU.add).then_inc(va.sem, 1)
                e.wait_ge(va.sem, va.at("ve", s))
                rsqrt_seed(e, va, s, "", ve[:, 1, :].bitcast(I32), y[:, 1, :].bitcast(I32))
                e.wait_ge(ga.sem, ga.at("rs", s))
                for t in range(T):
                    e.tensor_scalar(X[:, s, t, :], res[:, t, :], mv[:, 1, t, 0:1], y[:, 1, t:t + 1], ALU.subtract, ALU.mult)\
                        .then_inc(va.sem, 1)
            each_sequence(e, sequence)

        @block.scalar
        def _(e):
            e.wait_ge(loaded, 16 * LOADS)
            e.wait_ge(gset, 1)
            def sequence(s):
                e.wait_ge(pe.sem, pe.at("xt", s))
                e.activation(xn[:, TAPS - 1:], px[:, 0:L], ACT.Identity, bias=gb[:, 1:2], scale=gb[:, 0:1]).then_inc(aa.sem, 1)
                e.wait_ge(pe.sem, pe.at("conv", s))
                for c in range(CI):
                    e.activation(sg[:, c, :], pc[:, c, :], ACT.Silu, bias=cvb[:, c:c + 1]).then_inc(aa.sem, 1)
                e.wait_ge(pe.sem, pe.at("z", s))
                e.activation(sz[:, :, :], pz[:, :, :], ACT.Sigmoid).then_inc(aa.sem, 1)
            each_sequence(e, sequence)

        @block.tensor
        def _(e):
            e.wait_ge(loaded, 16 * LOADS)
            for c in range(CI):
                m = e.matmul(po[:, 0:S1], winu[:, c, :], bmT[:, c, :], start=c == 0, stop=c == CI - 1)
            m.then_inc(pset, 1)
            for k in range(1, NK):
                if k > 1:
                    e.wait_ge(vset, TAPS + k)
                e.matmul(pst[0][:, 0:S1], am[:, k - 1, 1, :], am[:, k - 1, 0, :], start=True, stop=True)
                e.matmul(pst[0][:, S1:2 * S1], am[:, k - 1, 0, :], am[:, k - 1, 1, :], start=True, stop=True).then_inc(pset, 1)
            e.wait_ge(vset, TAPS + NK)
            def sequence(s):
                e.wait_ge(va.sem, va.at("xh", s))
                for t in range(T):
                    m = e.transpose(px[:, t * P:(t + 1) * P], xh[:, t, :], ident[:, :])
                m.then_inc(pe.sem, 1)
                e.wait_ge(aa.sem, aa.at("xn", s))
                e.matmul(po[0:S1, 0:L], bw[:, :], xn[:, TAPS - 1:], start=True, stop=True).then_inc(pe.sem, 1)
                for c in range(CI):
                    for k in range(TAPS):
                        m = e.matmul(pc[:, c, :], wc[:, k, c * P:(c + 1) * P], xn[:, k:k + L], start=k == 0, stop=k == TAPS - 1)
                m.then_inc(pe.sem, 1)
                for c in range(CI):
                    m = e.matmul(pz[:, c, :], winT[:, DI + c * P:DI + (c + 1) * P], xn[:, TAPS - 1:], start=True, stop=True)
                m.then_inc(pe.sem, 1)
                for k in range(NK):
                    e.wait_ge(va.sem, va.at(f"ad{k - 1}" if k else "v0", s))
                    at_rest(e)
                    e.matmul(pst[k % 2][:, 0:L - (1 << k)], am[:, k, 1, :], st[k % 2][:, 0:L - (1 << k)], start=True, stop=True)\
                        .then_inc(pe.sem, 1)
                e.wait_ge(va.sem, va.at(f"ad{NK - 1}", s))
                for c in range(CI):
                    m = e.matmul(pk[:, c, :], cm[:, c * P:(c + 1) * P], st[NK % 2][:, :], start=True, stop=True)
                m.then_inc(pe.sem, 1)
                e.wait_ge(va.sem, va.at("ky", s))
                for t in range(T):
                    for c in range(CI):
                        m = e.matmul(po[:, t * P:(t + 1) * P], yT[:, c, t * P:(t + 1) * P], wot[:, c, :], start=c == 0, stop=c == CI - 1)
                m.then_inc(pe.sem, 1)
            each_sequence(e, sequence)


def transformer_phase(nc, I, X, ident, out):
    ctx, sb, ps = tools(nc)
    ORDER = [1, 3, 5, 7, 0, 2, 4, 6]
    N = HEADS * HD
    with ctx:
        X0 = sb("X0", [P, NSEQ, T, D])
        wqkv = sb("wqkv", [P, 3 * N])
        wo = sb("wo", [P, N // P, D])
        w1 = sb("w1", [P, 2 * HC, P])
        w2 = sb("w2", [P, HC, D])
        vec = sb("vec", [P, 2 + 2 * HC])
        b2 = sb("b2", [1, D])
        ones = sb("ones", [1, P])
        rows = sb("rows", [P, 4, HD])
        tab = sb("tab", [P, T, 4, HD])
        tabl = sb("tabl", [P, T, 4, HD])
        mask = sb("mask", [P, NW * KEYS])
        maskb = sb("maskb", [P, NW * KEYS], BF16)
        identb = sb("identb", [P, P], BF16)
        xin = sb("xin", [P, L])
        xs = sb("xs", [P, WIN + L + 1])
        sq = sb("sq", [P, N])
        n2 = sb("n2", [P, HEADS])
        nh = sb("nh", [P, HEADS])
        nt = sb("nt", [P, HEADS])
        rn = sb("rn", [P, HEADS])
        qn = sb("qn", [P, HEADS, HD])
        m1 = sb("m1", [P, N])
        m2 = sb("m2", [P, HEADS, HD])
        rot = [sb(f"rot{i}", [P, N]) for i in range(2)]
        qT = [sb(f"qT{i}", [P, N // P, L]) for i in range(2)]
        kT = [sb(f"kT{i}", [P, N // P, WIN + L]) for i in range(2)]
        V = [sb(f"V{i}", [P, T, 2, N]) for i in range(2)]
        mx = sb("mx", [P, NG, NW])
        sm = sb("sm", [P, NG, NW])
        rc = sb("rc", [P, NG, NW])
        E = [sb(f"E{i}", [P, NW * KEYS]) for i in range(2)]
        PT = [sb(f"PT{i}", [P, NW * KEYS]) for i in range(2)]
        oT = sb("oT", [P, N // P, L])
        yin = sb("yin", [P, L])
        ys = sb("ys", [P, L + 1])
        stats = sb("stats", [P, T, 6])
        mv = sb("mv", [P, T, 2])
        ve = sb("ve", [P, T])
        yr = sb("yr", [P, T])
        yh = sb("yh", [P, T])
        yt = sb("yt", [P, T])
        xh = sb("xh", [P, T, D])
        xnT = sb("xnT", [P, L])
        gl = sb("gl", [P, HC, L])
        hh = sb("hh", [P, HC, L])
        fst = sb("fst", [P, NSEQ * T, 6])
        fmv = sb("fmv", [P, NSEQ * T, 2])
        fv = [sb(f"fv{i}", [P, NSEQ * T]) for i in range(4)]

        pQ = ps("pQ", [P, N])
        pM = [ps("pM0", [P, 512]), ps("pM1", [P, 512])]
        pC = ps("pC", [P, 512])
        pS = ps("pS", [P, NW * KEYS])
        pT = ps("pT", [P, 512])
        pO = ps("pO", [P, 512])
        pOV = [x[:, 0:L].rearrange("p (c t k) -> p c t k", c=2, t=T) for x in (pO, pT)]

        sem = {k: ctx.enter_context(nc.semaphore(k)) for k in
               ("const_loaded", "wqkv_loaded", "wo_loaded", "mlp_loaded", "rows_loaded", "v_setup", "g_setup",
                "tables", "end_v", "end_g", "stored")}
        A_PE = "xt qk0 v0a v0b qk1 v1a v1b qk2 tr0a tr0b v2a v2b qk3 tr1a tr1b v3a v3b tr2a tr2b tr3a tr3b"
        A_ACT = "xs*2 sq0 v0a v0b sq1 v1a v1b sq2 tr0a tr0b v2a v2b sq3 tr1a tr1b v3a v3b tr2a tr2b tr3a tr3b"
        pa = Steps(ctx, nc, "pe_a", A_PE)
        sa = Steps(ctx, nc, "act_a", A_ACT)
        va = Steps(ctx, nc, "dve_a", " ".join(f"rd{u} mn{u} sh{u} sd{u} qn{u} cs{u} sn{u}*2" for u in range(4)))
        ga = Steps(ctx, nc, "pool_a", "st " + " ".join(f"rs{u}*{RS} ad{u}" for u in range(4)))
        pb = Steps(ctx, nc, "pe_b", "s0 s1 pt0 pv0 s2 pt1 pv1 s3 pt2 pv2 pt3 pv3 wo")
        sb_ = Steps(ctx, nc, "act_b", "ex0 ex1 pt0 ov0*2 ex2 pt1 ov1*2 ex3 pt2 ov2*2 pt3 ov3*2")
        vb = Steps(ctx, nc, "dve_b", " ".join(f"mx{g} su{g} sm{g} rc{g} no{g}" for g in range(4)) + " xa")
        pc = Steps(ctx, nc, "pe_c", "xt back xn h0 h1 h2 w2")
        sc = Steps(ctx, nc, "act_c", "sh*2 xn ge0 ge1 ge2")
        vc = Steps(ctx, nc, "dve_c", "bn*2 ag*2 ve sh sd xh*2 hid0 hid1 hid2 add")
        gc = Steps(ctx, nc, "pool_c", f"st rs*{RS}")
        V_SETUP = 5
        block = ctx.enter_context(nc.Block())

        layer0 = {}

        def passes(run, eng):
            layer0["now"] = True
            run((0, 0, 0, 0), None, None)
            run((1, 1, 1, None), (0, 0, 0, 0), None)

            run((2, 2, 0, None), (1, 1, 1, None), (0, 0, 0, 0))
            run((3, 3, 1, None), (2, 2, 0, None), (1, 1, 1, None))
            with eng.Fori(0, (NSEQ - 4) // 2) as i:
                for p in range(2):
                    n = 2 * i + (4 + p)
                    run((n, n, p, None), (n - 1, n - 1, 1 - p, None), (n - 2, n - 2, p, None))
            layer0["now"] = False
            with eng.Fori(1, DEPTH) as l:
                n0 = l * NSEQ
                run((n0, 0, 0, l), (n0 - 1, NSEQ - 1, 1, None), (n0 - 2, NSEQ - 2, 0, None))
                run((n0 + 1, 1, 1, None), (n0, 0, 0, l), (n0 - 1, NSEQ - 1, 1, None))
                run((n0 + 2, 2, 0, None), (n0 + 1, 1, 1, None), (n0, 0, 0, l))
                run((n0 + 3, 3, 1, None), (n0 + 2, 2, 0, None), (n0 + 1, 1, 1, None))
                with eng.Fori(0, (NSEQ - 4) // 2) as i:
                    for p in range(2):
                        s = 2 * i + (4 + p)
                        n = n0 + s
                        run((n, s, p, None), (n - 1, s - 1, 1 - p, None), (n - 2, s - 2, p, None))
            last = DEPTH * NSEQ
            run(None, (last - 1, NSEQ - 1, 1, None), (last - 2, NSEQ - 2, 0, None))
            run(None, None, (last - 1, NSEQ - 1, 1, None))

        @block.sync
        def _(e):
            for dst, src in [(tab[:, :, :, :], I["tab"]), (mask[:, :], I["mask"]), (ones[:, :], I["ones"])]:
                e.dma_start(dst, src).then_inc(sem["const_loaded"], 16)

            def load(l, which):
                if which == "a":
                    e.dma_start(rows[:, :, :], I["rows"][l, :, :, :].to_broadcast([P, 4, HD])).then_inc(sem["rows_loaded"], 16)
                    e.dma_start(wqkv[:, :], I["wqkv"][l, :, :]).then_inc(sem["wqkv_loaded"], 16)
                elif which == "b":
                    e.dma_start(wo[:, :, :], I["wo"][l, :, :, :]).then_inc(sem["wo_loaded"], 16)
                else:
                    e.dma_start(w1[:, :, :], I["w1"][l, :, :, :]).then_inc(sem["mlp_loaded"], 16)
                    e.dma_start(w2[:, :, :], I["w2"][l, :, :, :]).then_inc(sem["mlp_loaded"], 16)
                    e.dma_start(vec[:, :], I["vec"][l, :, :]).then_inc(sem["mlp_loaded"], 16)
                    e.dma_start(b2[:, :], I["b2"][l, :, :]).then_inc(sem["mlp_loaded"], 16)
            for which in "abc":
                load(0, which)
            with e.Fori(1, DEPTH) as l:
                e.wait_ge(sem["tables"], l * 4 * T)
                e.wait_ge(pa.sem, pa.at("v3b", l * NSEQ - 1))
                load(l, "a")
                e.wait_ge(pb.sem, pb.at("wo", l * NSEQ - 1))
                load(l, "b")
                e.wait_ge(pc.sem, pc.at("w2", l * NSEQ - 1))
                load(l, "c")
            e.wait_ge(sem["end_v"], 4 + 3 * NSEQ * T)
            e.dma_start(out, X[:, :, :, :]).then_inc(sem["stored"], 16)
            e.wait_ge(sem["stored"], 16)

        @block.gpsimd
        def _(e):
            e.memset(xs[:, 0:WIN + 1], 0.0).then_inc(sem["g_setup"], 1)
            e.memset(ys[:, 0:1], 0.0).then_inc(sem["g_setup"], 1)
            for i in range(2):
                e.memset(kT[i][:, :, 0:WIN], 0.0).then_inc(sem["g_setup"], 1)

            def run(A, B, C):
                if A:
                    n, s, par, l = A
                    if not layer0["now"]:
                        e.wait_ge(vc.sem, vc.at("add", n - NSEQ))
                    if later(n):
                        e.wait_ge(pa.sem, pa.at("xt", n - 1))
                    at_rest(e)
                    e.tensor_copy(xin[:, :], X[:, s, :, :].rearrange("p t d -> p (t d)")).then_inc(ga.sem, 1)
                if C:
                    n, s, par, l = C
                    e.wait_ge(vb.sem, vb.at("xa", n))
                    if later(n):
                        e.wait_ge(pc.sem, pc.at("xt", n - 1))
                    at_rest(e)
                    e.tensor_copy(yin[:, :], X[:, s, :, :].rearrange("p t d -> p (t d)")).then_inc(gc.sem, 1)
                for u in range(4):
                    if A:
                        n = A[0]
                        e.wait_ge(va.sem, va.at(f"sd{u}", n))
                        at_rest(e)
                        newton_rsqrt(e, ga, n, f"rs{u}", rn[:, :], n2[:, :], nh[:, :], nt[:, :])
                    if C and u == 1:
                        e.wait_ge(vc.sem, vc.at("sd", C[0]))
                        at_rest(e)
                        newton_rsqrt(e, gc, C[0], "rs", yr[:, :], ve[:, :], yh[:, :], yt[:, :])
                    if A:
                        e.wait_ge(va.sem, va.at(f"sn{u}", n))
                        if u >= 2:
                            e.wait_ge(pa.sem, pa.at(f"tr{u - 2}b", n))
                        elif later(n):
                            e.wait_ge(pa.sem, pa.at(f"tr{u + 2}b", n - 1))
                        at_rest(e)
                        e.tensor_tensor(rot[u % 2][:, :], m1[:, :], m2[:, :, :].rearrange("p h d -> p (h d)"), ALU.add)\
                            .then_inc(ga.sem, 1)
            passes(run, e)
            e.wait_ge(sem["end_v"], 4 + 2 * NSEQ * T)
            at_rest(e)
            f = fv
            h, t, y, v = f[0][:, :], f[1][:, :], f[2][:, :], f[3][:, :]
            k = 0
            for op in range(14):
                if op >= 1:
                    e.wait_ge(sem["end_g"], op)
                    at_rest(e)
                if op == 0:
                    e.tensor_scalar(h, v, -0.5, 0.0, ALU.mult, ALU.add).then_inc(sem["end_g"], 1)
                elif op == 13:
                    e.tensor_copy(t, y).then_inc(sem["end_g"], 1)
                elif op % 4 == 1:
                    e.tensor_tensor(t, y, y, ALU.mult).then_inc(sem["end_g"], 1)
                elif op % 4 == 2:
                    e.tensor_tensor(t, t, h, ALU.mult).then_inc(sem["end_g"], 1)
                elif op % 4 == 3:
                    e.tensor_scalar(t, t, 1.0, 1.5, ALU.mult, ALU.add).then_inc(sem["end_g"], 1)
                else:
                    e.tensor_tensor(y, y, t, ALU.mult).then_inc(sem["end_g"], 1)

        @block.vector
        def _(e):
            e.wait_ge(sem["const_loaded"], 48)
            e.tensor_copy(maskb[:, :], mask[:, :]).then_inc(sem["v_setup"], 1)
            e.tensor_copy(identb[:, :], ident[:, :]).then_inc(sem["v_setup"], 1)
            e.tensor_copy(X0[:, :, :, :], X[:, :, :, :]).then_inc(sem["v_setup"], 1)
            e.wait_ge(sem["v_setup"], 3)

            def wide(a, shape):
                return a.to_broadcast(shape)

            def run(A, B, C):
                if A:
                    n, s, par, l = A
                    if l is not None:
                        e.wait_ge(sem["rows_loaded"], 16 * (l + 1))
                        if later(n):
                            e.wait_ge(va.sem, va.at("sn3", n - 1))
                        for t in range(T):
                            for k in range(4):
                                e.tensor_tensor(tabl[:, t, k, :], tab[:, t, k, :], rows[:, k, :], ALU.mult).then_inc(sem["tables"], 1)
                        e.wait_ge(sem["tables"], (l + 1) * 4 * T)
                for u in range(4):
                    if C and u == 2:
                        c = C[0]
                        e.wait_ge(gc.sem, gc.at("rs", c))
                        for t in range(T):
                            e.tensor_scalar(xh[:, t, :], pC[:, L + t * P:L + (t + 1) * P], mv[:, t, 0:1], yr[:, t:t + 1],
                                            ALU.subtract, ALU.mult).then_inc(vc.sem, 1)
                    if B:
                        b = B[0]
                        e.wait_ge(pb.sem, pb.at(f"s{u}", b))
                        if u >= 2:
                            e.wait_ge(pb.sem, pb.at(f"pt{u - 2}", b))
                        elif later(b):
                            e.wait_ge(pb.sem, pb.at(f"pt{u + 2}", b - 1))
                        sv = pS[:, :].rearrange("p (w k) -> p w k", k=KEYS)
                        ev = E[u % 2][:, :].rearrange("p (w k) -> p w k", k=KEYS)
                        e.tensor_reduce(mx[:, u, :], sv, AX.X, ALU.max).then_inc(vb.sem, 1)
                        e.wait_ge(vb.sem, vb.at(f"mx{u}", b))
                        e.tensor_tensor(ev, sv, wide(mx[:, u, :].unsqueeze(2), [P, NW, KEYS]), ALU.subtract).then_inc(vb.sem, 1)
                    if A:
                        n = A[0]
                        t, w = u // 2, u % 2
                        e.wait_ge(sa.sem, sa.at(f"sq{u}", n))
                        e.wait_ge(ga.sem, ga.at(f"ad{u - 1}", n) if u else (ga.at("st", n)))
                        e.tensor_reduce(n2[:, :], sq[:, :].rearrange("p (h d) -> p h d", d=HD), AX.X, ALU.add).then_inc(va.sem, 1)
                        e.wait_ge(va.sem, va.at(f"rd{u}", n))
                        e.tensor_scalar(n2[:, :], n2[:, :], 1e-24, None, ALU.max).then_inc(va.sem, 1)
                        e.wait_ge(va.sem, va.at(f"mn{u}", n))
                        e.tensor_scalar(rn[:, :].bitcast(I32), n2[:, :].bitcast(I32), 1, None, ALU.logical_shift_right).then_inc(va.sem, 1)
                        e.wait_ge(va.sem, va.at(f"sh{u}", n))
                        e.tensor_scalar(rn[:, :].bitcast(I32), rn[:, :].bitcast(I32), -1.0, MAGIC, ALU.mult, ALU.add).then_inc(va.sem, 1)
                    if B:
                        e.wait_ge(sb_.sem, sb_.at(f"ex{u}", b))
                        e.tensor_reduce(sm[:, u, :], ev, AX.X, ALU.add).then_inc(vb.sem, 1)
                        e.wait_ge(vb.sem, vb.at(f"sm{u}", b))
                        e.reciprocal(rc[:, u, :], sm[:, u, :]).then_inc(vb.sem, 1)
                        e.wait_ge(vb.sem, vb.at(f"rc{u}", b))
                        e.tensor_tensor(ev, ev, wide(rc[:, u, :].unsqueeze(2), [P, NW, KEYS]), ALU.mult).then_inc(vb.sem, 1)
                    if C and u == 1:
                        e.wait_ge(pc.sem, pc.at("back", c := C[0]))
                        layernorm_stats(e, vc, c, lambda t: pC[:, L + t * P:L + (t + 1) * P], stats, mv, "")
                        e.wait_ge(vc.sem, vc.at("ag", c))
                        e.tensor_scalar(ve[:, :], mv[:, :, 1], EPS, None, ALU.add).then_inc(vc.sem, 1)
                        e.wait_ge(vc.sem, vc.at("ve", c))
                        rsqrt_seed(e, vc, c, "", ve[:, :].bitcast(I32), yr[:, :].bitcast(I32))
                    if A:
                        e.wait_ge(ga.sem, ga.at(f"rs{u}", n))
                        e.tensor_tensor(qn[:, :, :], pQ[:, :].rearrange("p (h d) -> p h d", d=HD),
                                        wide(rn[:, :].unsqueeze(2), [P, HEADS, HD]), ALU.mult).then_inc(va.sem, 1)
                        e.wait_ge(va.sem, va.at(f"qn{u}", n))
                        e.tensor_tensor(m1[:, :].rearrange("p (h d) -> p h d", d=HD), qn[:, :, :],
                                        wide(tabl[:, t, 2 * w, :].unsqueeze(1), [P, HEADS, HD]), ALU.mult).then_inc(va.sem, 1)
                        for a, b_ in ((0, HD // 2), (HD // 2, 0)):
                            e.tensor_tensor(m2[:, :, a:a + HD // 2], qn[:, :, b_:b_ + HD // 2],
                                            wide(tabl[:, t, 2 * w + 1, a:a + HD // 2].unsqueeze(1), [P, HEADS, HD // 2]),
                                            ALU.mult).then_inc(va.sem, 1)
                if C:
                    def hid(j):
                        e.wait_ge(sc.sem, sc.at(f"ge{j}", c))
                        e.scalar_tensor_tensor(hh[:, j, :], pC[:, 0:L], vec[:, 2 + j:3 + j], gl[:, j, :], ALU.add, ALU.mult)\
                            .then_inc(vc.sem, 1)
                    hid(0)
                    hid(1)
                if B:
                    e.wait_ge(pb.sem, pb.at("wo", b))
                    xv = X[:, B[1], :, :].rearrange("p t d -> p (t d)")
                    e.tensor_tensor(xv, xv, pT[:, 0:L], ALU.add).then_inc(vb.sem, 1)
                if C:
                    hid(2)
                    e.wait_ge(pc.sem, pc.at("w2", c))
                    xv = X[:, C[1], :, :].rearrange("p t d -> p (t d)")
                    e.tensor_tensor(xv, xv, pC[:, 0:L], ALU.add).then_inc(vc.sem, 1)
            passes(run, e)
            ev = sem["end_v"]
            NT = NSEQ * T
            e.wait_ge(vc.sem, vc.at("add", DEPTH * NSEQ - 1))
            e.tensor_tensor(X0[:, :, :, :], X0[:, :, :, :], X[:, :, :, :], ALU.add).then_inc(ev, 1)
            e.wait_ge(ev, 1)
            xf = X0[:, :, :, :].rearrange("p s t d -> p (s t) d")
            for t in range(NT):
                e.bn_stats(fst[:, t, :], xf[:, t, :]).then_inc(ev, 1)
            e.wait_ge(ev, 1 + NT)
            for t in range(NT):
                e.bn_aggr(fmv[:, t, :], fst[:, t, :]).then_inc(ev, 1)
            e.wait_ge(ev, 1 + 2 * NT)
            e.tensor_scalar(fv[3][:, :], fmv[:, :, 1], EPS, None, ALU.add).then_inc(ev, 1)
            e.wait_ge(ev, 2 + 2 * NT)
            e.tensor_scalar(fv[2][:, :].bitcast(I32), fv[3][:, :].bitcast(I32), 1, None, ALU.logical_shift_right).then_inc(ev, 1)
            e.wait_ge(ev, 3 + 2 * NT)
            e.tensor_scalar(fv[2][:, :].bitcast(I32), fv[2][:, :].bitcast(I32), -1.0, MAGIC, ALU.mult, ALU.add).then_inc(ev, 1)
            e.wait_ge(sem["end_g"], 14)
            xo = X[:, :, :, :].rearrange("p s t d -> p (s t) d")
            for t in range(NT):
                e.tensor_scalar(xo[:, t, :], xf[:, t, :], fmv[:, t, 0:1], fv[2][:, t:t + 1], ALU.subtract, ALU.mult).then_inc(ev, 1)

        @block.scalar
        def _(e):
            e.wait_ge(sem["g_setup"], 4)

            def run(A, B, C):
                def copy_m(u, kind):
                    n, s, par, l = A
                    t, w = u // 2, u % 2
                    for i, half in enumerate("ab"):
                        e.wait_ge(pa.sem, pa.at(f"{kind}{u}{half}", n))
                        if kind == "v":
                            dst, src = V[par][:, t, w, i * 512:(i + 1) * 512], pM[i][:, :]
                        else:
                            buf, off = (kT[par], WIN) if w else (qT[par], 0)
                            dst = buf[:, 4 * i:4 * i + 4, off + t * P:off + (t + 1) * P]
                            src = pM[i][:, :].rearrange("p (c t) -> p c t", c=4)
                        e.activation(dst, src, ACT.Copy).then_inc(sa.sem, 1)

                def copy_b(g):
                    b = B[0]
                    e.wait_ge(pb.sem, pb.at(f"pt{g}", b))
                    e.activation(PT[g % 2][:, :], pT[:, :], ACT.Copy).then_inc(sb_.sem, 1)

                def copy_o(g):
                    b = B[0]
                    e.wait_ge(pb.sem, pb.at(f"pv{g}", b))
                    for i in range(2):
                        e.activation(oT[:, 2 * g:2 * g + 2, :].rearrange("p c (t k) -> p c t k", t=T)[:, :, :, KEYS * i:KEYS * (i + 1)],
                                     pOV[i], ACT.Copy).then_inc(sb_.sem, 1)

                def gelu(j):
                    e.wait_ge(pc.sem, pc.at(f"h{j}", C[0]))
                    e.activation(gl[:, j, :], pC[:, L:2 * L], ACT.Gelu, bias=vec[:, 2 + HC + j:3 + HC + j]).then_inc(sc.sem, 1)
                if A:
                    e.wait_ge(pa.sem, pa.at("xt", A[0]))
                    e.activation(xs[0:HALF, WIN:WIN + L], pM[0][0:HALF, 0:L], ACT.Copy).then_inc(sa.sem, 1)
                    e.activation(xs[HALF:P, WIN + 1:WIN + L + 1], pM[0][HALF:P, 0:L], ACT.Copy).then_inc(sa.sem, 1)
                if C:
                    e.wait_ge(pc.sem, pc.at("xt", C[0]))
                    e.activation(ys[0:HALF, 0:L], pC[0:HALF, 0:L], ACT.Copy).then_inc(sc.sem, 1)
                    e.activation(ys[HALF:P, 1:L + 1], pC[HALF:P, 0:L], ACT.Copy).then_inc(sc.sem, 1)
                for u in range(4):
                    if A:
                        e.wait_ge(pa.sem, pa.at(f"qk{u}", A[0]))
                        if u or later(A[0]):
                            e.wait_ge(va.sem, va.at(f"rd{u - 1}", A[0]) if u else va.at("rd3", A[0] - 1))
                        e.activation(sq[:, :], pQ[:, :], ACT.Square).then_inc(sa.sem, 1)
                    if B:
                        e.wait_ge(vb.sem, vb.at(f"su{u}", B[0]))
                        e.activation(E[u % 2][:, :], E[u % 2][:, :], ACT.Exp, scale=8.0).then_inc(sb_.sem, 1)
                        if u:
                            copy_b(u - 1)
                    if A:
                        if u >= 2:
                            copy_m(u - 2, "tr")
                        copy_m(u, "v")
                    if B and u:
                        copy_o(u - 1)
                    if C and u == 2:
                        if C[3] is not None:
                            e.wait_ge(sem["mlp_loaded"], 64 * (C[3] + 1))
                        e.wait_ge(pc.sem, pc.at("xn", C[0]))
                        e.activation(xnT[:, :], pC[:, 0:L], ACT.Identity, bias=vec[:, 1:2], scale=vec[:, 0:1]).then_inc(sc.sem, 1)
                    if C and u == 3:
                        gelu(0)
                if A:
                    copy_m(2, "tr")
                if B:
                    copy_b(3)
                    copy_o(3)
                if C:
                    gelu(1)
                if A:
                    copy_m(3, "tr")
                if C:
                    gelu(2)
            passes(run, e)

        @block.tensor
        def _(e):
            e.wait_ge(sem["v_setup"], 3)
            e.wait_ge(sem["g_setup"], 4)
            fills = A_ACT.replace("xs*2", "xs").split()
            lasta = {}
            prev = ["tr3a", "tr3b"]
            for name in [x for x in A_PE.split() if x[0:2] in ("xt", "v0", "v1", "v2", "v3", "tr")]:
                i = 0 if name == "xt" or name[-1] == "a" else 1
                lasta[name] = prev[i]
                prev[i] = "xs" if name == "xt" else name

            def run(A, B, C):
                def bank_free(n, name):
                    back = lasta[name]
                    first = name == "xt" or name == "v0b"
                    if not first:
                        e.wait_ge(sa.sem, sa.at(back, n))
                    elif later(n):
                        e.wait_ge(sa.sem, sa.at(back, n - 1))

                def a_xt():
                    n, s, par, l = A
                    e.wait_ge(ga.sem, ga.at("st", n))
                    bank_free(n, "xt")
                    for t in range(T):
                        m = e.transpose(pM[0][:, t * P:(t + 1) * P], xin[:, t * P:(t + 1) * P], ident[:, :])
                    m.then_inc(pa.sem, 1)

                def a_qk(u):
                    n, s, par, l = A
                    t, w = u // 2, u % 2
                    if u == 0:
                        if l is not None:
                            e.wait_ge(sem["wqkv_loaded"], 16 * (l + 1))
                        e.wait_ge(sa.sem, sa.at("xs", n))
                    if u or later(n):
                        e.wait_ge(va.sem, va.at(f"qn{u - 1}", n) if u else va.at("qn3", n - 1))
                    for i in range(2):
                        m = e.matmul(pQ[:, i * 512:(i + 1) * 512], xs[:, WIN + t * P:WIN + (t + 1) * P],
                                     wqkv[:, w * N + i * 512:w * N + (i + 1) * 512], start=True, stop=True)
                    m.then_inc(pa.sem, 1)

                def a_v(u):
                    n, s, par, l = A
                    t, w = u // 2, u % 2
                    o = t * P + (0 if w else WIN)
                    for i, half in enumerate("ab"):
                        bank_free(n, f"v{u}{half}")
                        e.matmul(pM[i][:, :], xs[:, o:o + P], wqkv[:, 2 * N + i * 512:2 * N + (i + 1) * 512],
                                 start=True, stop=True).then_inc(pa.sem, 1)

                def a_tr(u):
                    n, s, par, l = A
                    e.wait_ge(ga.sem, ga.at(f"ad{u}", n))
                    for i, half in enumerate("ab"):
                        bank_free(n, f"tr{u}{half}")
                        for c in range(4):
                            m = e.transpose(pM[i][:, c * P:(c + 1) * P], rot[u % 2][:, (4 * i + c) * P:(4 * i + c + 1) * P], ident[:, :])
                        m.then_inc(pa.sem, 1)

                def b_s(g):
                    b, s, par, l = B
                    if g == 0:
                        e.wait_ge(sa.sem, sa.at("tr3b", b))
                    if g or later(b):
                        e.wait_ge(vb.sem, vb.at(f"su{g - 1}", b) if g else vb.at("su3", b - 1))
                    e.matmul(pS[:, :], identb[:, :], maskb[:, :], start=True, stop=False, skip_group_check=True)
                    for i, w in enumerate(ORDER):
                        for j in range(4):
                            h = 4 * g + j
                            r = HD * (h % 2)
                            m = e.matmul(pS[32 * j:32 * j + 32, i * KEYS:(i + 1) * KEYS], qT[par][r:r + HD, h // 2, WIN * w:WIN * (w + 1)],
                                         kT[par][r:r + HD, h // 2, WIN * w:WIN * (w + 2)], start=False, stop=(i == NW - 1),
                                         skip_group_check=True, tile_position=(r, 32 * j))
                    m.then_inc(pb.sem, 1)

                def b_pt(g):
                    b = B[0]
                    e.wait_ge(vb.sem, vb.at(f"no{g}", b))
                    if g:
                        e.wait_ge(sb_.sem, sb_.at(f"ov{g - 1}", b))
                    elif later(b):
                        e.wait_ge(vb.sem, vb.at("xa", b - 1))
                    for i in range(4):
                        m = e.transpose(pT[:, i * P:(i + 1) * P], E[g % 2][:, i * P:(i + 1) * P], ident[:, :])
                    m.then_inc(pb.sem, 1)

                def b_pv(g):
                    b, s, par, l = B
                    e.wait_ge(sb_.sem, sb_.at(f"pt{g}", b))
                    at_rest(e)
                    for i, w in enumerate(ORDER):
                        r = KEYS * (i % 2)
                        for j in range(4):
                            h = 4 * g + j
                            c = HD * (j % 2)
                            m = e.matmul(pOV[i % 2][c:c + HD, j // 2, w // 4, WIN * (w % 2):WIN * (w % 2 + 1)], V[par][r:r + KEYS, w // 4, 1 - w % 2, h * HD:(h + 1) * HD],
                                         PT[g % 2][r:r + KEYS, (i // 2) * P + 32 * j:(i // 2) * P + 32 * j + 32],
                                         start=True, stop=True, tile_position=(r, c))
                    m.then_inc(pb.sem, 1)

                def b_wo():
                    b, s, par, l = B
                    if l is not None:
                        e.wait_ge(sem["wo_loaded"], 16 * (l + 1))
                    e.wait_ge(sb_.sem, sb_.at("ov3", b))
                    for t in range(T):
                        for c in range(N // P):
                            m = e.matmul(pT[:, t * P:(t + 1) * P], oT[:, c, t * P:(t + 1) * P], wo[:, c, :], start=c == 0, stop=c == N // P - 1)
                    m.then_inc(pb.sem, 1)

                def c_xt():
                    c, s, par, l = C
                    e.wait_ge(gc.sem, gc.at("st", c))
                    if later(c):
                        e.wait_ge(vc.sem, vc.at("add", c - 1))
                    for t in range(T):
                        m = e.transpose(pC[:, t * P:(t + 1) * P], yin[:, t * P:(t + 1) * P], ident[:, :])
                    m.then_inc(pc.sem, 1)

                def c_back():
                    c = C[0]
                    e.wait_ge(sc.sem, sc.at("sh", c))
                    for t in range(T):
                        m = e.transpose(pC[:, L + t * P:L + (t + 1) * P], ys[:, t * P:(t + 1) * P], ident[:, :])
                    m.then_inc(pc.sem, 1)

                def c_xn():
                    c = C[0]
                    e.wait_ge(vc.sem, vc.at("xh", c))
                    for t in range(T):
                        m = e.transpose(pC[:, t * P:(t + 1) * P], xh[:, t, :], ident[:, :])
                    m.then_inc(pc.sem, 1)

                def c_h(j):
                    c, s, par, l = C
                    if j == 0:
                        if l is not None:
                            e.wait_ge(sem["mlp_loaded"], 64 * (l + 1))
                        e.wait_ge(sc.sem, sc.at("xn", c))
                    else:
                        e.wait_ge(vc.sem, vc.at(f"hid{j - 1}", c))
                    e.matmul(pC[:, 0:L], w1[:, j, :], xnT[:, :], start=True, stop=True)
                    e.matmul(pC[:, L:2 * L], w1[:, HC + j, :], xnT[:, :], start=True, stop=True).then_inc(pc.sem, 1)

                def c_w2():
                    c = C[0]
                    e.wait_ge(vc.sem, vc.at("hid2", c))
                    for t in range(T):
                        for j in range(HC):
                            e.matmul(pC[:, t * P:(t + 1) * P], hh[:, j, t * P:(t + 1) * P], w2[:, j, :], start=j == 0, stop=False)
                        m = e.matmul(pC[:, t * P:(t + 1) * P], ones[:, :], b2[:, :], start=False, stop=True)
                    m.then_inc(pc.sem, 1)

                if A:
                    a_xt()
                if C:
                    c_xt()
                for u in range(4):
                    if B:
                        b_s(u)
                    if C and u == 1:
                        c_back()
                    if A:
                        a_qk(u)
                    if B and u:
                        b_pt(u - 1)
                    if A:
                        if u >= 2:
                            a_tr(u - 2)
                        a_v(u)
                    if B and u:
                        b_pv(u - 1)
                    if C and u == 2:
                        c_xn()
                    if C and u == 3:
                        c_h(0)
                if A:
                    a_tr(2)
                if B:
                    b_pt(3)
                    b_pv(3)
                if C:
                    c_h(1)
                if B:
                    b_wo()
                if A:
                    a_tr(3)
                if C:
                    c_h(2)
                    c_w2()
            passes(run, e)


def layout(i):
    f = np.float32

    def rows(a, inner=P):
        return a.reshape(a.shape[0] // inner, inner, *a.shape[1:]).swapaxes(0, 1)
    a = {}
    g = lambda k: np.asarray(i[k])
    a["x"] = g("L0_attn_x").reshape(NSEQ, T, P, D).transpose(2, 0, 1, 3)
    a["a_win"] = rows(g("L0_attn_W_in"))
    a["a_wxd"] = rows(np.concatenate([g("L0_attn_W_dt").T, g("L0_attn_W_x").T], 1))
    a["a_cw"] = rows(g("L0_attn_conv_w")[:, 0, :])
    a["a_bias_in"] = rows(np.stack([g("L0_attn_b_in"), g("L0_attn_conv_b")], 1))
    a["a_svec"] = np.stack([g("L0_attn_b_dt"), g("L0_attn_b_x"), g("L0_attn_A_log")], 1)
    a["a_dmt"] = rows(g("L0_attn_D_mat").T)
    a["a_wot"] = rows(g("L0_attn_W_out").T)
    a["a_bout"] = g("L0_attn_b_out")[None]
    a["b_wg"] = g("L0_ffn_w_gate").transpose(2, 0, 1)
    a["b_wu"] = g("L0_ffn_w_up").transpose(2, 0, 1)
    a["b_wd"] = rows(g("L0_ffn_w_down").transpose(2, 0, 1).reshape(FI, NE * D))
    a["b_rgu"] = np.concatenate([g("L0_ffn_router_gate").T, g("L0_ffn_router_up").T], 1)
    a["b_rd"] = rows(g("L0_ffn_router_down").T)
    a["c_winT"] = g("L1_attn_W_in").T
    a["c_winu"] = rows(g("L1_attn_W_in")[0:DI])
    a["c_cw"] = g("L1_attn_conv_w")[:, 0, :].T[None]
    a["c_cvb"] = g("L1_attn_conv_b").reshape(CI, P).T
    a["c_gb"] = np.stack([g("L1_attn_ln_gamma"), g("L1_attn_ln_beta")], 1)
    a["c_wot"] = rows(g("L1_attn_W_out").T)
    a["c_am"] = np.stack([g("L1_attn_A"), g("L1_attn_A").T], 1)
    a["c_bmT"] = rows(g("L1_attn_Bm").T)
    a["c_cm"] = g("L1_attn_Cm")
    a["wqkv"] = g("L1_ffn_Wqkv")
    a["wo"] = g("L1_ffn_Wo").reshape(DEPTH, HEADS * HD // P, P, D).transpose(0, 2, 1, 3)
    m = g("L1_ffn_W2").shape[1]
    w1 = np.zeros((DEPTH, D, 2, HC * P), f)
    w1[:, :, :, :m] = g("L1_ffn_W1").reshape(DEPTH, D, 2, m)
    a["w1"] = w1.reshape(DEPTH, D, 2 * HC, P)
    w2 = np.zeros((DEPTH, HC * P, D), f)
    w2[:, :m] = g("L1_ffn_W2")
    a["w2"] = w2.reshape(DEPTH, HC, P, D).transpose(0, 2, 1, 3)
    b1 = np.zeros((DEPTH, 2, HC * P), f)
    b1[:, :, :m] = g("L1_ffn_b1").reshape(DEPTH, 2, m)
    a["vec"] = np.concatenate([np.stack([g("L1_ffn_ln_g"), g("L1_ffn_ln_b")], 2),
                               b1.reshape(DEPTH, 2 * HC, P).transpose(0, 2, 1)], 2)
    a["b2"] = g("L1_ffn_b2")[:, None]
    q, k = g("L1_ffn_q_scale"), g("L1_ffn_k_scale")
    swap = lambda v: np.concatenate([v[:, HD // 2:], v[:, :HD // 2]], 1)
    a["rows"] = np.stack([q, swap(q), k, swap(k)], 1)[:, None]
    a["ident"] = np.eye(P, dtype=f)
    a["ones"] = np.ones((1, P), f)
    a["iota"] = np.tile(np.arange(NE, dtype=f), (P, 1))
    a["ind"] = np.stack([(np.arange(L) >= TAPS - 1 - t) for t in range(TAPS)] + [np.ones(L, bool)]).astype(f)
    half = np.arange(0, HD, 2, dtype=f)
    inv = (f(1) / f(10000) ** (half / f(HD))).astype(f)
    t = np.arange(L, dtype=f)
    fr = np.concatenate([t[:, None] * inv[None]] * 2, 1)
    base = (half + f(0.4 * HD)) / f(1.4 * HD)
    sc = base[None].astype(np.float64) ** ((t[:, None] - L // 2) / (WIN // 2))
    sc = np.concatenate([sc, sc], 1)
    sign = np.where(np.arange(HD) < HD // 2, -1.0, 1.0)
    co, si = np.cos(fr.astype(np.float64)), np.sin(fr.astype(np.float64)) * sign
    tab = np.stack([co * sc, si * sc, co / sc, si / sc], 1).astype(f)
    a["tab"] = tab.reshape(T, P, 4, HD).swapaxes(0, 1)
    qi, kj = np.arange(WIN)[:, None], np.arange(WIN)[None]
    pair = np.concatenate([np.where(qi > kj, -1e30, 0), np.where(qi < kj, -1e30, 0)], 1)
    mask = np.stack([pair] * NW, 1)
    mask[:, 4, 0:WIN] = -1e30
    a["mask"] = np.tile(mask.reshape(WIN, NW * KEYS), (4, 1)).astype(f)
    return {k: np.ascontiguousarray(v) for k, v in a.items()}


def kernel(**inputs):
    import concourse.bacc as _bacc
    from concourse.bass_utils import run_bass_kernel_spmd as _run

    nc = _bacc.Bacc("TRN2", target_bir_lowering=False, num_devices=1)
    arrays = layout(inputs)
    I = {k: nc.dram_tensor("in_" + k, v.shape, mybir.dt.from_np(v.dtype), kind="ExternalInput").ap() for k, v in arrays.items()}
    out = nc.dram_tensor("out", (P, NSEQ, T, D), F32, kind="ExternalOutput").ap()
    program(nc, I, out)
    r = _run(nc, [{"in_" + k: v for k, v in arrays.items()}], core_ids=[0])
    return r.results[0]["out"].transpose(1, 2, 0, 3).reshape(NSEQ, L, D)
```

```python
from contextlib import ExitStack

import numpy as np
import concourse.bass as bass
from concourse import mybir

F32 = mybir.dt.float32
BF16 = mybir.dt.bfloat16
I32 = mybir.dt.int32
U32 = mybir.dt.uint32
ALU = mybir.AluOpType
ACT = mybir.ActivationFunctionType
AX = mybir.AxisListType

NSEQ, L, D, P = 16, 256, 128, 128
T = L // P
DI = 256
CI = DI // P
TAPS = 4
S0, S1 = 64, 16
NE, FI = 8, 512
CF = FI // P
DEPTH, HEADS, HD, WIN = 6, 16, 64, 32
NW = L // WIN
NG = 4
KEYS = 2 * WIN
HALF = D // 2
HC = 3
EPS = 1e-5
ROUNDS = 3
RS = 1 + 4 * ROUNDS
VRS = 3 + 3 * ROUNDS
MAGIC = float(0x5F3759DF)


class Steps:

    def __init__(self, ctx, nc, name, steps):
        self.sem = ctx.enter_context(nc.semaphore(name))
        self.index, k = {}, 0
        for s in steps.split():
            s, _, m = s.partition("*")
            k += int(m or 1)
            self.index[s] = k
        self.per = k

    def passed(self, n):
        return n * self.per

    def at(self, step, n, back=0):
        return n * self.per + (self.index[step] - back)


def later(n):
    return not isinstance(n, int) or n > 0


def each_sequence(eng, body):
    body(0)
    with eng.Fori(1, NSEQ) as s:
        body(s)


def at_rest(eng):
    eng.nop(nofuse=True)


def newton_rsqrt(eng, st, n, step, y, var, h, t):
    def own(k):
        count = st.at(step, n, RS - k)
        if not isinstance(count, int) or count > 0:
            eng.wait_ge(st.sem, count)
            at_rest(eng)
    own(0)
    eng.tensor_scalar(h, var, -0.5, 0.0, ALU.mult, ALU.add).then_inc(st.sem, 1)
    for r in range(ROUNDS):
        if r:
            own(1 + 4 * r)
        eng.tensor_tensor(t, y, y, ALU.mult).then_inc(st.sem, 1)
        own(2 + 4 * r)
        eng.tensor_tensor(t, t, h, ALU.mult).then_inc(st.sem, 1)
        own(3 + 4 * r)
        eng.tensor_scalar(t, t, 1.0, 1.5, ALU.mult, ALU.add).then_inc(st.sem, 1)
        own(4 + 4 * r)
        eng.tensor_tensor(y, y, t, ALU.mult).then_inc(st.sem, 1)


def vector_rsqrt(v, st, n, step, y, var, h, t):
    def own(k):
        v.wait_ge(st.sem, st.at(step, n, VRS - k))
    own(0)
    v.tensor_scalar(y.bitcast(I32), var.bitcast(I32), 1, None, ALU.logical_shift_right).then_inc(st.sem, 1)
    v.tensor_scalar(h, var, -0.5, None, ALU.mult).then_inc(st.sem, 1)
    own(1)
    v.tensor_scalar(y.bitcast(I32), y.bitcast(I32), -1.0, MAGIC, ALU.mult, ALU.add).then_inc(st.sem, 1)
    for r in range(ROUNDS):
        own(3 + 3 * r)
        v.tensor_tensor(t, y, y, ALU.mult).then_inc(st.sem, 1)
        own(4 + 3 * r)
        v.tensor_tensor(t, t, h, ALU.mult).then_inc(st.sem, 1)
        own(5 + 3 * r)
        v.scalar_tensor_tensor(y, t, 1.5, y, ALU.add, ALU.mult).then_inc(st.sem, 1)


def layernorm_stats(v, st, n, src, stats, mv, step_in):
    for t in range(T):
        v.bn_stats(stats[:, t, :], src(t)).then_inc(st.sem, 1)
    v.wait_ge(st.sem, st.at(step_in + "bn", n))
    at_rest(v)
    for t in range(T):
        v.bn_aggr(mv[:, t, :], stats[:, t, :]).then_inc(st.sem, 1)


def rsqrt_seed(v, st, n, pre, var, bits):
    v.tensor_scalar(bits, var, 1, None, ALU.logical_shift_right).then_inc(st.sem, 1)
    v.wait_ge(st.sem, st.at(pre + "sh", n))
    v.tensor_scalar(bits, bits, -1.0, MAGIC, ALU.mult, ALU.add).then_inc(st.sem, 1)


def program(nc, I, out):
    top = ExitStack()
    with top:
        X = top.enter_context(nc.sbuf_tensor("X", [P, NSEQ, T, D], F32))
        ident = top.enter_context(nc.sbuf_tensor("ident", [P, P], F32))
        ssm_phase(nc, I, X, ident)
        moe_phase(nc, I, X, ident)
        ssm2_phase(nc, I, X, ident)
        transformer_phase(nc, I, X, ident, out)


def tools(nc):
    ctx = ExitStack()

    def sb(name, shape, dt=F32):
        return ctx.enter_context(nc.sbuf_tensor(name, shape, dt))

    def ps(name, shape, dt=F32):
        return ctx.enter_context(nc.psum_tensor(name, shape, dt))
    return ctx, sb, ps


def ssm_phase(nc, I, X, ident):
    ctx, sb, ps = tools(nc)
    with ctx:
        win = sb("a_win", [P, CI, D])
        wxd = sb("a_wxd", [P, CI, 2 * S0])
        cw = sb("a_cw", [P, CI, TAPS])
        bias_in = sb("a_bias_in", [P, CI, 2])
        svec = sb("a_svec", [S0, 3])
        dmt = sb("a_dmt", [P, CI, S0])
        wot = sb("a_wot", [P, CI, D])
        bout = sb("a_bout", [1, D])
        ind = sb("a_ind", [TAPS + 1, L])
        ones = sb("a_ones", [1, P])
        scaled = sb("a_scaled", [P, CI, TAPS, 2 * S0])
        bsc = sb("a_bsc", [P, CI, TAPS + 1])
        fused = sb("a_fused", [P, TAPS, 2 * S0])
        beta = sb("a_beta", [TAPS + 1, 2 * S0])
        wzo = sb("a_wzo", [S0, D])
        aneg = sb("a_aneg", [S0, 2])
        ealog = sb("a_ealog", [S0, 1])
        xst = sb("a_xst", [P, 2, L])
        xpad = sb("a_xpad", [P, 2, TAPS - 1 + L])
        pre = sb("a_pre", [S0, 4, L])
        dt_ = sb("a_dt", [S0, L])
        dA = sb("a_dA", [S0, L])
        wx = sb("a_wx", [S0, L])
        om = sb("a_om", [S0, L])
        dbx = sb("a_dbx", [S0, L])
        z = sb("a_z", [S0, 2, L])
        res = sb("a_res", [P, T, D])
        stats = sb("a_stats", [P, T, 6])
        mv = sb("a_mv", [P, T, 2])
        ve = sb("a_ve", [P, T])
        y = sb("a_y", [P, T])
        h = sb("a_h", [P, T])
        tt = sb("a_t", [P, T])
        pf = ps("a_pf", [P, 512])
        pb = ps("a_pb", [TAPS + 1, 512])
        px = ps("a_px", [P, 512])
        pu = ps("a_pu", [S0, 512])
        pz = ps("a_pz", [P, 512])
        loaded = ctx.enter_context(nc.semaphore("a_loaded"))
        xl = ctx.enter_context(nc.semaphore("a_xl"))
        pset = ctx.enter_context(nc.semaphore("a_pset"))
        vset = ctx.enter_context(nc.semaphore("a_vset"))
        aset = ctx.enter_context(nc.semaphore("a_aset"))
        gset = ctx.enter_context(nc.semaphore("a_gset"))
        pe = Steps(ctx, nc, "a_pe", "xt u y")
        va = Steps(ctx, nc, "a_va", "pre rel wx om dbx scan res bn*2 ag*2 ve sh sd out*2")
        aa = Steps(ctx, nc, "a_aa", "xpad abs exp ln dA")
        ga = Steps(ctx, nc, "a_ga", f"stage rs*{RS}")
        LOADS = 11
        block = ctx.enter_context(nc.Block())

        @block.sync
        def _(e):
            for dst, src in [(ident[:, :], I["ident"]), (win[:, :, :], I["a_win"]), (wxd[:, :, :], I["a_wxd"]),
                             (cw[:, :, :], I["a_cw"]), (bias_in[:, :, :], I["a_bias_in"]), (svec[:, :], I["a_svec"]),
                             (dmt[:, :, :], I["a_dmt"]), (wot[:, :, :], I["a_wot"]), (bout[:, :], I["a_bout"]),
                             (ind[:, :], I["ind"]), (ones[:, :], I["ones"])]:
                e.dma_start(dst, src).then_inc(loaded, 16)
            e.dma_start(X[:, :, :, :], I["x"]).then_inc(xl, 16)

        @block.gpsimd
        def _(e):
            e.memset(xpad[:, :, 0:TAPS - 1], 0.0).then_inc(gset, 1)
            e.wait_ge(xl, 16)
            def sequence(s):
                if later(s):
                    e.wait_ge(pe.sem, pe.passed(s))
                at_rest(e)
                e.tensor_copy(xst[:, 0, :], X[:, s, :, :].rearrange("p t d -> p (t d)")).then_inc(ga.sem, 1)
                e.wait_ge(va.sem, va.at("sd", s))
                at_rest(e)
                newton_rsqrt(e, ga, s, "rs", y[:, :], ve[:, :], h[:, :], tt[:, :])
            each_sequence(e, sequence)

        @block.vector
        def _(e):
            e.wait_ge(loaded, 16 * LOADS)
            for c in range(CI):
                for k in range(TAPS):
                    e.tensor_scalar(scaled[:, c, k, :], wxd[:, c, :], cw[:, c, k:k + 1], None, ALU.mult).then_inc(vset, 1)
                e.tensor_scalar(bsc[:, c, 0:TAPS], cw[:, c, :], bias_in[:, c, 0:1], None, ALU.mult).then_inc(vset, 1)
                e.tensor_copy(bsc[:, c, TAPS:TAPS + 1], bias_in[:, c, 1:2]).then_inc(vset, 1)
            e.wait_ge(pset, 1)
            e.tensor_copy(fused[:, :, :], pf[:, :].rearrange("p (k m) -> p k m", k=TAPS)).then_inc(vset, 1)
            e.tensor_copy(beta[:, :], pb[:, 0:2 * S0]).then_inc(vset, 1)
            e.wait_ge(pset, 2)
            e.tensor_copy(wzo[:, :], pf[0:S0, 0:D]).then_inc(vset, 1)
            e.wait_ge(aset, 1)
            e.tensor_scalar(aneg[:, 0:1], ealog[:, :], -1.0, None, ALU.mult).then_inc(vset, 1)
            e.wait_ge(vset, CI * (TAPS + 2) + 4)
            e.reciprocal(aneg[:, 1:2], aneg[:, 0:1]).then_inc(vset, 1)
            e.wait_ge(vset, CI * (TAPS + 2) + 5)
            def sequence(s):
                e.wait_ge(pe.sem, pe.at("u", s))
                if later(s):
                    e.wait_ge(aa.sem, aa.passed(s))
                e.tensor_scalar(pre[:, 0, :], pu[:, 0:L], svec[:, 0:1], None, ALU.add).then_inc(va.sem, 1)
                e.wait_ge(aa.sem, aa.at("ln", s))
                e.scalar_tensor_tensor(dt_[:, :], pre[:, 0, :], 0.0, pre[:, 3, :], ALU.max, ALU.add).then_inc(va.sem, 1)
                e.tensor_scalar(wx[:, :], pu[:, L:2 * L], svec[:, 1:2], aneg[:, 1:2], ALU.add, ALU.mult).then_inc(va.sem, 1)
                e.wait_ge(aa.sem, aa.at("dA", s))
                e.tensor_scalar(om[:, :], dA[:, :], -1.0, 1.0, ALU.mult, ALU.add).then_inc(va.sem, 1)
                e.wait_ge(va.sem, va.at("om", s))
                e.tensor_tensor(dbx[:, :], om[:, :], wx[:, :], ALU.mult).then_inc(va.sem, 1)
                e.wait_ge(va.sem, va.at("dbx", s))
                e.tensor_tensor_scan(z[:, 0, :], dA[:, :], dbx[:, :], 0.0, ALU.mult, ALU.add).then_inc(va.sem, 1)
                e.wait_ge(pe.sem, pe.at("y", s))
                e.tensor_tensor(res[:, :, :], X[:, s, :, :], pz[:, 0:L].rearrange("p (t d) -> p t d", t=T), ALU.add)\
                    .then_inc(va.sem, 1)
                e.wait_ge(va.sem, va.at("res", s))
                layernorm_stats(e, va, s, lambda t: res[:, t, :], stats, mv, "")
                e.wait_ge(va.sem, va.at("ag", s))
                e.tensor_scalar(ve[:, :], mv[:, :, 1], EPS, None, ALU.add).then_inc(va.sem, 1)
                e.wait_ge(va.sem, va.at("ve", s))
                rsqrt_seed(e, va, s, "", ve[:, :].bitcast(I32), y[:, :].bitcast(I32))
                e.wait_ge(ga.sem, ga.at("rs", s))
                for t in range(T):
                    e.tensor_scalar(X[:, s, t, :], res[:, t, :], mv[:, t, 0:1], y[:, t:t + 1], ALU.subtract, ALU.mult)\
                        .then_inc(va.sem, 1)
            each_sequence(e, sequence)

        @block.scalar
        def _(e):
            e.wait_ge(loaded, 16 * LOADS)
            e.activation(ealog[:, :], svec[:, 2:3], ACT.Exp).then_inc(aset, 1)
            e.wait_ge(gset, 1)
            e.wait_ge(vset, CI * (TAPS + 2) + 5)
            def sequence(s):
                e.wait_ge(pe.sem, pe.at("xt", s))
                e.activation(xpad[:, 0, TAPS - 1:], px[:, 0:L], ACT.Copy).then_inc(aa.sem, 1)
                e.wait_ge(va.sem, va.at("pre", s))
                e.activation(pre[:, 1, :], pre[:, 0, :], ACT.Abs).then_inc(aa.sem, 1)
                e.wait_ge(aa.sem, aa.at("abs", s))
                e.activation(pre[:, 2, :], pre[:, 1, :], ACT.Exp, scale=-1.0).then_inc(aa.sem, 1)
                e.wait_ge(aa.sem, aa.at("exp", s))
                e.activation(pre[:, 3, :], pre[:, 2, :], ACT.Ln, bias=1.0).then_inc(aa.sem, 1)
                e.wait_ge(va.sem, va.at("rel", s))
                e.activation(dA[:, :], dt_[:, :], ACT.Exp, scale=aneg[:, 0:1]).then_inc(aa.sem, 1)
            each_sequence(e, sequence)

        @block.tensor
        def _(e):
            e.wait_ge(loaded, 16 * LOADS)
            e.wait_ge(vset, CI * (TAPS + 2))
            for k in range(TAPS):
                for c in range(CI):
                    e.matmul(pf[:, k * P:(k + 1) * P], win[:, c, :], scaled[:, c, k, :], start=c == 0, stop=c == CI - 1)
            for c in range(CI):
                m = e.matmul(pb[:, 0:2 * S0], bsc[:, c, :], wxd[:, c, :], start=c == 0, stop=c == CI - 1)
            m.then_inc(pset, 1)
            e.wait_ge(vset, CI * (TAPS + 2) + 2)
            for c in range(CI):
                m = e.matmul(pf[0:S0, 0:D], dmt[:, c, :], wot[:, c, :], start=c == 0, stop=c == CI - 1)
            m.then_inc(pset, 1)
            e.wait_ge(vset, CI * (TAPS + 2) + 3)
            def sequence(s):
                e.wait_ge(ga.sem, ga.at("stage", s))
                if later(s):
                    e.wait_ge(aa.sem, aa.passed(s))
                for t in range(T):
                    m = e.transpose(px[:, t * P:(t + 1) * P], xst[:, 0, t * P:(t + 1) * P], ident[:, :])
                m.then_inc(pe.sem, 1)
                e.wait_ge(aa.sem, aa.at("xpad", s))
                for a in range(2):
                    o = pu[:, a * L:(a + 1) * L]
                    for k in range(TAPS):
                        e.matmul(o, fused[:, k, a * S0:(a + 1) * S0], xpad[:, 0, k:k + L], start=k == 0, stop=False)
                    m = e.matmul(o, beta[:, a * S0:(a + 1) * S0], ind[:, :], start=False, stop=True)
                m.then_inc(pe.sem, 1)
                e.wait_ge(va.sem, va.at("scan", s))
                for t in range(T):
                    o = pz[:, t * P:(t + 1) * P]
                    e.matmul(o, z[:, 0, t * P:(t + 1) * P], wzo[:, :], start=True, stop=False)
                    m = e.matmul(o, ones[:, :], bout[:, :], start=False, stop=True)
                m.then_inc(pe.sem, 1)
            each_sequence(e, sequence)


def moe_phase(nc, I, X, ident):
    ctx, sb, ps = tools(nc)
    with ctx:
        wg = sb("b_wg", [P, NE, FI])
        wu = sb("b_wu", [P, NE, FI])
        wd = sb("b_wd", [P, CF, NE * D])
        rgu = sb("b_rgu", [P, 2 * NE])
        rd = sb("b_rd", [P, CF, NE])
        iota = sb("b_iota", [P, NE])
        xst = sb("b_xst", [P, L])
        xT = sb("b_xT", [P, L])
        lg = sb("b_lg", [P, 3 * T, NE])
        mx = sb("b_mx", [P, 3 * T, 8])
        ix = sb("b_ix", [P, 3 * T, 8], U32)
        ixf = sb("b_ixf", [P, 3 * T, 8])
        df = sb("b_df", [P, 3 * T])
        ex = sb("b_ex", [P, 3 * T])
        sm = sb("b_sm", [P, 3 * T])
        pr = sb("b_pr", [P, 2, 3 * T])
        oh = sb("b_oh", [P, 3 * T, NE])
        o2 = sb("b_o2", [P, 3 * T, NE])
        cb = sb("b_cb", [P, 3 * T, NE])
        xc = sb("b_xc", [P, T, 2 * NE, D])
        xcT = sb("b_xcT", [P, 2 * NE, L])
        sig = sb("b_sig", [P, CF, L])
        it = sb("b_it", [P, CF, L])
        acc = sb("b_acc", [P, T, D])
        stats = sb("b_stats", [P, T, 6])
        mv = sb("b_mv", [P, T, 2])
        ve = sb("b_ve", [P, T])
        y = sb("b_y", [P, T])
        h = sb("b_h", [P, T])
        tt = sb("b_t", [P, T])
        pg = ps("b_pg", [P, CF, L])
        pu = ps("b_pu", [P, CF, L])
        pd = ps("b_pd", [P, NE, D])
        pm = [ps("b_pm0", [P, 512]), ps("b_pm1", [P, 512])]
        loaded = ctx.enter_context(nc.semaphore("b_loaded"))
        pe = Steps(ctx, nc, "b_pe", "xt lg ct*16 g u ld d*2")
        route = "mx{0}*{1} ix{0}*{1} xf{0} df{0} sm{0} p0{0} p1{0} oh{0}*{1} o2{0}*{1} cb{0}"
        va = Steps(ctx, nc, "b_va", "lc " + route.format("g", 2 * T) + f" xc*{T * 2 * NE} gu ldc "
                   + route.format("d", T) + f" acc*{T * NE} bn*2 ag*2 ve sh sd out*2")
        aa = Steps(ctx, nc, "b_aa", "xT exg ctc*16 sig exd")
        ga = Steps(ctx, nc, "b_ga", f"stage rs*{RS}")
        LOADS = 6
        block = ctx.enter_context(nc.Block())

        @block.sync
        def _(e):
            for dst, src in [(rgu[:, :], I["b_rgu"]), (iota[:, :], I["iota"]), (rd[:, :, :], I["b_rd"]),
                             (wg[:, :, :], I["b_wg"]), (wu[:, :, :], I["b_wu"]), (wd[:, :, :], I["b_wd"])]:
                e.dma_start(dst, src).then_inc(loaded, 16)

        @block.gpsimd
        def _(e):
            def sequence(s):
                if later(s):
                    e.wait_ge(pe.sem, pe.passed(s))
                if later(s):
                    e.wait_ge(va.sem, va.passed(s))
                at_rest(e)
                e.tensor_copy(xst[:, :], X[:, s, :, :].rearrange("p t d -> p (t d)")).then_inc(ga.sem, 1)
                e.wait_ge(va.sem, va.at("sd", s))
                at_rest(e)
                newton_rsqrt(e, ga, s, "rs", y[:, :], ve[:, :], h[:, :], tt[:, :])
            each_sequence(e, sequence)

        def top2(e, s, q, a, b):
            at_rest(e)
            for j in range(a, b):
                e.max(mx[:, j, :], lg[:, j, :]).then_inc(va.sem, 1)
            e.wait_ge(va.sem, va.at("mx" + q, s))
            at_rest(e)
            for j in range(a, b):
                e.max_index(ix[:, j, :], mx[:, j, :], lg[:, j, :]).then_inc(va.sem, 1)
            e.wait_ge(va.sem, va.at("ix" + q, s))
            e.tensor_copy(ixf[:, a:b, :], ix[:, a:b, :]).then_inc(va.sem, 1)
            e.tensor_tensor(df[:, a:b], mx[:, a:b, 1], mx[:, a:b, 0], ALU.subtract).then_inc(va.sem, 1)
            e.wait_ge(aa.sem, aa.at("ex" + q, s))
            e.tensor_scalar(sm[:, a:b], ex[:, a:b], 1.0, None, ALU.add).then_inc(va.sem, 1)
            e.wait_ge(va.sem, va.at("sm" + q, s))
            e.reciprocal(pr[:, 0, a:b], sm[:, a:b]).then_inc(va.sem, 1)
            e.wait_ge(va.sem, va.at("p0" + q, s))
            e.tensor_tensor(pr[:, 1, a:b], pr[:, 0, a:b], ex[:, a:b], ALU.mult).then_inc(va.sem, 1)
            e.wait_ge(va.sem, va.at("p1" + q, s))
            for j in range(a, b):
                e.tensor_scalar(oh[:, j, :], iota[:, :], ixf[:, j, 0:1], pr[:, 0, j:j + 1], ALU.is_equal, ALU.mult)\
                    .then_inc(va.sem, 1)
            for j in range(a, b):
                e.tensor_scalar(o2[:, j, :], iota[:, :], ixf[:, j, 1:2], pr[:, 1, j:j + 1], ALU.is_equal, ALU.mult)\
                    .then_inc(va.sem, 1)
            e.wait_ge(va.sem, va.at("o2" + q, s))
            e.tensor_tensor(cb[:, a:b, :], oh[:, a:b, :], o2[:, a:b, :], ALU.add).then_inc(va.sem, 1)
            e.wait_ge(va.sem, va.at("cb" + q, s))

        @block.vector
        def _(e):
            e.wait_ge(loaded, 16 * LOADS)
            def sequence(s):
                e.wait_ge(pe.sem, pe.at("lg", s))
                e.tensor_copy(lg[:, 0:2 * T, :], pm[1][:, 0:2 * T * NE].rearrange("p (j n) -> p j n", n=NE)).then_inc(va.sem, 1)
                e.wait_ge(va.sem, va.at("lc", s))
                top2(e, s, "g", 0, 2 * T)
                for t in range(T):
                    for r in range(2):
                        for n in range(NE):
                            if t == 0 and r == 0 and n == 0:
                                if later(s):
                                    e.wait_ge(pe.sem, pe.passed(s))
                            j = 2 * t + r
                            e.tensor_scalar(xc[:, t, r * NE + n, :], xst[:, t * D:(t + 1) * D], cb[:, j, n:n + 1],
                                            None, ALU.mult).then_inc(va.sem, 1)
                e.wait_ge(aa.sem, aa.at("sig", s))
                e.wait_ge(pe.sem, pe.at("u", s))
                e.tensor_tensor(it[:, :, :], pu[:, :, :], sig[:, :, :], ALU.mult).then_inc(va.sem, 1)
                e.wait_ge(pe.sem, pe.at("ld", s))
                e.tensor_copy(lg[:, 2 * T:3 * T, :], pm[1][:, 0:T * NE].rearrange("p (j n) -> p j n", n=NE)).then_inc(va.sem, 1)
                e.wait_ge(va.sem, va.at("ldc", s))
                top2(e, s, "d", 2 * T, 3 * T)
                for t in range(T):
                    e.wait_ge(pe.sem, pe.at("d", s, T - 1 - t))
                    for n in range(NE):
                        src = xst[:, t * D:(t + 1) * D] if n == 0 else acc[:, t, :]
                        if n:
                            e.wait_ge(va.sem, va.at("acc", s, T * NE - t * NE - n))
                        e.scalar_tensor_tensor(acc[:, t, :], pd[:, n, :], cb[:, 2 * T + t, n:n + 1], src,
                                               ALU.mult, ALU.add).then_inc(va.sem, 1)
                e.wait_ge(va.sem, va.at("acc", s))
                layernorm_stats(e, va, s, lambda t: acc[:, t, :], stats, mv, "")
                e.wait_ge(va.sem, va.at("ag", s))
                e.tensor_scalar(ve[:, :], mv[:, :, 1], EPS, None, ALU.add).then_inc(va.sem, 1)
                e.wait_ge(va.sem, va.at("ve", s))
                rsqrt_seed(e, va, s, "", ve[:, :].bitcast(I32), y[:, :].bitcast(I32))
                e.wait_ge(ga.sem, ga.at("rs", s))
                for t in range(T):
                    e.tensor_scalar(X[:, s, t, :], acc[:, t, :], mv[:, t, 0:1], y[:, t:t + 1], ALU.subtract, ALU.mult)\
                        .then_inc(va.sem, 1)
            each_sequence(e, sequence)

        @block.scalar
        def _(e):
            def sequence(s):
                e.wait_ge(pe.sem, pe.at("xt", s))
                e.activation(xT[:, :], pm[0][:, 0:L], ACT.Copy).then_inc(aa.sem, 1)
                e.wait_ge(va.sem, va.at("dfg", s))
                e.activation(ex[:, 0:2 * T], df[:, 0:2 * T], ACT.Exp).then_inc(aa.sem, 1)
                for n in range(2 * NE):
                    e.wait_ge(pe.sem, pe.at("ct", s, 2 * NE - 1 - n))
                    e.activation(xcT[:, n, :], pm[n % 2][:, 0:L], ACT.Copy).then_inc(aa.sem, 1)
                e.wait_ge(pe.sem, pe.at("g", s))
                e.activation(sig[:, :, :], pg[:, :, :], ACT.Silu).then_inc(aa.sem, 1)
                e.wait_ge(va.sem, va.at("dfd", s))
                e.activation(ex[:, 2 * T:3 * T], df[:, 2 * T:3 * T], ACT.Exp).then_inc(aa.sem, 1)
            each_sequence(e, sequence)

        @block.tensor
        def _(e):
            e.wait_ge(loaded, 16 * LOADS)
            def sequence(s):
                e.wait_ge(ga.sem, ga.at("stage", s))
                for t in range(T):
                    m = e.transpose(pm[0][:, t * P:(t + 1) * P], xst[:, t * P:(t + 1) * P], ident[:, :])
                m.then_inc(pe.sem, 1)
                e.wait_ge(aa.sem, aa.at("xT", s))
                for t in range(T):
                    m = e.matmul(pm[1][:, t * 2 * NE:(t + 1) * 2 * NE], xT[:, t * P:(t + 1) * P], rgu[:, :], start=True, stop=True)
                m.then_inc(pe.sem, 1)
                for n in range(2 * NE):
                    e.wait_ge(va.sem, va.at("xc", s))
                    if n >= 2:
                        e.wait_ge(aa.sem, aa.at("ctc", s, 2 * NE + 1 - n))
                    for t in range(T):
                        m = e.transpose(pm[n % 2][:, t * P:(t + 1) * P], xc[:, t, n, :], ident[:, :])
                    m.then_inc(pe.sem, 1)
                for r, (w, o) in enumerate(((wg, pg), (wu, pu))):
                    e.wait_ge(aa.sem, aa.at("ctc", s, NE * (1 - r)))
                    for j in range(CF):
                        for n in range(NE):
                            m = e.matmul(o[:, j, :], w[:, n, j * P:(j + 1) * P], xcT[:, r * NE + n, :], start=n == 0, stop=n == NE - 1)
                    m.then_inc(pe.sem, 1)
                e.wait_ge(va.sem, va.at("gu", s))
                for t in range(T):
                    for j in range(CF):
                        m = e.matmul(pm[1][:, t * NE:(t + 1) * NE], it[:, j, t * P:(t + 1) * P], rd[:, j, :], start=j == 0, stop=j == CF - 1)
                m.then_inc(pe.sem, 1)
                for t in range(T):
                    if t:
                        e.wait_ge(va.sem, va.at("acc", s, (T - t) * NE))
                    for b in range(2):
                        for j in range(CF):
                            m = e.matmul(pd[:, 4 * b:4 * b + 4, :].rearrange("p n d -> p (n d)"), it[:, j, t * P:(t + 1) * P],
                                         wd[:, j, b * 512:(b + 1) * 512], start=j == 0, stop=j == CF - 1)
                    m.then_inc(pe.sem, 1)
            each_sequence(e, sequence)


def ssm2_phase(nc, I, X, ident):
    ctx, sb, ps = tools(nc)
    NK = 8
    with ctx:
        winT = sb("c_winT", [P, 2 * DI])
        winu = sb("c_winu", [P, CI, D])
        cwb = sb("c_cwb", [P, TAPS, DI])
        cvb = sb("c_cvb", [P, CI])
        gb = sb("c_gb", [P, 2])
        wot = sb("c_wot", [P, CI, D])
        am = sb("c_am", [S1, NK, 2, S1])
        bmT = sb("c_bmT", [P, CI, S1])
        cm = sb("c_cm", [S1, DI])
        wc = sb("c_wc", [P, TAPS, DI])
        bw = sb("c_bw", [P, S1])
        xh = sb("c_xh", [P, T, D])
        xn = sb("c_xn", [P, TAPS - 1 + L])
        sg = sb("c_sg", [P, CI, L])
        sz = sb("c_sz", [P, CI, L])
        st = [sb("c_st0", [S1, L]), sb("c_st1", [S1, L])]
        yT = sb("c_yT", [P, CI, L])
        res = sb("c_res", [P, T, D])
        stats = sb("c_stats", [P, T, 6])
        mv = sb("c_mv", [P, 2, T, 2])
        ve = sb("c_ve", [P, 2, T])
        y = sb("c_y", [P, 2, T])
        h = sb("c_h", [P, T])
        tt = sb("c_t", [P, T])
        px = ps("c_px", [P, 512])
        pc = ps("c_pc", [P, CI, L])
        pz = ps("c_pz", [P, CI, L])
        pst = [ps("c_ps0", [S1, 512]), ps("c_ps1", [S1, 512])]
        pk = ps("c_pk", [P, CI, L])
        po = ps("c_po", [P, 512])
        loaded = ctx.enter_context(nc.semaphore("c_loaded"))
        vset = ctx.enter_context(nc.semaphore("c_vset"))
        pset = ctx.enter_context(nc.semaphore("c_pset"))
        gset = ctx.enter_context(nc.semaphore("c_gset"))
        pe = Steps(ctx, nc, "c_pe", f"xt v conv z dbl*{NK} k y")
        va = Steps(ctx, nc, "c_va", f"Ibn*2 Iag*2 Ive Ish Isd xh*2 v0 hd*{NK} ad*{NK} kc ky res bn*2 ag*2 ve sh sd out*2"
                   .replace(f"hd*{NK} ad*{NK}", " ".join(f"hd{k} ad{k}" for k in range(NK))))
        aa = Steps(ctx, nc, "c_aa", "xn sg*2 sz")
        ga = Steps(ctx, nc, "c_ga", f"Irs*{RS} rs*{RS}")
        LOADS = 9
        block = ctx.enter_context(nc.Block())

        @block.sync
        def _(e):
            for dst, src in [(winT[:, :], I["c_winT"]), (winu[:, :, :], I["c_winu"]),
                             (cwb[:, :, :], I["c_cw"].to_broadcast([P, TAPS, DI])),
                             (cvb[:, :], I["c_cvb"]), (gb[:, :], I["c_gb"]), (wot[:, :, :], I["c_wot"]),
                             (am[:, 0, :, :], I["c_am"]), (bmT[:, :, :], I["c_bmT"]), (cm[:, :], I["c_cm"])]:
                e.dma_start(dst, src).then_inc(loaded, 16)

        @block.gpsimd
        def _(e):
            e.memset(xn[:, 0:TAPS - 1], 0.0).then_inc(gset, 1)
            def sequence(s):
                e.wait_ge(va.sem, va.at("Isd", s))
                at_rest(e)
                newton_rsqrt(e, ga, s, "Irs", y[:, 0, :], ve[:, 0, :], h[:, :], tt[:, :])
                e.wait_ge(va.sem, va.at("sd", s))
                e.wait_ge(ga.sem, ga.at("Irs", s))
                at_rest(e)
                newton_rsqrt(e, ga, s, "rs", y[:, 1, :], ve[:, 1, :], h[:, :], tt[:, :])
            each_sequence(e, sequence)

        @block.vector
        def _(e):
            e.wait_ge(loaded, 16 * LOADS)
            for k in range(TAPS):
                e.tensor_tensor(wc[:, k, :], winT[:, 0:DI], cwb[:, k, :], ALU.mult).then_inc(vset, 1)
            e.wait_ge(pset, 1)
            e.tensor_copy(bw[:, :], po[:, 0:S1]).then_inc(vset, 1)
            for k in range(1, NK):
                e.wait_ge(pset, k + 1)
                e.tensor_copy(am[:, k, :, :], pst[0][:, 0:2 * S1].rearrange("p (a b) -> p a b", a=2)).then_inc(vset, 1)
            e.wait_ge(vset, TAPS + NK)
            def sequence(s):
                layernorm_stats(e, va, s, lambda t: X[:, s, t, :], stats, mv[:, 0, :, :], "I")
                e.wait_ge(va.sem, va.at("Iag", s))
                e.tensor_scalar(ve[:, 0, :], mv[:, 0, :, 1], EPS, None, ALU.add).then_inc(va.sem, 1)
                e.wait_ge(va.sem, va.at("Ive", s))
                rsqrt_seed(e, va, s, "I", ve[:, 0, :].bitcast(I32), y[:, 0, :].bitcast(I32))
                e.wait_ge(ga.sem, ga.at("Irs", s))
                for t in range(T):
                    e.tensor_scalar(xh[:, t, :], X[:, s, t, :], mv[:, 0, t, 0:1], y[:, 0, t:t + 1], ALU.subtract, ALU.mult)\
                        .then_inc(va.sem, 1)
                e.wait_ge(pe.sem, pe.at("v", s))
                e.tensor_copy(st[0][:, :], po[0:S1, 0:L]).then_inc(va.sem, 1)
                for k in range(NK):
                    a, b, d = st[k % 2], st[(k + 1) % 2], 1 << k
                    e.wait_ge(va.sem, va.at(f"ad{k - 1}" if k else "v0", s))
                    e.tensor_copy(b[:, 0:d], a[:, 0:d]).then_inc(va.sem, 1)
                    e.wait_ge(pe.sem, pe.at("dbl", s, NK - 1 - k))
                    e.tensor_tensor(b[:, d:L], pst[k % 2][:, 0:L - d], a[:, d:L], ALU.add).then_inc(va.sem, 1)
                e.wait_ge(aa.sem, aa.at("sg", s))
                e.wait_ge(pe.sem, pe.at("k", s))
                e.tensor_tensor(yT[:, :, :], pk[:, :, :], sg[:, :, :], ALU.add).then_inc(va.sem, 1)
                e.wait_ge(va.sem, va.at("kc", s))
                e.wait_ge(aa.sem, aa.at("sz", s))
                e.tensor_tensor(yT[:, :, :], yT[:, :, :], sz[:, :, :], ALU.mult).then_inc(va.sem, 1)
                e.wait_ge(pe.sem, pe.at("y", s))
                e.scalar_tensor_tensor(res[:, :, :], X[:, s, :, :], 2.0, po[:, 0:L].rearrange("p (t d) -> p t d", t=T),
                                       ALU.mult, ALU.add).then_inc(va.sem, 1)
                e.wait_ge(va.sem, va.at("res", s))
                layernorm_stats(e, va, s, lambda t: res[:, t, :], stats, mv[:, 1, :, :], "")
                e.wait_ge(va.sem, va.at("ag", s))
                e.tensor_scalar(ve[:, 1, :], mv[:, 1, :, 1], EPS, None, ALU.add).then_inc(va.sem, 1)
                e.wait_ge(va.sem, va.at("ve", s))
                rsqrt_seed(e, va, s, "", ve[:, 1, :].bitcast(I32), y[:, 1, :].bitcast(I32))
                e.wait_ge(ga.sem, ga.at("rs", s))
                for t in range(T):
                    e.tensor_scalar(X[:, s, t, :], res[:, t, :], mv[:, 1, t, 0:1], y[:, 1, t:t + 1], ALU.subtract, ALU.mult)\
                        .then_inc(va.sem, 1)
            each_sequence(e, sequence)

        @block.scalar
        def _(e):
            e.wait_ge(loaded, 16 * LOADS)
            e.wait_ge(gset, 1)
            def sequence(s):
                e.wait_ge(pe.sem, pe.at("xt", s))
                e.activation(xn[:, TAPS - 1:], px[:, 0:L], ACT.Identity, bias=gb[:, 1:2], scale=gb[:, 0:1]).then_inc(aa.sem, 1)
                e.wait_ge(pe.sem, pe.at("conv", s))
                for c in range(CI):
                    e.activation(sg[:, c, :], pc[:, c, :], ACT.Silu, bias=cvb[:, c:c + 1]).then_inc(aa.sem, 1)
                e.wait_ge(pe.sem, pe.at("z", s))
                e.activation(sz[:, :, :], pz[:, :, :], ACT.Sigmoid).then_inc(aa.sem, 1)
            each_sequence(e, sequence)

        @block.tensor
        def _(e):
            e.wait_ge(loaded, 16 * LOADS)
            for c in range(CI):
                m = e.matmul(po[:, 0:S1], winu[:, c, :], bmT[:, c, :], start=c == 0, stop=c == CI - 1)
            m.then_inc(pset, 1)
            for k in range(1, NK):
                if k > 1:
                    e.wait_ge(vset, TAPS + k)
                e.matmul(pst[0][:, 0:S1], am[:, k - 1, 1, :], am[:, k - 1, 0, :], start=True, stop=True)
                e.matmul(pst[0][:, S1:2 * S1], am[:, k - 1, 0, :], am[:, k - 1, 1, :], start=True, stop=True).then_inc(pset, 1)
            e.wait_ge(vset, TAPS + NK)
            def sequence(s):
                e.wait_ge(va.sem, va.at("xh", s))
                for t in range(T):
                    m = e.transpose(px[:, t * P:(t + 1) * P], xh[:, t, :], ident[:, :])
                m.then_inc(pe.sem, 1)
                e.wait_ge(aa.sem, aa.at("xn", s))
                e.matmul(po[0:S1, 0:L], bw[:, :], xn[:, TAPS - 1:], start=True, stop=True).then_inc(pe.sem, 1)
                for c in range(CI):
                    for k in range(TAPS):
                        m = e.matmul(pc[:, c, :], wc[:, k, c * P:(c + 1) * P], xn[:, k:k + L], start=k == 0, stop=k == TAPS - 1)
                m.then_inc(pe.sem, 1)
                for c in range(CI):
                    m = e.matmul(pz[:, c, :], winT[:, DI + c * P:DI + (c + 1) * P], xn[:, TAPS - 1:], start=True, stop=True)
                m.then_inc(pe.sem, 1)
                for k in range(NK):
                    e.wait_ge(va.sem, va.at(f"ad{k - 1}" if k else "v0", s))
                    at_rest(e)
                    e.matmul(pst[k % 2][:, 0:L - (1 << k)], am[:, k, 1, :], st[k % 2][:, 0:L - (1 << k)], start=True, stop=True)\
                        .then_inc(pe.sem, 1)
                e.wait_ge(va.sem, va.at(f"ad{NK - 1}", s))
                for c in range(CI):
                    m = e.matmul(pk[:, c, :], cm[:, c * P:(c + 1) * P], st[NK % 2][:, :], start=True, stop=True)
                m.then_inc(pe.sem, 1)
                e.wait_ge(va.sem, va.at("ky", s))
                for t in range(T):
                    for c in range(CI):
                        m = e.matmul(po[:, t * P:(t + 1) * P], yT[:, c, t * P:(t + 1) * P], wot[:, c, :], start=c == 0, stop=c == CI - 1)
                m.then_inc(pe.sem, 1)
            each_sequence(e, sequence)


def transformer_phase(nc, I, X, ident, out):
    ctx, sb, ps = tools(nc)
    ORDER = [1, 3, 5, 7, 0, 2, 4, 6]
    N = HEADS * HD
    with ctx:
        X0 = sb("X0", [P, NSEQ, T, D])
        wqkv = sb("wqkv", [P, 3 * N])
        wo = sb("wo", [P, N // P, D])
        w1 = sb("w1", [P, 2 * HC, P])
        w2 = sb("w2", [P, HC, D])
        vec = sb("vec", [P, 2 + 2 * HC])
        b2 = sb("b2", [1, D])
        ones = sb("ones", [1, P])
        rows = sb("rows", [P, 4, HD])
        tab = sb("tab", [P, T, 4, HD])
        tabl = sb("tabl", [P, T, 4, HD])
        mask = sb("mask", [P, NW * KEYS])
        maskb = sb("maskb", [P, NW * KEYS], BF16)
        identb = sb("identb", [P, P], BF16)
        xin = sb("xin", [P, L])
        xs = sb("xs", [P, WIN + L + 1])
        sq = [sb(f"sq{i}", [P, N]) for i in range(2)]
        n2 = sb("n2", [P, 2, HEADS])
        nh = sb("nh", [P, 2, HEADS])
        nt = sb("nt", [P, 2, HEADS])
        rn = sb("rn", [P, 2, HEADS])
        qk = [sb(f"qk{i}", [P, HEADS, HD]) for i in range(4)]
        m2 = [sb(f"m2_{i}", [P, HEADS, HD]) for i in range(2)]
        rot = [sb(f"rot{i}", [P, N]) for i in range(2)]
        qT = [sb(f"qT{i}", [P, N // P, L]) for i in range(2)]
        kT = [sb(f"kT{i}", [P, N // P, WIN + L]) for i in range(2)]
        V = [sb(f"V{i}", [P, T, 2, N]) for i in range(2)]
        mx = sb("mx", [P, NG, NW])
        sm = sb("sm", [P, NG, NW])
        rc = sb("rc", [P, NG, NW])
        E = [sb(f"E{i}", [P, NW * KEYS]) for i in range(2)]
        PT = [sb(f"PT{i}", [P, NW * KEYS]) for i in range(2)]
        oT = sb("oT", [P, N // P, L])
        yin = sb("yin", [P, L])
        ys = sb("ys", [P, L + 1])
        stats = sb("stats", [P, T, 6])
        mv = sb("mv", [P, T, 2])
        ve = sb("ve", [P, T])
        yr = sb("yr", [P, T])
        yh = sb("yh", [P, T])
        yt = sb("yt", [P, T])
        xh = sb("xh", [P, T, D])
        xnT = sb("xnT", [P, L])
        gl = sb("gl", [P, HC, L])
        hh = sb("hh", [P, HC, L])
        fst = sb("fst", [P, NSEQ * T, 6])
        fmv = sb("fmv", [P, NSEQ * T, 2])
        fv = [sb(f"fv{i}", [P, NSEQ * T]) for i in range(4)]

        pQ = ps("pQ", [P, N])
        pM = [ps("pM0", [P, 512]), ps("pM1", [P, 512])]
        pC = ps("pC", [P, 512])
        pS = ps("pS", [P, NW * KEYS])
        pT = ps("pT", [P, 512])
        pO = ps("pO", [P, 512])
        pOV = [x[:, 0:L].rearrange("p (c t k) -> p c t k", c=2, t=T) for x in (pO, pT)]

        sem = {k: ctx.enter_context(nc.semaphore(k)) for k in
               ("const_loaded", "wqkv_loaded", "wo_loaded", "mlp_loaded", "rows_loaded", "v_setup", "g_setup",
                "tables", "v_shifted", "end_v", "stored")}
        root = Steps(ctx, nc, "end_g", f"rs*{RS}")
        PM = "v0a v0b tr0a tr0b tr1a tr1b v1a v1b tr2a tr2b tr3a tr3b"
        pa = Steps(ctx, nc, "pe_a", "xt qk0 v0a v0b qk1 qk2 qk3 tr0a tr0b tr1a tr1b v1a v1b tr2a tr2b tr3a tr3b")
        sa = Steps(ctx, nc, "act_a", "xs*2 sq0 cp0 v0a v0b sq1 cp1 sq2 cp2 sq3 cp3 tr0a tr0b tr1a tr1b v1a v1b "
                   "tr2a tr2b tr3a tr3b")
        va = Steps(ctx, nc, "dve_a", f"rd0 rd1 mn0 nw0*{VRS} qn0 qn1 cs0 sn0*2 cs1 sn1*2 rd2 rd3 mn1 nw1*{VRS} "
                   "qn2 cs2 sn2*2 qn3 cs3 sn3*2")
        ga = Steps(ctx, nc, "pool_a", "st ad0 ad1 ad2 ad3")
        pb = Steps(ctx, nc, "pe_b", "s0 pt0 s1 pv0 pt1 s2 pv1 pt2 s3 pv2 pt3 pv3 wo")
        sb_ = Steps(ctx, nc, "act_b", "ex0 pt0 ex1 ov0*2 pt1 ex2 ov1*2 pt2 ex3 ov2*2 pt3 ov3*2")
        vb = Steps(ctx, nc, "dve_b", " ".join(f"mx{g} su{g} sm{g} rc{g} no{g}" for g in range(4)) + " xa")
        pc = Steps(ctx, nc, "pe_c", "xt back xn h0 h1 h2 w2")
        sc = Steps(ctx, nc, "act_c", "sh*2 xn ge0 ge1 ge2")
        vc = Steps(ctx, nc, "dve_c", "bn*2 ag*2 ve sh sd xh*2 hid0 hid1 hid2 add")
        gc = Steps(ctx, nc, "pool_c", f"st rs*{RS}")
        block = ctx.enter_context(nc.Block())

        layer0 = {}

        def passes(run, eng):
            layer0["now"] = True
            run((0, 0, 0, 0), None, None)
            run((1, 1, 1, None), (0, 0, 0, 0), None)

            run((2, 2, 0, None), (1, 1, 1, None), (0, 0, 0, 0))
            run((3, 3, 1, None), (2, 2, 0, None), (1, 1, 1, None))
            with eng.Fori(0, (NSEQ - 4) // 2) as i:
                for p in range(2):
                    n = 2 * i + (4 + p)
                    run((n, n, p, None), (n - 1, n - 1, 1 - p, None), (n - 2, n - 2, p, None))
            layer0["now"] = False
            with eng.Fori(1, DEPTH) as l:
                n0 = l * NSEQ
                run((n0, 0, 0, l), (n0 - 1, NSEQ - 1, 1, None), (n0 - 2, NSEQ - 2, 0, None))
                run((n0 + 1, 1, 1, None), (n0, 0, 0, l), (n0 - 1, NSEQ - 1, 1, None))
                run((n0 + 2, 2, 0, None), (n0 + 1, 1, 1, None), (n0, 0, 0, l))
                run((n0 + 3, 3, 1, None), (n0 + 2, 2, 0, None), (n0 + 1, 1, 1, None))
                with eng.Fori(0, (NSEQ - 4) // 2) as i:
                    for p in range(2):
                        s = 2 * i + (4 + p)
                        n = n0 + s
                        run((n, s, p, None), (n - 1, s - 1, 1 - p, None), (n - 2, s - 2, p, None))
            last = DEPTH * NSEQ
            run(None, (last - 1, NSEQ - 1, 1, None), (last - 2, NSEQ - 2, 0, None))
            run(None, None, (last - 1, NSEQ - 1, 1, None))

        @block.sync
        def _(e):
            for dst, src in [(tab[:, :, :, :], I["tab"]), (mask[:, :], I["mask"]), (ones[:, :], I["ones"])]:
                e.dma_start(dst, src).then_inc(sem["const_loaded"], 16)

            def load(l, which):
                if which == "a":
                    e.dma_start(rows[:, :, :], I["rows"][l, :, :, :].to_broadcast([P, 4, HD])).then_inc(sem["rows_loaded"], 16)
                    e.dma_start(wqkv[:, :], I["wqkv"][l, :, :]).then_inc(sem["wqkv_loaded"], 16)
                elif which == "b":
                    e.dma_start(wo[:, :, :], I["wo"][l, :, :, :]).then_inc(sem["wo_loaded"], 16)
                else:
                    e.dma_start(w1[:, :, :], I["w1"][l, :, :, :]).then_inc(sem["mlp_loaded"], 16)
                    e.dma_start(w2[:, :, :], I["w2"][l, :, :, :]).then_inc(sem["mlp_loaded"], 16)
                    e.dma_start(vec[:, :], I["vec"][l, :, :]).then_inc(sem["mlp_loaded"], 16)
                    e.dma_start(b2[:, :], I["b2"][l, :, :]).then_inc(sem["mlp_loaded"], 16)

            def run(A, B, C):
                if A and A[3] is not None:
                    if later(A[0]):
                        e.wait_ge(sem["tables"], A[3] * 4 * T)
                        e.wait_ge(pa.sem, pa.at("v1b", A[0] - 1))
                    load(A[3], "a")
                if B and B[3] is not None:
                    if later(B[0]):
                        e.wait_ge(pb.sem, pb.at("wo", B[0] - 1))
                    load(B[3], "b")
                if C and C[3] is not None:
                    if later(C[0]):
                        e.wait_ge(pc.sem, pc.at("w2", C[0] - 1))
                    load(C[3], "c")
                if A:
                    n, s, par, l = A
                    if not layer0["now"] or not isinstance(n, int) or n >= 2:
                        e.wait_ge(pb.sem, pb.at("pv3", n - 2))
                    v, w = V[par][:, :, 0, :], V[par][:, :, 1, :]
                    e.wait_ge(sa.sem, sa.at("v0b", n))
                    e.dma_start(w[WIN:P, 0, :], v[0:P - WIN, 0, :]).then_inc(sem["v_shifted"], 16)
                    e.dma_start(w[0:WIN, 1, :], v[P - WIN:P, 0, :]).then_inc(sem["v_shifted"], 16)
                    e.wait_ge(sa.sem, sa.at("v1b", n))
                    e.dma_start(w[WIN:P, 1, :], v[0:P - WIN, 1, :]).then_inc(sem["v_shifted"], 16)
            passes(run, e)
            e.wait_ge(sem["end_v"], 4 + 3 * NSEQ * T)
            e.dma_start(out, X[:, :, :, :]).then_inc(sem["stored"], 16)
            e.wait_ge(sem["stored"], 16)

        @block.gpsimd
        def _(e):
            e.memset(xs[:, 0:WIN + 1], 0.0).then_inc(sem["g_setup"], 1)
            e.memset(ys[:, 0:1], 0.0).then_inc(sem["g_setup"], 1)
            for i in range(2):
                e.memset(kT[i][:, :, 0:WIN], 0.0).then_inc(sem["g_setup"], 1)
                e.memset(V[i][0:WIN, 0, 1, :], 0.0).then_inc(sem["g_setup"], 1)

            def run(A, B, C):
                if A:
                    n, s, par, l = A
                    if not layer0["now"]:
                        e.wait_ge(vc.sem, vc.at("add", n - NSEQ))
                    if later(n):
                        e.wait_ge(pa.sem, pa.at("xt", n - 1))
                    at_rest(e)
                    e.tensor_copy(xin[:, :], X[:, s, :, :].rearrange("p t d -> p (t d)")).then_inc(ga.sem, 1)
                if C:
                    n, s, par, l = C
                    e.wait_ge(vb.sem, vb.at("xa", n))
                    if later(n):
                        e.wait_ge(pc.sem, pc.at("xt", n - 1))
                    at_rest(e)
                    e.tensor_copy(yin[:, :], X[:, s, :, :].rearrange("p t d -> p (t d)")).then_inc(gc.sem, 1)
                def add(u):
                    if A:
                        n = A[0]
                        e.wait_ge(va.sem, va.at(f"sn{u}", n))
                        at_rest(e)
                        e.tensor_tensor(rot[u % 2][:, :], rot[u % 2][:, :], m2[u % 2][:, :, :].rearrange("p h d -> p (h d)"),
                                        ALU.add).then_inc(ga.sem, 1)
                if C:
                    e.wait_ge(vc.sem, vc.at("sd", C[0]))
                    at_rest(e)
                    newton_rsqrt(e, gc, C[0], "rs", yr[:, :], ve[:, :], yh[:, :], yt[:, :])
                add(0)
                add(1)
                add(2)
                add(3)
            passes(run, e)
            e.wait_ge(sem["end_v"], 4 + 2 * NSEQ * T)
            at_rest(e)
            newton_rsqrt(e, root, 0, "rs", *(fv[i][:, :] for i in (2, 3, 0, 1)))

        @block.vector
        def _(e):
            e.wait_ge(sem["const_loaded"], 48)
            e.tensor_copy(maskb[:, :], mask[:, :]).then_inc(sem["v_setup"], 1)
            e.tensor_copy(identb[:, :], ident[:, :]).then_inc(sem["v_setup"], 1)
            e.tensor_copy(X0[:, :, :, :], X[:, :, :, :]).then_inc(sem["v_setup"], 1)
            e.wait_ge(sem["v_setup"], 3)

            def wide(a, shape):
                return a.to_broadcast(shape)

            def run(A, B, C):
                if A:
                    n, s, par, l = A
                    if l is not None:
                        e.wait_ge(sem["rows_loaded"], 16 * (l + 1))
                        if later(n):
                            e.wait_ge(va.sem, va.at("sn3", n - 1))
                        for t in range(T):
                            for k in range(4):
                                e.tensor_tensor(tabl[:, t, k, :], tab[:, t, k, :], rows[:, k, :], ALU.mult).then_inc(sem["tables"], 1)
                        e.wait_ge(sem["tables"], (l + 1) * 4 * T)
                sv = pS[:, :].rearrange("p (w k) -> p w k", k=KEYS)

                def ev(g):
                    return E[g % 2][:, :].rearrange("p (w k) -> p w k", k=KEYS)

                def less_max(g):
                    if B:
                        b = B[0]
                        e.wait_ge(pb.sem, pb.at(f"s{g}", b))
                        e.tensor_reduce(mx[:, g, :], sv, AX.X, ALU.max).then_inc(vb.sem, 1)
                        e.wait_ge(vb.sem, vb.at(f"mx{g}", b))
                        e.tensor_tensor(ev(g), sv, wide(mx[:, g, :].unsqueeze(2), [P, NW, KEYS]), ALU.subtract).then_inc(vb.sem, 1)

                def by_sum(g):
                    if B:
                        b = B[0]
                        e.wait_ge(sb_.sem, sb_.at(f"ex{g}", b))
                        e.tensor_reduce(sm[:, g, :], ev(g), AX.X, ALU.add).then_inc(vb.sem, 1)
                        e.wait_ge(vb.sem, vb.at(f"sm{g}", b))
                        e.reciprocal(rc[:, g, :], sm[:, g, :]).then_inc(vb.sem, 1)
                        e.wait_ge(vb.sem, vb.at(f"rc{g}", b))
                        e.tensor_tensor(ev(g), ev(g), wide(rc[:, g, :].unsqueeze(2), [P, NW, KEYS]), ALU.mult).then_inc(vb.sem, 1)

                def norm2(u):
                    if A:
                        n = A[0]
                        e.wait_ge(sa.sem, sa.at(f"sq{u}", n))
                        e.tensor_reduce(n2[:, u % 2, :], sq[u % 2][:, :].rearrange("p (h d) -> p h d", d=HD), AX.X, ALU.add)\
                            .then_inc(va.sem, 1)

                def roots(t):
                    if A:
                        n = A[0]
                        e.wait_ge(va.sem, va.at(f"rd{2 * t + 1}", n))
                        e.tensor_scalar(n2[:, :, :], n2[:, :, :], 1e-24, None, ALU.max).then_inc(va.sem, 1)
                        vector_rsqrt(e, va, n, f"nw{t}", rn[:, :, :], n2[:, :, :], nh[:, :, :], nt[:, :, :])

                def unit(u):
                    if A:
                        n = A[0]
                        e.wait_ge(sa.sem, sa.at(f"cp{u}", n))
                        e.wait_ge(va.sem, va.at(f"nw{u // 2}", n))
                        e.tensor_tensor(qk[u][:, :, :], qk[u][:, :, :],
                                        wide(rn[:, u % 2, :].unsqueeze(2), [P, HEADS, HD]), ALU.mult).then_inc(va.sem, 1)

                def rotate(u):
                    if A:
                        n = A[0]
                        t, w = u // 2, u % 2
                        e.wait_ge(va.sem, va.at(f"qn{u}", n))
                        if u >= 2:
                            e.wait_ge(pa.sem, pa.at(f"tr{u - 2}b", n))
                        elif later(n):
                            e.wait_ge(pa.sem, pa.at(f"tr{u + 2}b", n - 1))
                        e.tensor_tensor(rot[u % 2][:, :].rearrange("p (h d) -> p h d", d=HD), qk[u][:, :, :],
                                        wide(tabl[:, t, 2 * w, :].unsqueeze(1), [P, HEADS, HD]), ALU.mult).then_inc(va.sem, 1)
                        for a, b_ in ((0, HD // 2), (HD // 2, 0)):
                            e.tensor_tensor(m2[u % 2][:, :, a:a + HD // 2], qk[u][:, :, b_:b_ + HD // 2],
                                            wide(tabl[:, t, 2 * w + 1, a:a + HD // 2].unsqueeze(1), [P, HEADS, HD // 2]),
                                            ALU.mult).then_inc(va.sem, 1)

                def hid(j):
                    if C:
                        e.wait_ge(sc.sem, sc.at(f"ge{j}", C[0]))
                        e.scalar_tensor_tensor(hh[:, j, :], pC[:, 0:L], vec[:, 2 + j:3 + j], gl[:, j, :], ALU.add, ALU.mult)\
                            .then_inc(vc.sem, 1)
                def stats_c():
                    if C:
                        c = C[0]
                        e.wait_ge(pc.sem, pc.at("back", c))
                        layernorm_stats(e, vc, c, lambda t: pC[:, L + t * P:L + (t + 1) * P], stats, mv, "")
                        e.wait_ge(vc.sem, vc.at("ag", c))
                        e.tensor_scalar(ve[:, :], mv[:, :, 1], EPS, None, ALU.add).then_inc(vc.sem, 1)
                        e.wait_ge(vc.sem, vc.at("ve", c))
                        rsqrt_seed(e, vc, c, "", ve[:, :].bitcast(I32), yr[:, :].bitcast(I32))

                def normal_c():
                    if C:
                        e.wait_ge(gc.sem, gc.at("rs", C[0]))
                        for t in range(T):
                            e.tensor_scalar(xh[:, t, :], pC[:, L + t * P:L + (t + 1) * P], mv[:, t, 0:1], yr[:, t:t + 1],
                                            ALU.subtract, ALU.mult).then_inc(vc.sem, 1)
                less_max(0)
                by_sum(0)
                norm2(0)
                norm2(1)
                less_max(1)
                roots(0)
                by_sum(1)
                stats_c()
                unit(0)
                unit(1)
                rotate(0)
                less_max(2)
                normal_c()
                rotate(1)
                by_sum(2)
                norm2(2)
                norm2(3)
                less_max(3)
                roots(1)
                unit(2)
                rotate(2)
                by_sum(3)
                hid(0)
                unit(3)
                hid(1)
                rotate(3)
                hid(2)
                if C:
                    e.wait_ge(pc.sem, pc.at("w2", C[0]))
                    xv = X[:, C[1], :, :].rearrange("p t d -> p (t d)")
                    e.tensor_tensor(xv, xv, pC[:, 0:L], ALU.add).then_inc(vc.sem, 1)
                if B:
                    e.wait_ge(pb.sem, pb.at("wo", B[0]))
                    xv = X[:, B[1], :, :].rearrange("p t d -> p (t d)")
                    e.tensor_tensor(xv, xv, pT[:, 0:L], ALU.add).then_inc(vb.sem, 1)
            passes(run, e)
            ev = sem["end_v"]
            NT = NSEQ * T
            e.wait_ge(vc.sem, vc.at("add", DEPTH * NSEQ - 1))
            e.tensor_tensor(X0[:, :, :, :], X0[:, :, :, :], X[:, :, :, :], ALU.add).then_inc(ev, 1)
            e.wait_ge(ev, 1)
            xf = X0[:, :, :, :].rearrange("p s t d -> p (s t) d")
            for t in range(NT):
                e.bn_stats(fst[:, t, :], xf[:, t, :]).then_inc(ev, 1)
            e.wait_ge(ev, 1 + NT)
            for t in range(NT):
                e.bn_aggr(fmv[:, t, :], fst[:, t, :]).then_inc(ev, 1)
            e.wait_ge(ev, 1 + 2 * NT)
            e.tensor_scalar(fv[3][:, :], fmv[:, :, 1], EPS, None, ALU.add).then_inc(ev, 1)
            e.wait_ge(ev, 2 + 2 * NT)
            e.tensor_scalar(fv[2][:, :].bitcast(I32), fv[3][:, :].bitcast(I32), 1, None, ALU.logical_shift_right).then_inc(ev, 1)
            e.wait_ge(ev, 3 + 2 * NT)
            e.tensor_scalar(fv[2][:, :].bitcast(I32), fv[2][:, :].bitcast(I32), -1.0, MAGIC, ALU.mult, ALU.add).then_inc(ev, 1)
            e.wait_ge(root.sem, RS)
            xo = X[:, :, :, :].rearrange("p s t d -> p (s t) d")
            for t in range(NT):
                e.tensor_scalar(xo[:, t, :], xf[:, t, :], fmv[:, t, 0:1], fv[2][:, t:t + 1], ALU.subtract, ALU.mult).then_inc(ev, 1)

        @block.scalar
        def _(e):
            e.wait_ge(sem["g_setup"], 6)

            def run(A, B, C):
                def copy_m(kind, u):
                    if A:
                        n, s, par, l = A
                        for i, half in enumerate("ab"):
                            if kind == "v" and i == 0 and u == 0 and (not layer0["now"] or not isinstance(n, int) or n >= 2):
                                e.wait_ge(sem["v_shifted"], 48 * (n - 1))
                                e.wait_ge(pb.sem, pb.at("pv3", n - 2))
                            e.wait_ge(pa.sem, pa.at(f"{kind}{u}{half}", n))
                            if kind == "v":
                                dst, src = V[par][:, u, 0, i * 512:(i + 1) * 512], pM[i][:, :]
                            else:
                                t, w = u // 2, u % 2
                                buf, off = (kT[par], WIN) if w else (qT[par], 0)
                                dst = buf[:, 4 * i:4 * i + 4, off + t * P:off + (t + 1) * P]
                                src = pM[i][:, :].rearrange("p (c t) -> p c t", c=4)
                            e.activation(dst, src, ACT.Copy).then_inc(sa.sem, 1)

                def squares(u):
                    if A:
                        n = A[0]
                        e.wait_ge(pa.sem, pa.at(f"qk{u}", n))
                        if u >= 2:
                            e.wait_ge(va.sem, va.at(f"rd{u - 2}", n))
                        elif later(n):
                            e.wait_ge(va.sem, va.at(f"rd{u + 2}", n - 1))
                        e.activation(sq[u % 2][:, :], pQ[:, :], ACT.Square).then_inc(sa.sem, 1)
                        if later(n):
                            e.wait_ge(va.sem, va.at(f"sn{u}", n - 1))
                        e.activation(qk[u][:, :, :].rearrange("p h d -> p (h d)"), pQ[:, :], ACT.Copy).then_inc(sa.sem, 1)

                def exps(g):
                    if B:
                        e.wait_ge(vb.sem, vb.at(f"su{g}", B[0]))
                        e.activation(E[g % 2][:, :], E[g % 2][:, :], ACT.Exp, scale=8.0).then_inc(sb_.sem, 1)

                def copy_b(g):
                    if B:
                        e.wait_ge(pb.sem, pb.at(f"pt{g}", B[0]))
                        e.activation(PT[g % 2][:, :], pT[:, :], ACT.Copy).then_inc(sb_.sem, 1)

                def copy_o(g):
                    if B:
                        e.wait_ge(pb.sem, pb.at(f"pv{g}", B[0]))
                        for i in range(2):
                            e.activation(oT[:, 2 * g:2 * g + 2, :].rearrange("p c (t k) -> p c t k", t=T)[:, :, :, KEYS * i:KEYS * (i + 1)],
                                         pOV[i], ACT.Copy).then_inc(sb_.sem, 1)

                def gelu(j):
                    if C:
                        e.wait_ge(pc.sem, pc.at(f"h{j}", C[0]))
                        e.activation(gl[:, j, :], pC[:, L:2 * L], ACT.Gelu, bias=vec[:, 2 + HC + j:3 + HC + j]).then_inc(sc.sem, 1)
                if A:
                    e.wait_ge(pa.sem, pa.at("xt", A[0]))
                    e.activation(xs[0:HALF, WIN:WIN + L], pM[0][0:HALF, 0:L], ACT.Copy).then_inc(sa.sem, 1)
                    e.activation(xs[HALF:P, WIN + 1:WIN + L + 1], pM[0][HALF:P, 0:L], ACT.Copy).then_inc(sa.sem, 1)
                exps(0)
                squares(0)
                copy_m("v", 0)
                if C:
                    e.wait_ge(pc.sem, pc.at("xt", C[0]))
                    e.activation(ys[0:HALF, 0:L], pC[0:HALF, 0:L], ACT.Copy).then_inc(sc.sem, 1)
                    e.activation(ys[HALF:P, 1:L + 1], pC[HALF:P, 0:L], ACT.Copy).then_inc(sc.sem, 1)
                squares(1)
                copy_b(0)
                exps(1)
                squares(2)
                copy_o(0)
                copy_b(1)
                exps(2)
                squares(3)
                copy_o(1)
                copy_m("tr", 0)
                if C:
                    if C[3] is not None:
                        e.wait_ge(sem["mlp_loaded"], 64 * (C[3] + 1))
                    e.wait_ge(pc.sem, pc.at("xn", C[0]))
                    e.activation(xnT[:, :], pC[:, 0:L], ACT.Identity, bias=vec[:, 1:2], scale=vec[:, 0:1]).then_inc(sc.sem, 1)
                copy_b(2)
                exps(3)
                copy_m("tr", 1)
                gelu(0)
                copy_m("v", 1)
                copy_o(2)
                gelu(1)
                copy_m("tr", 2)
                copy_b(3)
                gelu(2)
                copy_o(3)
                copy_m("tr", 3)
            passes(run, e)

        @block.tensor
        def _(e):
            e.wait_ge(sem["v_setup"], 3)
            e.wait_ge(sem["g_setup"], 6)
            before = {}
            prev = ["tr3a", "tr3b"]
            for name in ["xt"] + PM.split():
                i = 0 if name == "xt" or name[-1] == "a" else 1
                before[name] = prev[i]
                prev[i] = "xs" if name == "xt" else name

            def run(A, B, C):
                def bank_free(n, name):
                    back = before[name]
                    first = name == "xt" or name == "v0b"
                    if not first:
                        e.wait_ge(sa.sem, sa.at(back, n))
                    elif later(n):
                        e.wait_ge(sa.sem, sa.at(back, n - 1))

                def a_xt():
                    if not A:
                        return
                    n, s, par, l = A
                    e.wait_ge(ga.sem, ga.at("st", n))
                    bank_free(n, "xt")
                    for t in range(T):
                        m = e.transpose(pM[0][:, t * P:(t + 1) * P], xin[:, t * P:(t + 1) * P], ident[:, :])
                    m.then_inc(pa.sem, 1)

                def a_qk(u):
                    if not A:
                        return
                    n, s, par, l = A
                    t, w = u // 2, u % 2
                    if u == 0:
                        if l is not None:
                            e.wait_ge(sem["wqkv_loaded"], 16 * (l + 1))
                        e.wait_ge(sa.sem, sa.at("xs", n))
                    if u:
                        e.wait_ge(sa.sem, sa.at(f"cp{u - 1}", n))
                    for i in range(2):
                        m = e.matmul(pQ[:, i * 512:(i + 1) * 512], xs[:, WIN + t * P:WIN + (t + 1) * P],
                                     wqkv[:, w * N + i * 512:w * N + (i + 1) * 512], start=True, stop=True)
                    m.then_inc(pa.sem, 1)

                def a_v(u):
                    if not A:
                        return
                    n, s, par, l = A
                    o = WIN + u * P
                    for i, half in enumerate("ab"):
                        bank_free(n, f"v{u}{half}")
                        e.matmul(pM[i][:, :], xs[:, o:o + P], wqkv[:, 2 * N + i * 512:2 * N + (i + 1) * 512],
                                 start=True, stop=True).then_inc(pa.sem, 1)

                def a_tr(u):
                    if not A:
                        return
                    n, s, par, l = A
                    e.wait_ge(ga.sem, ga.at(f"ad{u}", n))
                    for i, half in enumerate("ab"):
                        bank_free(n, f"tr{u}{half}")
                        for c in range(4):
                            m = e.transpose(pM[i][:, c * P:(c + 1) * P], rot[u % 2][:, (4 * i + c) * P:(4 * i + c + 1) * P], ident[:, :])
                        m.then_inc(pa.sem, 1)

                def b_s(g):
                    if not B:
                        return
                    b, s, par, l = B
                    if g == 0:
                        e.wait_ge(sa.sem, sa.at("tr3b", b))
                        e.wait_ge(sem["v_shifted"], 48 * (b + 1))
                    if g or later(b):
                        e.wait_ge(vb.sem, vb.at(f"su{g - 1}", b) if g else vb.at("su3", b - 1))
                    e.matmul(pS[:, :], identb[:, :], maskb[:, :], start=True, stop=False, skip_group_check=True)
                    for i, w in enumerate(ORDER):
                        for j in range(4):
                            h = 4 * g + j
                            r = HD * (h % 2)
                            m = e.matmul(pS[32 * j:32 * j + 32, i * KEYS:(i + 1) * KEYS], qT[par][r:r + HD, h // 2, WIN * w:WIN * (w + 1)],
                                         kT[par][r:r + HD, h // 2, WIN * w:WIN * (w + 2)], start=False, stop=(i == NW - 1),
                                         skip_group_check=True, tile_position=(r, 32 * j))
                    m.then_inc(pb.sem, 1)

                def b_pt(g):
                    if not B:
                        return
                    b = B[0]
                    e.wait_ge(vb.sem, vb.at(f"no{g}", b))
                    if g:
                        e.wait_ge(sb_.sem, sb_.at(f"ov{g - 1}", b))
                    elif later(b):
                        e.wait_ge(vb.sem, vb.at("xa", b - 1))
                    for i in range(4):
                        m = e.transpose(pT[:, i * P:(i + 1) * P], E[g % 2][:, i * P:(i + 1) * P], ident[:, :])
                    m.then_inc(pb.sem, 1)

                def b_pv(g):
                    if not B:
                        return
                    b, s, par, l = B
                    e.wait_ge(sb_.sem, sb_.at(f"pt{g}", b))
                    at_rest(e)
                    for i, w in enumerate(ORDER):
                        r = KEYS * (i % 2)
                        for j in range(4):
                            h = 4 * g + j
                            c = HD * (j % 2)
                            m = e.matmul(pOV[i % 2][c:c + HD, j // 2, w // 4, WIN * (w % 2):WIN * (w % 2 + 1)], V[par][r:r + KEYS, w // 4, 1 - w % 2, h * HD:(h + 1) * HD],
                                         PT[g % 2][r:r + KEYS, (i // 2) * P + 32 * j:(i // 2) * P + 32 * j + 32],
                                         start=True, stop=True, tile_position=(r, c))
                    m.then_inc(pb.sem, 1)

                def b_wo():
                    if not B:
                        return
                    b, s, par, l = B
                    if l is not None:
                        e.wait_ge(sem["wo_loaded"], 16 * (l + 1))
                    e.wait_ge(sb_.sem, sb_.at("ov3", b))
                    for t in range(T):
                        for c in range(N // P):
                            m = e.matmul(pT[:, t * P:(t + 1) * P], oT[:, c, t * P:(t + 1) * P], wo[:, c, :], start=c == 0, stop=c == N // P - 1)
                    m.then_inc(pb.sem, 1)

                def c_xt():
                    if not C:
                        return
                    c, s, par, l = C
                    e.wait_ge(gc.sem, gc.at("st", c))
                    if later(c):
                        e.wait_ge(vc.sem, vc.at("add", c - 1))
                    for t in range(T):
                        m = e.transpose(pC[:, t * P:(t + 1) * P], yin[:, t * P:(t + 1) * P], ident[:, :])
                    m.then_inc(pc.sem, 1)

                def c_back():
                    if not C:
                        return
                    c = C[0]
                    e.wait_ge(sc.sem, sc.at("sh", c))
                    for t in range(T):
                        m = e.transpose(pC[:, L + t * P:L + (t + 1) * P], ys[:, t * P:(t + 1) * P], ident[:, :])
                    m.then_inc(pc.sem, 1)

                def c_xn():
                    if not C:
                        return
                    c = C[0]
                    e.wait_ge(vc.sem, vc.at("xh", c))
                    for t in range(T):
                        m = e.transpose(pC[:, t * P:(t + 1) * P], xh[:, t, :], ident[:, :])
                    m.then_inc(pc.sem, 1)

                def c_h(j):
                    if not C:
                        return
                    c, s, par, l = C
                    if j == 0:
                        if l is not None:
                            e.wait_ge(sem["mlp_loaded"], 64 * (l + 1))
                        e.wait_ge(sc.sem, sc.at("xn", c))
                    else:
                        e.wait_ge(vc.sem, vc.at(f"hid{j - 1}", c))
                    e.matmul(pC[:, 0:L], w1[:, j, :], xnT[:, :], start=True, stop=True)
                    e.matmul(pC[:, L:2 * L], w1[:, HC + j, :], xnT[:, :], start=True, stop=True).then_inc(pc.sem, 1)

                def c_w2():
                    if not C:
                        return
                    c = C[0]
                    e.wait_ge(vc.sem, vc.at("hid2", c))
                    for t in range(T):
                        for j in range(HC):
                            e.matmul(pC[:, t * P:(t + 1) * P], hh[:, j, t * P:(t + 1) * P], w2[:, j, :], start=j == 0, stop=False)
                        m = e.matmul(pC[:, t * P:(t + 1) * P], ones[:, :], b2[:, :], start=False, stop=True)
                    m.then_inc(pc.sem, 1)

                a_xt()
                b_s(0)
                a_qk(0)
                c_xt()
                a_v(0)
                a_qk(1)
                c_back()
                b_pt(0)
                b_s(1)
                a_qk(2)
                b_pv(0)
                b_pt(1)
                b_s(2)
                a_qk(3)
                b_pv(1)
                a_tr(0)
                c_xn()
                b_pt(2)
                b_s(3)
                a_tr(1)
                c_h(0)
                a_v(1)
                b_pv(2)
                c_h(1)
                a_tr(2)
                b_pt(3)
                c_h(2)
                b_pv(3)
                c_w2()
                a_tr(3)
                b_wo()
            passes(run, e)


def layout(i):
    f = np.float32

    def rows(a, inner=P):
        return a.reshape(a.shape[0] // inner, inner, *a.shape[1:]).swapaxes(0, 1)
    a = {}
    g = lambda k: np.asarray(i[k])
    a["x"] = g("L0_attn_x").reshape(NSEQ, T, P, D).transpose(2, 0, 1, 3)
    a["a_win"] = rows(g("L0_attn_W_in"))
    a["a_wxd"] = rows(np.concatenate([g("L0_attn_W_dt").T, g("L0_attn_W_x").T], 1))
    a["a_cw"] = rows(g("L0_attn_conv_w")[:, 0, :])
    a["a_bias_in"] = rows(np.stack([g("L0_attn_b_in"), g("L0_attn_conv_b")], 1))
    a["a_svec"] = np.stack([g("L0_attn_b_dt"), g("L0_attn_b_x"), g("L0_attn_A_log")], 1)
    a["a_dmt"] = rows(g("L0_attn_D_mat").T)
    a["a_wot"] = rows(g("L0_attn_W_out").T)
    a["a_bout"] = g("L0_attn_b_out")[None]
    a["b_wg"] = g("L0_ffn_w_gate").transpose(2, 0, 1)
    a["b_wu"] = g("L0_ffn_w_up").transpose(2, 0, 1)
    a["b_wd"] = rows(g("L0_ffn_w_down").transpose(2, 0, 1).reshape(FI, NE * D))
    a["b_rgu"] = np.concatenate([g("L0_ffn_router_gate").T, g("L0_ffn_router_up").T], 1)
    a["b_rd"] = rows(g("L0_ffn_router_down").T)
    a["c_winT"] = g("L1_attn_W_in").T
    a["c_winu"] = rows(g("L1_attn_W_in")[0:DI])
    a["c_cw"] = g("L1_attn_conv_w")[:, 0, :].T[None]
    a["c_cvb"] = g("L1_attn_conv_b").reshape(CI, P).T
    a["c_gb"] = np.stack([g("L1_attn_ln_gamma"), g("L1_attn_ln_beta")], 1)
    a["c_wot"] = rows(g("L1_attn_W_out").T)
    a["c_am"] = np.stack([g("L1_attn_A"), g("L1_attn_A").T], 1)
    a["c_bmT"] = rows(g("L1_attn_Bm").T)
    a["c_cm"] = g("L1_attn_Cm")
    a["wqkv"] = g("L1_ffn_Wqkv")
    a["wo"] = g("L1_ffn_Wo").reshape(DEPTH, HEADS * HD // P, P, D).transpose(0, 2, 1, 3)
    m = g("L1_ffn_W2").shape[1]
    w1 = np.zeros((DEPTH, D, 2, HC * P), f)
    w1[:, :, :, :m] = g("L1_ffn_W1").reshape(DEPTH, D, 2, m)
    a["w1"] = w1.reshape(DEPTH, D, 2 * HC, P)
    w2 = np.zeros((DEPTH, HC * P, D), f)
    w2[:, :m] = g("L1_ffn_W2")
    a["w2"] = w2.reshape(DEPTH, HC, P, D).transpose(0, 2, 1, 3)
    b1 = np.zeros((DEPTH, 2, HC * P), f)
    b1[:, :, :m] = g("L1_ffn_b1").reshape(DEPTH, 2, m)
    a["vec"] = np.concatenate([np.stack([g("L1_ffn_ln_g"), g("L1_ffn_ln_b")], 2),
                               b1.reshape(DEPTH, 2 * HC, P).transpose(0, 2, 1)], 2)
    a["b2"] = g("L1_ffn_b2")[:, None]
    q, k = g("L1_ffn_q_scale"), g("L1_ffn_k_scale")
    swap = lambda v: np.concatenate([v[:, HD // 2:], v[:, :HD // 2]], 1)
    a["rows"] = np.stack([q, swap(q), k, swap(k)], 1)[:, None]
    a["ident"] = np.eye(P, dtype=f)
    a["ones"] = np.ones((1, P), f)
    a["iota"] = np.tile(np.arange(NE, dtype=f), (P, 1))
    a["ind"] = np.stack([(np.arange(L) >= TAPS - 1 - t) for t in range(TAPS)] + [np.ones(L, bool)]).astype(f)
    half = np.arange(0, HD, 2, dtype=f)
    inv = (f(1) / f(10000) ** (half / f(HD))).astype(f)
    t = np.arange(L, dtype=f)
    fr = np.concatenate([t[:, None] * inv[None]] * 2, 1)
    base = (half + f(0.4 * HD)) / f(1.4 * HD)
    sc = base[None].astype(np.float64) ** ((t[:, None] - L // 2) / (WIN // 2))
    sc = np.concatenate([sc, sc], 1)
    sign = np.where(np.arange(HD) < HD // 2, -1.0, 1.0)
    co, si = np.cos(fr.astype(np.float64)), np.sin(fr.astype(np.float64)) * sign
    tab = np.stack([co * sc, si * sc, co / sc, si / sc], 1).astype(f)
    a["tab"] = tab.reshape(T, P, 4, HD).swapaxes(0, 1)
    qi, kj = np.arange(WIN)[:, None], np.arange(WIN)[None]
    pair = np.concatenate([np.where(qi > kj, -1e30, 0), np.where(qi < kj, -1e30, 0)], 1)
    mask = np.stack([pair] * NW, 1)
    mask[:, 4, 0:WIN] = -1e30
    a["mask"] = np.tile(mask.reshape(WIN, NW * KEYS), (4, 1)).astype(f)
    return {k: np.ascontiguousarray(v) for k, v in a.items()}


def kernel(**inputs):
    import concourse.bacc as _bacc
    from concourse.bass_utils import run_bass_kernel_spmd as _run

    nc = _bacc.Bacc("TRN2", target_bir_lowering=False, num_devices=1)
    arrays = layout(inputs)
    I = {k: nc.dram_tensor("in_" + k, v.shape, mybir.dt.from_np(v.dtype), kind="ExternalInput").ap() for k, v in arrays.items()}
    out = nc.dram_tensor("out", (P, NSEQ, T, D), F32, kind="ExternalOutput").ap()
    program(nc, I, out)
    r = _run(nc, [{"in_" + k: v for k, v in arrays.items()}], core_ids=[0])
    return r.results[0]["out"].transpose(1, 2, 0, 3).reshape(NSEQ, L, D)
```

```python
from contextlib import ExitStack

import numpy as np
import concourse.bass as bass
from concourse import mybir

F32 = mybir.dt.float32
BF16 = mybir.dt.bfloat16
I32 = mybir.dt.int32
U32 = mybir.dt.uint32
ALU = mybir.AluOpType
ACT = mybir.ActivationFunctionType
AX = mybir.AxisListType

NSEQ, L, D, P = 16, 256, 128, 128
T = L // P
DI = 256
CI = DI // P
TAPS = 4
S0, S1 = 64, 16
NE, FI = 8, 512
CF = FI // P
DEPTH, HEADS, HD, WIN = 6, 16, 64, 32
NW = L // WIN
NG = 4
KEYS = 2 * WIN
HALF = D // 2
HC = 3
EPS = 1e-5
ROUNDS = 3
RS = 1 + 4 * ROUNDS
VRS = 3 + 3 * ROUNDS
MAGIC = float(0x5F3759DF)


class Steps:

    def __init__(self, ctx, nc, name, steps):
        self.sem = ctx.enter_context(nc.semaphore(name))
        self.index, k = {}, 0
        for s in steps.split():
            s, _, m = s.partition("*")
            k += int(m or 1)
            self.index[s] = k
        self.per = k

    def passed(self, n):
        return n * self.per

    def at(self, step, n, back=0):
        return n * self.per + (self.index[step] - back)


def later(n):
    return not isinstance(n, int) or n > 0


def each_sequence(eng, body):
    body(0)
    with eng.Fori(1, NSEQ) as s:
        body(s)


def at_rest(eng):
    eng.nop(nofuse=True)


def newton_rsqrt(eng, st, n, step, y, var, h, t):
    def own(k):
        count = st.at(step, n, RS - k)
        if not isinstance(count, int) or count > 0:
            eng.wait_ge(st.sem, count)
            at_rest(eng)
    own(0)
    eng.tensor_scalar(h, var, -0.5, 0.0, ALU.mult, ALU.add).then_inc(st.sem, 1)
    for r in range(ROUNDS):
        if r:
            own(1 + 4 * r)
        eng.tensor_tensor(t, y, y, ALU.mult).then_inc(st.sem, 1)
        own(2 + 4 * r)
        eng.tensor_tensor(t, t, h, ALU.mult).then_inc(st.sem, 1)
        own(3 + 4 * r)
        eng.tensor_scalar(t, t, 1.0, 1.5, ALU.mult, ALU.add).then_inc(st.sem, 1)
        own(4 + 4 * r)
        eng.tensor_tensor(y, y, t, ALU.mult).then_inc(st.sem, 1)


def vector_rsqrt(v, st, n, step, y, var, h, t):
    def own(k):
        v.wait_ge(st.sem, st.at(step, n, VRS - k))
    own(0)
    v.tensor_scalar(y.bitcast(I32), var.bitcast(I32), 1, None, ALU.logical_shift_right).then_inc(st.sem, 1)
    v.tensor_scalar(h, var, -0.5, None, ALU.mult).then_inc(st.sem, 1)
    own(1)
    v.tensor_scalar(y.bitcast(I32), y.bitcast(I32), -1.0, MAGIC, ALU.mult, ALU.add).then_inc(st.sem, 1)
    for r in range(ROUNDS):
        own(3 + 3 * r)
        v.tensor_tensor(t, y, y, ALU.mult).then_inc(st.sem, 1)
        own(4 + 3 * r)
        v.tensor_tensor(t, t, h, ALU.mult).then_inc(st.sem, 1)
        own(5 + 3 * r)
        v.scalar_tensor_tensor(y, t, 1.5, y, ALU.add, ALU.mult).then_inc(st.sem, 1)


def layernorm_stats(v, st, n, src, stats, mv, step_in):
    for t in range(T):
        v.bn_stats(stats[:, t, :], src(t)).then_inc(st.sem, 1)
    v.wait_ge(st.sem, st.at(step_in + "bn", n))
    at_rest(v)
    for t in range(T):
        v.bn_aggr(mv[:, t, :], stats[:, t, :]).then_inc(st.sem, 1)


def rsqrt_seed(v, st, n, pre, var, bits):
    v.tensor_scalar(bits, var, 1, None, ALU.logical_shift_right).then_inc(st.sem, 1)
    v.wait_ge(st.sem, st.at(pre + "sh", n))
    v.tensor_scalar(bits, bits, -1.0, MAGIC, ALU.mult, ALU.add).then_inc(st.sem, 1)


def program(nc, I, out):
    top = ExitStack()
    with top:
        X = top.enter_context(nc.sbuf_tensor("X", [P, NSEQ, T, D], F32))
        ident = top.enter_context(nc.sbuf_tensor("ident", [P, P], F32))
        ssm_phase(nc, I, X, ident)
        moe_phase(nc, I, X, ident)
        ssm2_phase(nc, I, X, ident)
        transformer_phase(nc, I, X, ident, out)


def tools(nc):
    ctx = ExitStack()

    def sb(name, shape, dt=F32):
        return ctx.enter_context(nc.sbuf_tensor(name, shape, dt))

    def ps(name, shape, dt=F32):
        return ctx.enter_context(nc.psum_tensor(name, shape, dt))
    return ctx, sb, ps


def ssm_phase(nc, I, X, ident):
    ctx, sb, ps = tools(nc)
    with ctx:
        win = sb("a_win", [P, CI, D])
        wxd = sb("a_wxd", [P, CI, 2 * S0])
        cw = sb("a_cw", [P, CI, TAPS])
        bias_in = sb("a_bias_in", [P, CI, 2])
        svec = sb("a_svec", [S0, 3])
        dmt = sb("a_dmt", [P, CI, S0])
        wot = sb("a_wot", [P, CI, D])
        bout = sb("a_bout", [1, D])
        ind = sb("a_ind", [TAPS + 1, L])
        ones = sb("a_ones", [1, P])
        scaled = sb("a_scaled", [P, CI, TAPS, 2 * S0])
        bsc = sb("a_bsc", [P, CI, TAPS + 1])
        fused = sb("a_fused", [P, TAPS, 2 * S0])
        beta = sb("a_beta", [TAPS + 1, 2 * S0])
        wzo = sb("a_wzo", [S0, D])
        aneg = sb("a_aneg", [S0, 2])
        ealog = sb("a_ealog", [S0, 1])
        xst = sb("a_xst", [P, 2, L])
        xpad = sb("a_xpad", [P, 2, TAPS - 1 + L])
        pre = sb("a_pre", [S0, 4, L])
        dt_ = sb("a_dt", [S0, L])
        dA = sb("a_dA", [S0, L])
        wx = sb("a_wx", [S0, L])
        om = sb("a_om", [S0, L])
        dbx = sb("a_dbx", [S0, L])
        z = sb("a_z", [S0, 2, L])
        res = sb("a_res", [P, T, D])
        stats = sb("a_stats", [P, T, 6])
        mv = sb("a_mv", [P, T, 2])
        ve = sb("a_ve", [P, T])
        y = sb("a_y", [P, T])
        h = sb("a_h", [P, T])
        tt = sb("a_t", [P, T])
        pf = ps("a_pf", [P, 512])
        pb = ps("a_pb", [TAPS + 1, 512])
        px = ps("a_px", [P, 512])
        pu = ps("a_pu", [S0, 512])
        pz = ps("a_pz", [P, 512])
        loaded = ctx.enter_context(nc.semaphore("a_loaded"))
        xl = ctx.enter_context(nc.semaphore("a_xl"))
        pset = ctx.enter_context(nc.semaphore("a_pset"))
        vset = ctx.enter_context(nc.semaphore("a_vset"))
        aset = ctx.enter_context(nc.semaphore("a_aset"))
        gset = ctx.enter_context(nc.semaphore("a_gset"))
        pe = Steps(ctx, nc, "a_pe", "xt u y")
        va = Steps(ctx, nc, "a_va", "pre rel wx om dbx scan res bn*2 ag*2 ve sh sd out*2")
        aa = Steps(ctx, nc, "a_aa", "xpad abs exp ln dA")
        ga = Steps(ctx, nc, "a_ga", f"stage rs*{RS}")
        LOADS = 11
        block = ctx.enter_context(nc.Block())

        @block.sync
        def _(e):
            for dst, src in [(ident[:, :], I["ident"]), (win[:, :, :], I["a_win"]), (wxd[:, :, :], I["a_wxd"]),
                             (cw[:, :, :], I["a_cw"]), (bias_in[:, :, :], I["a_bias_in"]), (svec[:, :], I["a_svec"]),
                             (dmt[:, :, :], I["a_dmt"]), (wot[:, :, :], I["a_wot"]), (bout[:, :], I["a_bout"]),
                             (ind[:, :], I["ind"]), (ones[:, :], I["ones"])]:
                e.dma_start(dst, src).then_inc(loaded, 16)
            e.dma_start(X[:, :, :, :], I["x"]).then_inc(xl, 16)

        @block.gpsimd
        def _(e):
            e.memset(xpad[:, :, 0:TAPS - 1], 0.0).then_inc(gset, 1)
            e.wait_ge(xl, 16)
            def sequence(s):
                if later(s):
                    e.wait_ge(pe.sem, pe.passed(s))
                at_rest(e)
                e.tensor_copy(xst[:, 0, :], X[:, s, :, :].rearrange("p t d -> p (t d)")).then_inc(ga.sem, 1)
                e.wait_ge(va.sem, va.at("sd", s))
                at_rest(e)
                newton_rsqrt(e, ga, s, "rs", y[:, :], ve[:, :], h[:, :], tt[:, :])
            each_sequence(e, sequence)

        @block.vector
        def _(e):
            e.wait_ge(loaded, 16 * LOADS)
            for c in range(CI):
                for k in range(TAPS):
                    e.tensor_scalar(scaled[:, c, k, :], wxd[:, c, :], cw[:, c, k:k + 1], None, ALU.mult).then_inc(vset, 1)
                e.tensor_scalar(bsc[:, c, 0:TAPS], cw[:, c, :], bias_in[:, c, 0:1], None, ALU.mult).then_inc(vset, 1)
                e.tensor_copy(bsc[:, c, TAPS:TAPS + 1], bias_in[:, c, 1:2]).then_inc(vset, 1)
            e.wait_ge(pset, 1)
            e.tensor_copy(fused[:, :, :], pf[:, :].rearrange("p (k m) -> p k m", k=TAPS)).then_inc(vset, 1)
            e.tensor_copy(beta[:, :], pb[:, 0:2 * S0]).then_inc(vset, 1)
            e.wait_ge(pset, 2)
            e.tensor_copy(wzo[:, :], pf[0:S0, 0:D]).then_inc(vset, 1)
            e.wait_ge(aset, 1)
            e.tensor_scalar(aneg[:, 0:1], ealog[:, :], -1.0, None, ALU.mult).then_inc(vset, 1)
            e.wait_ge(vset, CI * (TAPS + 2) + 4)
            e.reciprocal(aneg[:, 1:2], aneg[:, 0:1]).then_inc(vset, 1)
            e.wait_ge(vset, CI * (TAPS + 2) + 5)
            def sequence(s):
                e.wait_ge(pe.sem, pe.at("u", s))
                if later(s):
                    e.wait_ge(aa.sem, aa.passed(s))
                e.tensor_scalar(pre[:, 0, :], pu[:, 0:L], svec[:, 0:1], None, ALU.add).then_inc(va.sem, 1)
                e.wait_ge(aa.sem, aa.at("ln", s))
                e.scalar_tensor_tensor(dt_[:, :], pre[:, 0, :], 0.0, pre[:, 3, :], ALU.max, ALU.add).then_inc(va.sem, 1)
                e.tensor_scalar(wx[:, :], pu[:, L:2 * L], svec[:, 1:2], aneg[:, 1:2], ALU.add, ALU.mult).then_inc(va.sem, 1)
                e.wait_ge(aa.sem, aa.at("dA", s))
                e.tensor_scalar(om[:, :], dA[:, :], -1.0, 1.0, ALU.mult, ALU.add).then_inc(va.sem, 1)
                e.wait_ge(va.sem, va.at("om", s))
                e.tensor_tensor(dbx[:, :], om[:, :], wx[:, :], ALU.mult).then_inc(va.sem, 1)
                e.wait_ge(va.sem, va.at("dbx", s))
                e.tensor_tensor_scan(z[:, 0, :], dA[:, :], dbx[:, :], 0.0, ALU.mult, ALU.add).then_inc(va.sem, 1)
                e.wait_ge(pe.sem, pe.at("y", s))
                e.tensor_tensor(res[:, :, :], X[:, s, :, :], pz[:, 0:L].rearrange("p (t d) -> p t d", t=T), ALU.add)\
                    .then_inc(va.sem, 1)
                e.wait_ge(va.sem, va.at("res", s))
                layernorm_stats(e, va, s, lambda t: res[:, t, :], stats, mv, "")
                e.wait_ge(va.sem, va.at("ag", s))
                e.tensor_scalar(ve[:, :], mv[:, :, 1], EPS, None, ALU.add).then_inc(va.sem, 1)
                e.wait_ge(va.sem, va.at("ve", s))
                rsqrt_seed(e, va, s, "", ve[:, :].bitcast(I32), y[:, :].bitcast(I32))
                e.wait_ge(ga.sem, ga.at("rs", s))
                for t in range(T):
                    e.tensor_scalar(X[:, s, t, :], res[:, t, :], mv[:, t, 0:1], y[:, t:t + 1], ALU.subtract, ALU.mult)\
                        .then_inc(va.sem, 1)
            each_sequence(e, sequence)

        @block.scalar
        def _(e):
            e.wait_ge(loaded, 16 * LOADS)
            e.activation(ealog[:, :], svec[:, 2:3], ACT.Exp).then_inc(aset, 1)
            e.wait_ge(gset, 1)
            e.wait_ge(vset, CI * (TAPS + 2) + 5)
            def sequence(s):
                e.wait_ge(pe.sem, pe.at("xt", s))
                e.activation(xpad[:, 0, TAPS - 1:], px[:, 0:L], ACT.Copy).then_inc(aa.sem, 1)
                e.wait_ge(va.sem, va.at("pre", s))
                e.activation(pre[:, 1, :], pre[:, 0, :], ACT.Abs).then_inc(aa.sem, 1)
                e.wait_ge(aa.sem, aa.at("abs", s))
                e.activation(pre[:, 2, :], pre[:, 1, :], ACT.Exp, scale=-1.0).then_inc(aa.sem, 1)
                e.wait_ge(aa.sem, aa.at("exp", s))
                e.activation(pre[:, 3, :], pre[:, 2, :], ACT.Ln, bias=1.0).then_inc(aa.sem, 1)
                e.wait_ge(va.sem, va.at("rel", s))
                e.activation(dA[:, :], dt_[:, :], ACT.Exp, scale=aneg[:, 0:1]).then_inc(aa.sem, 1)
            each_sequence(e, sequence)

        @block.tensor
        def _(e):
            e.wait_ge(loaded, 16 * LOADS)
            e.wait_ge(vset, CI * (TAPS + 2))
            for k in range(TAPS):
                for c in range(CI):
                    e.matmul(pf[:, k * P:(k + 1) * P], win[:, c, :], scaled[:, c, k, :], start=c == 0, stop=c == CI - 1)
            for c in range(CI):
                m = e.matmul(pb[:, 0:2 * S0], bsc[:, c, :], wxd[:, c, :], start=c == 0, stop=c == CI - 1)
            m.then_inc(pset, 1)
            e.wait_ge(vset, CI * (TAPS + 2) + 2)
            for c in range(CI):
                m = e.matmul(pf[0:S0, 0:D], dmt[:, c, :], wot[:, c, :], start=c == 0, stop=c == CI - 1)
            m.then_inc(pset, 1)
            e.wait_ge(vset, CI * (TAPS + 2) + 3)
            def sequence(s):
                e.wait_ge(ga.sem, ga.at("stage", s))
                if later(s):
                    e.wait_ge(aa.sem, aa.passed(s))
                for t in range(T):
                    m = e.transpose(px[:, t * P:(t + 1) * P], xst[:, 0, t * P:(t + 1) * P], ident[:, :])
                m.then_inc(pe.sem, 1)
                e.wait_ge(aa.sem, aa.at("xpad", s))
                for a in range(2):
                    o = pu[:, a * L:(a + 1) * L]
                    for k in range(TAPS):
                        e.matmul(o, fused[:, k, a * S0:(a + 1) * S0], xpad[:, 0, k:k + L], start=k == 0, stop=False)
                    m = e.matmul(o, beta[:, a * S0:(a + 1) * S0], ind[:, :], start=False, stop=True)
                m.then_inc(pe.sem, 1)
                e.wait_ge(va.sem, va.at("scan", s))
                for t in range(T):
                    o = pz[:, t * P:(t + 1) * P]
                    e.matmul(o, z[:, 0, t * P:(t + 1) * P], wzo[:, :], start=True, stop=False)
                    m = e.matmul(o, ones[:, :], bout[:, :], start=False, stop=True)
                m.then_inc(pe.sem, 1)
            each_sequence(e, sequence)


def moe_phase(nc, I, X, ident):
    ctx, sb, ps = tools(nc)
    with ctx:
        wg = sb("b_wg", [P, NE, FI])
        wu = sb("b_wu", [P, NE, FI])
        wd = sb("b_wd", [P, CF, NE * D])
        rgu = sb("b_rgu", [P, 2 * NE])
        rd = sb("b_rd", [P, CF, NE])
        iota = sb("b_iota", [P, NE])
        xst = [sb(f"b_xst{i}", [P, L]) for i in range(2)]
        xT = sb("b_xT", [P, L])
        lg = sb("b_lg", [P, 3 * T, NE])
        mx = sb("b_mx", [P, 3 * T, 8])
        ix = sb("b_ix", [P, 3 * T, 8], U32)
        ixf = sb("b_ixf", [P, 3 * T, 8])
        df = sb("b_df", [P, 3 * T])
        ex = sb("b_ex", [P, 3 * T])
        sm = sb("b_sm", [P, 3 * T])
        pr = sb("b_pr", [P, 2, 3 * T])
        oh = sb("b_oh", [P, 3 * T, NE])
        o2 = sb("b_o2", [P, 3 * T, NE])
        cb = sb("b_cb", [P, 3 * T, NE])
        xc = sb("b_xc", [P, T, 2 * NE, D])
        xcT = [sb(f"b_xcT{i}", [P, 2 * NE, L]) for i in range(2)]
        sig = sb("b_sig", [P, CF * L])
        it = sb("b_it", [P, CF, L])
        acc = sb("b_acc", [P, T, D])
        stats = sb("b_stats", [P, T, 6])
        mv = sb("b_mv", [P, T, 2])
        ve = sb("b_ve", [P, T])
        y = sb("b_y", [P, T])
        h = sb("b_h", [P, T])
        tt = sb("b_t", [P, T])
        pg = ps("b_pg", [P, CF * L])
        pu = ps("b_pu", [P, CF * L])
        pd = ps("b_pd", [P, NE * D])
        pm = [ps("b_pm0", [P, 512]), ps("b_pm1", [P, 512])]
        pdown = [pg, pd]
        loaded = ctx.enter_context(nc.semaphore("b_loaded"))
        route = "mx*{0} ix*{0} xf df sm p0 p1 oh*{0} o2*{0} cb"
        pr_ = Steps(ctx, nc, "b_pe_r", f"xt lg ct*{2 * NE}")
        vr = Steps(ctx, nc, "b_dve_r", "lc " + route.format(2 * T) + f" xc*{T * 2 * NE}")
        ar = Steps(ctx, nc, "b_act_r", f"xT ex ctc*{2 * NE}")
        gr = Steps(ctx, nc, "b_pool_r", "st")
        pm_ = Steps(ctx, nc, "b_pe_m", "g*2 u ld d0 d1")
        vm = Steps(ctx, nc, "b_dve_m", "gu lc " + route.format(T) + f" acc0*{NE} acc1*{NE} bn*2 ag*2 ve nw*{VRS} out*2")
        am_ = Steps(ctx, nc, "b_act_m", "sig*2 ex")
        LOADS = 6
        block = ctx.enter_context(nc.Block())

        def passes(run, eng):
            run((0, 0), None)
            run((1, 1), (0, 0))
            with eng.Fori(0, (NSEQ - 2) // 2) as i:
                for p in range(2):
                    n = 2 * i + (2 + p)
                    run((n, p), (n - 1, 1 - p))
            run(None, (NSEQ - 1, 1))

        @block.sync
        def _(e):
            for dst, src in [(rgu[:, :], I["b_rgu"]), (iota[:, :], I["iota"]), (rd[:, :, :], I["b_rd"]),
                             (wg[:, :, :], I["b_wg"]), (wu[:, :, :], I["b_wu"]), (wd[:, :, :], I["b_wd"])]:
                e.dma_start(dst, src).then_inc(loaded, 16)

        @block.gpsimd
        def _(e):
            def run(R, M):
                if R:
                    n, p = R
                    if not isinstance(n, int) or n >= 2:
                        e.wait_ge(vm.sem, vm.at("acc1", n - 2))
                        at_rest(e)
                    e.tensor_copy(xst[p][:, :], X[:, n, :, :].rearrange("p t d -> p (t d)")).then_inc(gr.sem, 1)
            passes(run, e)

        @block.vector
        def _(e):
            e.wait_ge(loaded, 16 * LOADS)

            def top2(st, act, n, a, b):
                e.wait_ge(st.sem, st.at("lc", n))
                at_rest(e)
                for j in range(a, b):
                    e.max(mx[:, j, :], lg[:, j, :]).then_inc(st.sem, 1)
                e.wait_ge(st.sem, st.at("mx", n))
                at_rest(e)
                for j in range(a, b):
                    e.max_index(ix[:, j, :], mx[:, j, :], lg[:, j, :]).then_inc(st.sem, 1)
                e.wait_ge(st.sem, st.at("ix", n))
                e.tensor_copy(ixf[:, a:b, :], ix[:, a:b, :]).then_inc(st.sem, 1)
                e.tensor_tensor(df[:, a:b], mx[:, a:b, 1], mx[:, a:b, 0], ALU.subtract).then_inc(st.sem, 1)
                e.wait_ge(act.sem, act.at("ex", n))
                e.tensor_scalar(sm[:, a:b], ex[:, a:b], 1.0, None, ALU.add).then_inc(st.sem, 1)
                e.wait_ge(st.sem, st.at("sm", n))
                e.reciprocal(pr[:, 0, a:b], sm[:, a:b]).then_inc(st.sem, 1)
                e.wait_ge(st.sem, st.at("p0", n))
                e.tensor_tensor(pr[:, 1, a:b], pr[:, 0, a:b], ex[:, a:b], ALU.mult).then_inc(st.sem, 1)
                e.wait_ge(st.sem, st.at("p1", n))
                for j in range(a, b):
                    e.tensor_scalar(oh[:, j, :], iota[:, :], ixf[:, j, 0:1], pr[:, 0, j:j + 1], ALU.is_equal, ALU.mult)\
                        .then_inc(st.sem, 1)
                for j in range(a, b):
                    e.tensor_scalar(o2[:, j, :], iota[:, :], ixf[:, j, 1:2], pr[:, 1, j:j + 1], ALU.is_equal, ALU.mult)\
                        .then_inc(st.sem, 1)
                e.wait_ge(st.sem, st.at("o2", n))
                e.tensor_tensor(cb[:, a:b, :], oh[:, a:b, :], o2[:, a:b, :], ALU.add).then_inc(st.sem, 1)
                e.wait_ge(st.sem, st.at("cb", n))

            def run(R, M):
                if R:
                    n, p = R
                    e.wait_ge(pr_.sem, pr_.at("lg", n))
                    e.tensor_copy(lg[:, 0:2 * T, :], pm[1][:, 0:2 * T * NE].rearrange("p (j n) -> p j n", n=NE))\
                        .then_inc(vr.sem, 1)
                    top2(vr, ar, n, 0, 2 * T)
                    for x in range(2 * NE):
                        for t in range(T):
                            j = 2 * t + x // NE
                            e.tensor_scalar(xc[:, t, x, :], xst[p][:, t * D:(t + 1) * D], cb[:, j, x % NE:x % NE + 1],
                                            None, ALU.mult).then_inc(vr.sem, 1)
                if M:
                    m, p = M
                    e.wait_ge(am_.sem, am_.at("sig", m))
                    e.wait_ge(pm_.sem, pm_.at("u", m))
                    e.tensor_tensor(it[:, :, :].rearrange("p c l -> p (c l)"), pu[:, :], sig[:, :], ALU.mult).then_inc(vm.sem, 1)
                    e.wait_ge(pm_.sem, pm_.at("ld", m))
                    e.tensor_copy(lg[:, 2 * T:3 * T, :], pm[1][:, 0:T * NE].rearrange("p (j n) -> p j n", n=NE))\
                        .then_inc(vm.sem, 1)
                    top2(vm, am_, m, 2 * T, 3 * T)
                    for t in range(T):
                        e.wait_ge(pm_.sem, pm_.at(f"d{t}", m))
                        for x in range(NE):
                            if x:
                                e.wait_ge(vm.sem, vm.at(f"acc{t}", m, NE - x))
                            e.scalar_tensor_tensor(acc[:, t, :], pdown[t][:, x * D:(x + 1) * D], cb[:, 2 * T + t, x:x + 1],
                                                   acc[:, t, :] if x else xst[p][:, t * D:(t + 1) * D],
                                                   ALU.mult, ALU.add).then_inc(vm.sem, 1)
                    e.wait_ge(vm.sem, vm.at("acc1", m))
                    layernorm_stats(e, vm, m, lambda t: acc[:, t, :], stats, mv, "")
                    e.wait_ge(vm.sem, vm.at("ag", m))
                    e.tensor_scalar(ve[:, :], mv[:, :, 1], EPS, None, ALU.add).then_inc(vm.sem, 1)
                    vector_rsqrt(e, vm, m, "nw", y[:, :], ve[:, :], h[:, :], tt[:, :])
                    e.wait_ge(vm.sem, vm.at("nw", m))
                    for t in range(T):
                        e.tensor_scalar(X[:, m, t, :], acc[:, t, :], mv[:, t, 0:1], y[:, t:t + 1], ALU.subtract, ALU.mult)\
                            .then_inc(vm.sem, 1)
            passes(run, e)

        @block.scalar
        def _(e):
            def run(R, M):
                if R:
                    n, p = R
                    e.wait_ge(pr_.sem, pr_.at("xt", n))
                    e.activation(xT[:, :], pm[0][:, 0:L], ACT.Copy).then_inc(ar.sem, 1)
                    e.wait_ge(vr.sem, vr.at("df", n))
                    e.activation(ex[:, 0:2 * T], df[:, 0:2 * T], ACT.Exp).then_inc(ar.sem, 1)
                if M:
                    m, q = M
                    for j in range(2):
                        e.wait_ge(pm_.sem, pm_.at("g", m, 1 - j))
                        if j == 0 and later(m):
                            e.wait_ge(vm.sem, vm.at("gu", m - 1))
                        e.activation(sig[:, j * 512:(j + 1) * 512], pg[:, j * 512:(j + 1) * 512], ACT.Silu).then_inc(am_.sem, 1)
                if R:
                    for x in range(2 * NE):
                        e.wait_ge(pr_.sem, pr_.at("ct", n, 2 * NE - 1 - x))
                        e.activation(xcT[p][:, x, :], pm[x % 2][:, 0:L], ACT.Copy).then_inc(ar.sem, 1)
                if M:
                    e.wait_ge(vm.sem, vm.at("df", m))
                    e.activation(ex[:, 2 * T:3 * T], df[:, 2 * T:3 * T], ACT.Exp).then_inc(am_.sem, 1)
            passes(run, e)

        @block.tensor
        def _(e):
            e.wait_ge(loaded, 16 * LOADS)

            def run(R, M):
                def r_xt():
                    if R:
                        n, p = R
                        e.wait_ge(gr.sem, gr.at("st", n))
                        if later(n):
                            e.wait_ge(ar.sem, ar.at("ctc", n - 1))
                        for t in range(T):
                            m = e.transpose(pm[0][:, t * P:(t + 1) * P], xst[p][:, t * P:(t + 1) * P], ident[:, :])
                        m.then_inc(pr_.sem, 1)

                def r_lg():
                    if R:
                        n, p = R
                        e.wait_ge(ar.sem, ar.at("xT", n))
                        if not isinstance(n, int) or n >= 2:
                            e.wait_ge(vm.sem, vm.at("lc", n - 2))
                        for t in range(T):
                            m = e.matmul(pm[1][:, t * 2 * NE:(t + 1) * 2 * NE], xT[:, t * P:(t + 1) * P], rgu[:, :],
                                         start=True, stop=True)
                        m.then_inc(pr_.sem, 1)

                def r_ct(a, b):
                    if R:
                        n, p = R
                        for x in range(a, b):
                            e.wait_ge(vr.sem, vr.at("xc", n, T * (2 * NE - 1 - x)))
                            if x >= 2:
                                e.wait_ge(ar.sem, ar.at("ctc", n, 2 * NE + 1 - x))
                            for t in range(T):
                                m = e.transpose(pm[x % 2][:, t * P:(t + 1) * P], xc[:, t, x, :], ident[:, :])
                            m.then_inc(pr_.sem, 1)

                def m_experts(r, a, b):
                    if M:
                        m, p = M
                        w, o = ((wg, pg), (wu, pu))[r]
                        if a == 0:
                            if r == 0:
                                e.wait_ge(ar.sem, ar.at("ctc", m))
                                if later(m):
                                    e.wait_ge(vm.sem, vm.at("acc0", m - 1))
                            elif later(m):
                                e.wait_ge(vm.sem, vm.at("gu", m - 1))
                        for j in range(a, b):
                            for x in range(NE):
                                last = e.matmul(o[:, j * L:(j + 1) * L], w[:, x, j * P:(j + 1) * P], xcT[p][:, r * NE + x, :],
                                                start=x == 0, stop=x == NE - 1)
                            if j == CF - 1 or (r == 0 and j == 1):
                                last.then_inc(pm_.sem, 1)

                def m_ld():
                    if M:
                        m, p = M
                        e.wait_ge(vm.sem, vm.at("gu", m))
                        if R:
                            e.wait_ge(ar.sem, ar.at("ctc", R[0]))
                        for t in range(T):
                            for j in range(CF):
                                last = e.matmul(pm[1][:, t * NE:(t + 1) * NE], it[:, j, t * P:(t + 1) * P], rd[:, j, :],
                                                start=j == 0, stop=j == CF - 1)
                        last.then_inc(pm_.sem, 1)

                def m_down(t):
                    if M:
                        m, p = M
                        if t and later(m):
                            e.wait_ge(vm.sem, vm.at("acc1", m - 1))
                        for b in range(2):
                            for j in range(CF):
                                last = e.matmul(pdown[t][:, b * 512:(b + 1) * 512], it[:, j, t * P:(t + 1) * P],
                                                wd[:, j, b * 512:(b + 1) * 512], start=j == 0, stop=j == CF - 1)
                        last.then_inc(pm_.sem, 1)
                r_xt()
                m_experts(0, 0, 2)
                r_lg()
                m_experts(0, 2, 4)
                m_experts(1, 0, 1)
                r_ct(0, 4)
                m_experts(1, 1, 2)
                r_ct(4, 8)
                m_experts(1, 2, 3)
                r_ct(8, 12)
                m_experts(1, 3, 4)
                r_ct(12, 16)
                m_ld()
                m_down(0)
                m_down(1)
            passes(run, e)


def ssm2_phase(nc, I, X, ident):
    ctx, sb, ps = tools(nc)
    NK = 8
    with ctx:
        winT = sb("c_winT", [P, 2 * DI])
        winu = sb("c_winu", [P, CI, D])
        cwb = sb("c_cwb", [P, TAPS, DI])
        cvb = sb("c_cvb", [P, CI])
        gb = sb("c_gb", [P, 2])
        wot = sb("c_wot", [P, CI, D])
        am = sb("c_am", [S1, NK, 2, S1])
        bmT = sb("c_bmT", [P, CI, S1])
        cm = sb("c_cm", [S1, DI])
        wc = sb("c_wc", [P, TAPS, DI])
        bw = sb("c_bw", [P, S1])
        xh = sb("c_xh", [P, T, D])
        xn = sb("c_xn", [P, TAPS - 1 + L])
        sg = sb("c_sg", [P, CI, L])
        sz = sb("c_sz", [P, CI, L])
        st = [sb("c_st0", [S1, L]), sb("c_st1", [S1, L])]
        yT = sb("c_yT", [P, CI, L])
        res = sb("c_res", [P, T, D])
        stats = sb("c_stats", [P, T, 6])
        mv = sb("c_mv", [P, 2, T, 2])
        ve = sb("c_ve", [P, 2, T])
        y = sb("c_y", [P, 2, T])
        h = sb("c_h", [P, T])
        tt = sb("c_t", [P, T])
        px = ps("c_px", [P, 512])
        pc = ps("c_pc", [P, CI, L])
        pz = ps("c_pz", [P, CI, L])
        pst = [ps("c_ps0", [S1, 512]), ps("c_ps1", [S1, 512])]
        pk = ps("c_pk", [P, CI, L])
        po = ps("c_po", [P, 512])
        loaded = ctx.enter_context(nc.semaphore("c_loaded"))
        vset = ctx.enter_context(nc.semaphore("c_vset"))
        pset = ctx.enter_context(nc.semaphore("c_pset"))
        gset = ctx.enter_context(nc.semaphore("c_gset"))
        pe = Steps(ctx, nc, "c_pe", f"xt v conv z dbl*{NK} k y")
        va = Steps(ctx, nc, "c_va", f"Ibn*2 Iag*2 Ive Ish Isd xh*2 v0 hd*{NK} ad*{NK} kc ky res bn*2 ag*2 ve sh sd out*2"
                   .replace(f"hd*{NK} ad*{NK}", " ".join(f"hd{k} ad{k}" for k in range(NK))))
        aa = Steps(ctx, nc, "c_aa", "xn sg*2 sz")
        ga = Steps(ctx, nc, "c_ga", f"Irs*{RS} rs*{RS}")
        LOADS = 9
        block = ctx.enter_context(nc.Block())

        @block.sync
        def _(e):
            for dst, src in [(winT[:, :], I["c_winT"]), (winu[:, :, :], I["c_winu"]),
                             (cwb[:, :, :], I["c_cw"].to_broadcast([P, TAPS, DI])),
                             (cvb[:, :], I["c_cvb"]), (gb[:, :], I["c_gb"]), (wot[:, :, :], I["c_wot"]),
                             (am[:, 0, :, :], I["c_am"]), (bmT[:, :, :], I["c_bmT"]), (cm[:, :], I["c_cm"])]:
                e.dma_start(dst, src).then_inc(loaded, 16)

        @block.gpsimd
        def _(e):
            e.memset(xn[:, 0:TAPS - 1], 0.0).then_inc(gset, 1)
            def sequence(s):
                e.wait_ge(va.sem, va.at("Isd", s))
                at_rest(e)
                newton_rsqrt(e, ga, s, "Irs", y[:, 0, :], ve[:, 0, :], h[:, :], tt[:, :])
                e.wait_ge(va.sem, va.at("sd", s))
                e.wait_ge(ga.sem, ga.at("Irs", s))
                at_rest(e)
                newton_rsqrt(e, ga, s, "rs", y[:, 1, :], ve[:, 1, :], h[:, :], tt[:, :])
            each_sequence(e, sequence)

        @block.vector
        def _(e):
            e.wait_ge(loaded, 16 * LOADS)
            for k in range(TAPS):
                e.tensor_tensor(wc[:, k, :], winT[:, 0:DI], cwb[:, k, :], ALU.mult).then_inc(vset, 1)
            e.wait_ge(pset, 1)
            e.tensor_copy(bw[:, :], po[:, 0:S1]).then_inc(vset, 1)
            for k in range(1, NK):
                e.wait_ge(pset, k + 1)
                e.tensor_copy(am[:, k, :, :], pst[0][:, 0:2 * S1].rearrange("p (a b) -> p a b", a=2)).then_inc(vset, 1)
            e.wait_ge(vset, TAPS + NK)
            def sequence(s):
                layernorm_stats(e, va, s, lambda t: X[:, s, t, :], stats, mv[:, 0, :, :], "I")
                e.wait_ge(va.sem, va.at("Iag", s))
                e.tensor_scalar(ve[:, 0, :], mv[:, 0, :, 1], EPS, None, ALU.add).then_inc(va.sem, 1)
                e.wait_ge(va.sem, va.at("Ive", s))
                rsqrt_seed(e, va, s, "I", ve[:, 0, :].bitcast(I32), y[:, 0, :].bitcast(I32))
                e.wait_ge(ga.sem, ga.at("Irs", s))
                for t in range(T):
                    e.tensor_scalar(xh[:, t, :], X[:, s, t, :], mv[:, 0, t, 0:1], y[:, 0, t:t + 1], ALU.subtract, ALU.mult)\
                        .then_inc(va.sem, 1)
                e.wait_ge(pe.sem, pe.at("v", s))
                e.tensor_copy(st[0][:, :], po[0:S1, 0:L]).then_inc(va.sem, 1)
                for k in range(NK):
                    a, b, d = st[k % 2], st[(k + 1) % 2], 1 << k
                    e.wait_ge(va.sem, va.at(f"ad{k - 1}" if k else "v0", s))
                    e.tensor_copy(b[:, 0:d], a[:, 0:d]).then_inc(va.sem, 1)
                    e.wait_ge(pe.sem, pe.at("dbl", s, NK - 1 - k))
                    e.tensor_tensor(b[:, d:L], pst[k % 2][:, 0:L - d], a[:, d:L], ALU.add).then_inc(va.sem, 1)
                e.wait_ge(aa.sem, aa.at("sg", s))
                e.wait_ge(pe.sem, pe.at("k", s))
                e.tensor_tensor(yT[:, :, :], pk[:, :, :], sg[:, :, :], ALU.add).then_inc(va.sem, 1)
                e.wait_ge(va.sem, va.at("kc", s))
                e.wait_ge(aa.sem, aa.at("sz", s))
                e.tensor_tensor(yT[:, :, :], yT[:, :, :], sz[:, :, :], ALU.mult).then_inc(va.sem, 1)
                e.wait_ge(pe.sem, pe.at("y", s))
                e.scalar_tensor_tensor(res[:, :, :], X[:, s, :, :], 2.0, po[:, 0:L].rearrange("p (t d) -> p t d", t=T),
                                       ALU.mult, ALU.add).then_inc(va.sem, 1)
                e.wait_ge(va.sem, va.at("res", s))
                layernorm_stats(e, va, s, lambda t: res[:, t, :], stats, mv[:, 1, :, :], "")
                e.wait_ge(va.sem, va.at("ag", s))
                e.tensor_scalar(ve[:, 1, :], mv[:, 1, :, 1], EPS, None, ALU.add).then_inc(va.sem, 1)
                e.wait_ge(va.sem, va.at("ve", s))
                rsqrt_seed(e, va, s, "", ve[:, 1, :].bitcast(I32), y[:, 1, :].bitcast(I32))
                e.wait_ge(ga.sem, ga.at("rs", s))
                for t in range(T):
                    e.tensor_scalar(X[:, s, t, :], res[:, t, :], mv[:, 1, t, 0:1], y[:, 1, t:t + 1], ALU.subtract, ALU.mult)\
                        .then_inc(va.sem, 1)
            each_sequence(e, sequence)

        @block.scalar
        def _(e):
            e.wait_ge(loaded, 16 * LOADS)
            e.wait_ge(gset, 1)
            def sequence(s):
                e.wait_ge(pe.sem, pe.at("xt", s))
                e.activation(xn[:, TAPS - 1:], px[:, 0:L], ACT.Identity, bias=gb[:, 1:2], scale=gb[:, 0:1]).then_inc(aa.sem, 1)
                e.wait_ge(pe.sem, pe.at("conv", s))
                for c in range(CI):
                    e.activation(sg[:, c, :], pc[:, c, :], ACT.Silu, bias=cvb[:, c:c + 1]).then_inc(aa.sem, 1)
                e.wait_ge(pe.sem, pe.at("z", s))
                e.activation(sz[:, :, :], pz[:, :, :], ACT.Sigmoid).then_inc(aa.sem, 1)
            each_sequence(e, sequence)

        @block.tensor
        def _(e):
            e.wait_ge(loaded, 16 * LOADS)
            for c in range(CI):
                m = e.matmul(po[:, 0:S1], winu[:, c, :], bmT[:, c, :], start=c == 0, stop=c == CI - 1)
            m.then_inc(pset, 1)
            for k in range(1, NK):
                if k > 1:
                    e.wait_ge(vset, TAPS + k)
                e.matmul(pst[0][:, 0:S1], am[:, k - 1, 1, :], am[:, k - 1, 0, :], start=True, stop=True)
                e.matmul(pst[0][:, S1:2 * S1], am[:, k - 1, 0, :], am[:, k - 1, 1, :], start=True, stop=True).then_inc(pset, 1)
            e.wait_ge(vset, TAPS + NK)
            def sequence(s):
                e.wait_ge(va.sem, va.at("xh", s))
                for t in range(T):
                    m = e.transpose(px[:, t * P:(t + 1) * P], xh[:, t, :], ident[:, :])
                m.then_inc(pe.sem, 1)
                e.wait_ge(aa.sem, aa.at("xn", s))
                e.matmul(po[0:S1, 0:L], bw[:, :], xn[:, TAPS - 1:], start=True, stop=True).then_inc(pe.sem, 1)
                for c in range(CI):
                    for k in range(TAPS):
                        m = e.matmul(pc[:, c, :], wc[:, k, c * P:(c + 1) * P], xn[:, k:k + L], start=k == 0, stop=k == TAPS - 1)
                m.then_inc(pe.sem, 1)
                for c in range(CI):
                    m = e.matmul(pz[:, c, :], winT[:, DI + c * P:DI + (c + 1) * P], xn[:, TAPS - 1:], start=True, stop=True)
                m.then_inc(pe.sem, 1)
                for k in range(NK):
                    e.wait_ge(va.sem, va.at(f"ad{k - 1}" if k else "v0", s))
                    at_rest(e)
                    e.matmul(pst[k % 2][:, 0:L - (1 << k)], am[:, k, 1, :], st[k % 2][:, 0:L - (1 << k)], start=True, stop=True)\
                        .then_inc(pe.sem, 1)
                e.wait_ge(va.sem, va.at(f"ad{NK - 1}", s))
                for c in range(CI):
                    m = e.matmul(pk[:, c, :], cm[:, c * P:(c + 1) * P], st[NK % 2][:, :], start=True, stop=True)
                m.then_inc(pe.sem, 1)
                e.wait_ge(va.sem, va.at("ky", s))
                for t in range(T):
                    for c in range(CI):
                        m = e.matmul(po[:, t * P:(t + 1) * P], yT[:, c, t * P:(t + 1) * P], wot[:, c, :], start=c == 0, stop=c == CI - 1)
                m.then_inc(pe.sem, 1)
            each_sequence(e, sequence)


def transformer_phase(nc, I, X, ident, out):
    ctx, sb, ps = tools(nc)
    ORDER = [1, 3, 5, 7, 0, 2, 4, 6]
    N = HEADS * HD
    with ctx:
        X0 = sb("X0", [P, NSEQ, T, D])
        wqkv = sb("wqkv", [P, 3 * N])
        wo = sb("wo", [P, N // P, D])
        w1 = sb("w1", [P, 2 * HC, P])
        w2 = sb("w2", [P, HC, D])
        vec = sb("vec", [P, 2 + 2 * HC])
        b2 = sb("b2", [1, D])
        ones = sb("ones", [1, P])
        rows = sb("rows", [P, 4, HD])
        tab = sb("tab", [P, T, 4, HD])
        tabl = sb("tabl", [P, T, 4, HD])
        mask = sb("mask", [P, NW * KEYS])
        maskb = sb("maskb", [P, NW * KEYS], BF16)
        identb = sb("identb", [P, P], BF16)
        xin = sb("xin", [P, L])
        xs = sb("xs", [P, WIN + L + 1])
        sq = [sb(f"sq{i}", [P, N]) for i in range(2)]
        n2 = sb("n2", [P, 2, HEADS])
        nh = sb("nh", [P, 2, HEADS])
        nt = sb("nt", [P, 2, HEADS])
        rn = sb("rn", [P, 2, HEADS])
        qk = [sb(f"qk{i}", [P, HEADS, HD]) for i in range(4)]
        m2 = [sb(f"m2_{i}", [P, HEADS, HD]) for i in range(2)]
        rot = [sb(f"rot{i}", [P, N]) for i in range(2)]
        qT = [sb(f"qT{i}", [P, N // P, L]) for i in range(2)]
        kT = [sb(f"kT{i}", [P, N // P, WIN + L]) for i in range(2)]
        V = [sb(f"V{i}", [P, T, 2, N]) for i in range(2)]
        mx = sb("mx", [P, NG, NW])
        sm = sb("sm", [P, NG, NW])
        rc = sb("rc", [P, NG, NW])
        E = [sb(f"E{i}", [P, NW * KEYS]) for i in range(2)]
        PT = [sb(f"PT{i}", [P, NW * KEYS]) for i in range(2)]
        oT = sb("oT", [P, N // P, L])
        yin = sb("yin", [P, L])
        ys = sb("ys", [P, L + 1])
        stats = sb("stats", [P, T, 6])
        mv = sb("mv", [P, T, 2])
        ve = sb("ve", [P, T])
        yr = sb("yr", [P, T])
        yh = sb("yh", [P, T])
        yt = sb("yt", [P, T])
        xh = sb("xh", [P, T, D])
        xnT = sb("xnT", [P, L])
        gl = sb("gl", [P, HC, L])
        hh = sb("hh", [P, HC, L])
        fst = sb("fst", [P, NSEQ * T, 6])
        fmv = sb("fmv", [P, NSEQ * T, 2])
        fv = [sb(f"fv{i}", [P, NSEQ * T]) for i in range(4)]

        pQ = ps("pQ", [P, N])
        pM = [ps("pM0", [P, 512]), ps("pM1", [P, 512])]
        pC = ps("pC", [P, 512])
        pS = ps("pS", [P, NW * KEYS])
        pT = ps("pT", [P, 512])
        pO = ps("pO", [P, 512])
        pOV = [x[:, 0:L].rearrange("p (c t k) -> p c t k", c=2, t=T) for x in (pO, pT)]

        sem = {k: ctx.enter_context(nc.semaphore(k)) for k in
               ("const_loaded", "wqkv_loaded", "wo_loaded", "mlp_loaded", "rows_loaded", "v_setup", "g_setup",
                "tables", "v_shifted", "end_v", "stored")}
        root = Steps(ctx, nc, "end_g", f"rs*{RS}")
        PM = "v0a v0b tr0a tr0b v1a v1b tr1a tr1b tr2a tr2b tr3a tr3b"
        pa = Steps(ctx, nc, "pe_a", "xt qk0 v0a v0b qk1 qk2 qk3 tr0a tr0b v1a v1b tr1a tr1b tr2a tr2b tr3a tr3b")
        sa = Steps(ctx, nc, "act_a", "xs*2 sq0 cp0 v0a v0b sq1 cp1 sq2 cp2 sq3 cp3 tr0a tr0b v1a v1b tr1a tr1b "
                   "tr2a tr2b tr3a tr3b")
        va = Steps(ctx, nc, "dve_a", "rd0 rd1 mn0 r0sh r0sd qn0 cs0 sn0*2 qn1 cs1 sn1*2 rd2 rd3 mn1 r1sh r1sd "
                   "qn2 cs2 sn2*2 qn3 cs3 sn3*2")
        ga = Steps(ctx, nc, "pool_a", f"st rt0*{RS} ad0 ad1 rt1*{RS} ad2 ad3")
        pb = Steps(ctx, nc, "pe_b", "s0 pt0 s1 pv0 pt1 s2 pv1 pt2 s3 pv2 pt3 pv3 wo")
        sb_ = Steps(ctx, nc, "act_b", "ex0 pt0 ex1 ov0*2 pt1 ex2 ov1*2 pt2 ex3 ov2*2 pt3 ov3*2")
        vb = Steps(ctx, nc, "dve_b", " ".join(f"mx{g} su{g} sm{g} rc{g} no{g}" for g in range(4)) + " xa")
        pc = Steps(ctx, nc, "pe_c", "xt back xn h0 h1 h2 w2")
        sc = Steps(ctx, nc, "act_c", "sh*2 xn ge0 ge1 ge2")
        vc = Steps(ctx, nc, "dve_c", "bn*2 ag*2 ve sh sd xh*2 hid0 hid1 hid2 add")
        gc = Steps(ctx, nc, "pool_c", f"st rs*{RS}")
        block = ctx.enter_context(nc.Block())

        layer0 = {}

        def passes(run, eng):
            def one(n, s, l=None, lb=None, lc=None, ln=None):
                s, p = s if isinstance(s, tuple) else (s, s % 2)
                run((n, s, p, l), (n - 1, (s - 1) % NSEQ if isinstance(s, int) else s - 1, 1 - p, lb),
                    (n - 2, (s - 2) % NSEQ if isinstance(s, int) else s - 2, p, lc), (n + 1, None, 1 - p, ln))

            def middle(n0):
                with eng.Fori(0, (NSEQ - 6) // 2) as i:
                    for p in range(2):
                        s = 2 * i + (4 + p)
                        one(s if n0 is None else n0 + s, (s, p))

            layer0["now"] = True
            run(None, None, None, (0, 0, 0, 0))
            run((0, 0, 0, 0), None, None, (1, 1, 1, None))
            run((1, 1, 1, None), (0, 0, 0, 0), None, (2, 2, 0, None))
            one(2, 2, lc=0)
            one(3, 3)
            middle(None)
            one(NSEQ - 2, NSEQ - 2)
            layer0["now"] = False
            with eng.Fori(1, DEPTH) as l:
                n0 = l * NSEQ
                one(n0 - 1, NSEQ - 1, ln=l)
                one(n0, 0, l=l)
                one(n0 + 1, 1, lb=l)
                one(n0 + 2, 2, lc=l)
                one(n0 + 3, 3)
                middle(n0)
                one(n0 + (NSEQ - 2), NSEQ - 2)
            last = DEPTH * NSEQ
            run((last - 1, NSEQ - 1, 1, None), (last - 2, NSEQ - 2, 0, None), (last - 3, NSEQ - 3, 1, None), None)
            run(None, (last - 1, NSEQ - 1, 1, None), (last - 2, NSEQ - 2, 0, None), None)
            run(None, None, (last - 1, NSEQ - 1, 1, None), None)

        @block.sync
        def _(e):
            for dst, src in [(tab[:, :, :, :], I["tab"]), (mask[:, :], I["mask"]), (ones[:, :], I["ones"])]:
                e.dma_start(dst, src).then_inc(sem["const_loaded"], 16)

            def load(l, which):
                if which == "a":
                    e.dma_start(rows[:, :, :], I["rows"][l, :, :, :].to_broadcast([P, 4, HD])).then_inc(sem["rows_loaded"], 16)
                    e.dma_start(wqkv[:, :], I["wqkv"][l, :, :]).then_inc(sem["wqkv_loaded"], 16)
                elif which == "b":
                    e.dma_start(wo[:, :, :], I["wo"][l, :, :, :]).then_inc(sem["wo_loaded"], 16)
                else:
                    e.dma_start(w1[:, :, :], I["w1"][l, :, :, :]).then_inc(sem["mlp_loaded"], 16)
                    e.dma_start(w2[:, :, :], I["w2"][l, :, :, :]).then_inc(sem["mlp_loaded"], 16)
                    e.dma_start(vec[:, :], I["vec"][l, :, :]).then_inc(sem["mlp_loaded"], 16)
                    e.dma_start(b2[:, :], I["b2"][l, :, :]).then_inc(sem["mlp_loaded"], 16)

            def run(A, B, C, nxt):
                if A and A[3] is not None:
                    if later(A[0]):
                        e.wait_ge(sem["tables"], A[3] * 4 * T)
                        e.wait_ge(pa.sem, pa.at("v1b", A[0] - 1))
                    load(A[3], "a")
                if B and B[3] is not None:
                    if later(B[0]):
                        e.wait_ge(pb.sem, pb.at("wo", B[0] - 1))
                    load(B[3], "b")
                if C and C[3] is not None:
                    if later(C[0]):
                        e.wait_ge(pc.sem, pc.at("w2", C[0] - 1))
                    load(C[3], "c")
                if A:
                    n, s, par, l = A
                    if not layer0["now"] or not isinstance(n, int) or n >= 2:
                        e.wait_ge(pb.sem, pb.at("pv3", n - 2))
                    v, w = V[par][:, :, 0, :], V[par][:, :, 1, :]
                    e.wait_ge(sa.sem, sa.at("v0b", n))
                    e.dma_start(w[WIN:P, 0, :], v[0:P - WIN, 0, :]).then_inc(sem["v_shifted"], 16)
                    e.dma_start(w[0:WIN, 1, :], v[P - WIN:P, 0, :]).then_inc(sem["v_shifted"], 16)
                    e.wait_ge(sa.sem, sa.at("v1b", n))
                    e.dma_start(w[WIN:P, 1, :], v[0:P - WIN, 1, :]).then_inc(sem["v_shifted"], 16)
            passes(run, e)
            e.wait_ge(sem["end_v"], 4 + 3 * NSEQ * T)
            e.dma_start(out, X[:, :, :, :]).then_inc(sem["stored"], 16)
            e.wait_ge(sem["stored"], 16)

        @block.gpsimd
        def _(e):
            e.memset(xs[:, 0:WIN + 1], 0.0).then_inc(sem["g_setup"], 1)
            e.memset(ys[:, 0:1], 0.0).then_inc(sem["g_setup"], 1)
            for i in range(2):
                e.memset(kT[i][:, :, 0:WIN], 0.0).then_inc(sem["g_setup"], 1)
                e.memset(V[i][0:WIN, 0, 1, :], 0.0).then_inc(sem["g_setup"], 1)

            def run(A, B, C, nxt):
                if A:
                    n, s, par, l = A
                    if later(n):
                        e.wait_ge(pa.sem, pa.at("xt", n - 1))
                    at_rest(e)
                    e.tensor_copy(xin[:, :], X[:, s, :, :].rearrange("p t d -> p (t d)")).then_inc(ga.sem, 1)
                if C:
                    n, s, par, l = C
                    e.wait_ge(vb.sem, vb.at("xa", n))
                    if later(n):
                        e.wait_ge(pc.sem, pc.at("xt", n - 1))
                    at_rest(e)
                    e.tensor_copy(yin[:, :], X[:, s, :, :].rearrange("p t d -> p (t d)")).then_inc(gc.sem, 1)
                def add(u):
                    if A:
                        n = A[0]
                        e.wait_ge(va.sem, va.at(f"sn{u}", n))
                        at_rest(e)
                        e.tensor_tensor(rot[u % 2][:, :], rot[u % 2][:, :], m2[u % 2][:, :, :].rearrange("p h d -> p (h d)"),
                                        ALU.add).then_inc(ga.sem, 1)

                def roots(t):
                    if A:
                        n = A[0]
                        e.wait_ge(va.sem, va.at(f"r{t}sd", n))
                        at_rest(e)
                        newton_rsqrt(e, ga, n, f"rt{t}", rn[:, :, :], n2[:, :, :], nh[:, :, :], nt[:, :, :])
                roots(0)
                if C:
                    e.wait_ge(vc.sem, vc.at("sd", C[0]))
                    at_rest(e)
                    newton_rsqrt(e, gc, C[0], "rs", yr[:, :], ve[:, :], yh[:, :], yt[:, :])
                add(0)
                add(1)
                roots(1)
                add(2)
                add(3)
            passes(run, e)
            e.wait_ge(sem["end_v"], 4 + 2 * NSEQ * T)
            at_rest(e)
            newton_rsqrt(e, root, 0, "rs", *(fv[i][:, :] for i in (2, 3, 0, 1)))

        @block.vector
        def _(e):
            e.wait_ge(sem["const_loaded"], 48)
            e.tensor_copy(maskb[:, :], mask[:, :]).then_inc(sem["v_setup"], 1)
            e.tensor_copy(identb[:, :], ident[:, :]).then_inc(sem["v_setup"], 1)
            e.tensor_copy(X0[:, :, :, :], X[:, :, :, :]).then_inc(sem["v_setup"], 1)
            e.wait_ge(sem["v_setup"], 3)

            def wide(a, shape):
                return a.to_broadcast(shape)

            def run(A, B, C, nxt):
                if A:
                    n, s, par, l = A
                    if l is not None:
                        e.wait_ge(sem["rows_loaded"], 16 * (l + 1))
                        if later(n):
                            e.wait_ge(va.sem, va.at("sn3", n - 1))
                        for t in range(T):
                            for k in range(4):
                                e.tensor_tensor(tabl[:, t, k, :], tab[:, t, k, :], rows[:, k, :], ALU.mult).then_inc(sem["tables"], 1)
                        e.wait_ge(sem["tables"], (l + 1) * 4 * T)
                sv = pS[:, :].rearrange("p (w k) -> p w k", k=KEYS)

                def ev(g):
                    return E[g % 2][:, :].rearrange("p (w k) -> p w k", k=KEYS)

                def less_max(g):
                    if B:
                        b = B[0]
                        e.wait_ge(pb.sem, pb.at(f"s{g}", b))
                        e.tensor_reduce(mx[:, g, :], sv, AX.X, ALU.max).then_inc(vb.sem, 1)
                        e.wait_ge(vb.sem, vb.at(f"mx{g}", b))
                        e.tensor_tensor(ev(g), sv, wide(mx[:, g, :].unsqueeze(2), [P, NW, KEYS]), ALU.subtract).then_inc(vb.sem, 1)

                def by_sum(g):
                    if B:
                        b = B[0]
                        e.wait_ge(sb_.sem, sb_.at(f"ex{g}", b))
                        e.tensor_reduce(sm[:, g, :], ev(g), AX.X, ALU.add).then_inc(vb.sem, 1)
                        e.wait_ge(vb.sem, vb.at(f"sm{g}", b))
                        e.reciprocal(rc[:, g, :], sm[:, g, :]).then_inc(vb.sem, 1)
                        e.wait_ge(vb.sem, vb.at(f"rc{g}", b))
                        e.tensor_tensor(ev(g), ev(g), wide(rc[:, g, :].unsqueeze(2), [P, NW, KEYS]), ALU.mult).then_inc(vb.sem, 1)

                def norm2(u):
                    if A:
                        n = A[0]
                        e.wait_ge(sa.sem, sa.at(f"sq{u}", n))
                        e.tensor_reduce(n2[:, u % 2, :], sq[u % 2][:, :].rearrange("p (h d) -> p h d", d=HD), AX.X, ALU.add)\
                            .then_inc(va.sem, 1)

                def roots(t):
                    if A:
                        n = A[0]
                        e.wait_ge(va.sem, va.at(f"rd{2 * t + 1}", n))
                        e.tensor_scalar(n2[:, :, :], n2[:, :, :], 1e-24, None, ALU.max).then_inc(va.sem, 1)
                        e.wait_ge(va.sem, va.at(f"mn{t}", n))
                        rsqrt_seed(e, va, n, f"r{t}", n2[:, :, :].bitcast(I32), rn[:, :, :].bitcast(I32))

                def unit(u):
                    if A:
                        n = A[0]
                        e.wait_ge(sa.sem, sa.at(f"cp{u}", n))
                        e.wait_ge(ga.sem, ga.at(f"rt{u // 2}", n))
                        e.tensor_tensor(qk[u][:, :, :], qk[u][:, :, :],
                                        wide(rn[:, u % 2, :].unsqueeze(2), [P, HEADS, HD]), ALU.mult).then_inc(va.sem, 1)

                def rotate(u):
                    if A:
                        n = A[0]
                        t, w = u // 2, u % 2
                        e.wait_ge(va.sem, va.at(f"qn{u}", n))
                        if u >= 2:
                            e.wait_ge(pa.sem, pa.at(f"tr{u - 2}b", n))
                        elif later(n):
                            e.wait_ge(pa.sem, pa.at(f"tr{u + 2}b", n - 1))
                        e.tensor_tensor(rot[u % 2][:, :].rearrange("p (h d) -> p h d", d=HD), qk[u][:, :, :],
                                        wide(tabl[:, t, 2 * w, :].unsqueeze(1), [P, HEADS, HD]), ALU.mult).then_inc(va.sem, 1)
                        for a, b_ in ((0, HD // 2), (HD // 2, 0)):
                            e.tensor_tensor(m2[u % 2][:, :, a:a + HD // 2], qk[u][:, :, b_:b_ + HD // 2],
                                            wide(tabl[:, t, 2 * w + 1, a:a + HD // 2].unsqueeze(1), [P, HEADS, HD // 2]),
                                            ALU.mult).then_inc(va.sem, 1)

                def hid(j):
                    if C:
                        e.wait_ge(sc.sem, sc.at(f"ge{j}", C[0]))
                        e.scalar_tensor_tensor(hh[:, j, :], pC[:, 0:L], vec[:, 2 + j:3 + j], gl[:, j, :], ALU.add, ALU.mult)\
                            .then_inc(vc.sem, 1)
                def stats_c():
                    if C:
                        c = C[0]
                        e.wait_ge(pc.sem, pc.at("back", c))
                        layernorm_stats(e, vc, c, lambda t: pC[:, L + t * P:L + (t + 1) * P], stats, mv, "")
                        e.wait_ge(vc.sem, vc.at("ag", c))
                        e.tensor_scalar(ve[:, :], mv[:, :, 1], EPS, None, ALU.add).then_inc(vc.sem, 1)
                        e.wait_ge(vc.sem, vc.at("ve", c))
                        rsqrt_seed(e, vc, c, "", ve[:, :].bitcast(I32), yr[:, :].bitcast(I32))

                def normal_c():
                    if C:
                        e.wait_ge(gc.sem, gc.at("rs", C[0]))
                        for t in range(T):
                            e.tensor_scalar(xh[:, t, :], pC[:, L + t * P:L + (t + 1) * P], mv[:, t, 0:1], yr[:, t:t + 1],
                                            ALU.subtract, ALU.mult).then_inc(vc.sem, 1)
                less_max(0)
                by_sum(0)
                norm2(0)
                stats_c()
                norm2(1)
                roots(0)
                less_max(1)
                by_sum(1)
                unit(0)
                rotate(0)
                less_max(2)
                normal_c()
                by_sum(2)
                unit(1)
                rotate(1)
                less_max(3)
                hid(0)
                norm2(2)
                norm2(3)
                roots(1)
                by_sum(3)
                unit(2)
                rotate(2)
                hid(1)
                unit(3)
                rotate(3)
                hid(2)
                if B:
                    e.wait_ge(pb.sem, pb.at("wo", B[0]))
                    xv = X[:, B[1], :, :].rearrange("p t d -> p (t d)")
                    e.tensor_tensor(xv, xv, pT[:, 0:L], ALU.add).then_inc(vb.sem, 1)
                if C:
                    e.wait_ge(pc.sem, pc.at("w2", C[0]))
                    xv = X[:, C[1], :, :].rearrange("p t d -> p (t d)")
                    e.tensor_tensor(xv, xv, pC[:, 0:L], ALU.add).then_inc(vc.sem, 1)
            passes(run, e)
            ev = sem["end_v"]
            NT = NSEQ * T
            e.wait_ge(vc.sem, vc.at("add", DEPTH * NSEQ - 1))
            e.tensor_tensor(X0[:, :, :, :], X0[:, :, :, :], X[:, :, :, :], ALU.add).then_inc(ev, 1)
            e.wait_ge(ev, 1)
            xf = X0[:, :, :, :].rearrange("p s t d -> p (s t) d")
            for t in range(NT):
                e.bn_stats(fst[:, t, :], xf[:, t, :]).then_inc(ev, 1)
            e.wait_ge(ev, 1 + NT)
            for t in range(NT):
                e.bn_aggr(fmv[:, t, :], fst[:, t, :]).then_inc(ev, 1)
            e.wait_ge(ev, 1 + 2 * NT)
            e.tensor_scalar(fv[3][:, :], fmv[:, :, 1], EPS, None, ALU.add).then_inc(ev, 1)
            e.wait_ge(ev, 2 + 2 * NT)
            e.tensor_scalar(fv[2][:, :].bitcast(I32), fv[3][:, :].bitcast(I32), 1, None, ALU.logical_shift_right).then_inc(ev, 1)
            e.wait_ge(ev, 3 + 2 * NT)
            e.tensor_scalar(fv[2][:, :].bitcast(I32), fv[2][:, :].bitcast(I32), -1.0, MAGIC, ALU.mult, ALU.add).then_inc(ev, 1)
            e.wait_ge(root.sem, RS)
            xo = X[:, :, :, :].rearrange("p s t d -> p (s t) d")
            for t in range(NT):
                e.tensor_scalar(xo[:, t, :], xf[:, t, :], fmv[:, t, 0:1], fv[2][:, t:t + 1], ALU.subtract, ALU.mult).then_inc(ev, 1)

        @block.scalar
        def _(e):
            e.wait_ge(sem["g_setup"], 6)

            def run(A, B, C, nxt):
                def copy_m(kind, u):
                    if A:
                        n, s, par, l = A
                        for i, half in enumerate("ab"):
                            if kind == "v" and i == 0 and u == 0 and (not layer0["now"] or not isinstance(n, int) or n >= 2):
                                e.wait_ge(sem["v_shifted"], 48 * (n - 1))
                                e.wait_ge(pb.sem, pb.at("pv3", n - 2))
                            e.wait_ge(pa.sem, pa.at(f"{kind}{u}{half}", n))
                            if kind == "v":
                                dst, src = V[par][:, u, 0, i * 512:(i + 1) * 512], pM[i][:, :]
                            else:
                                t, w = u // 2, u % 2
                                buf, off = (kT[par], WIN) if w else (qT[par], 0)
                                dst = buf[:, 4 * i:4 * i + 4, off + t * P:off + (t + 1) * P]
                                src = pM[i][:, :].rearrange("p (c t) -> p c t", c=4)
                            e.activation(dst, src, ACT.Copy).then_inc(sa.sem, 1)

                def squares(u):
                    if A:
                        n = A[0]
                        e.wait_ge(pa.sem, pa.at(f"qk{u}", n))
                        if u >= 2:
                            e.wait_ge(va.sem, va.at(f"rd{u - 2}", n))
                        elif later(n):
                            e.wait_ge(va.sem, va.at(f"rd{u + 2}", n - 1))
                        e.activation(sq[u % 2][:, :], pQ[:, :], ACT.Square).then_inc(sa.sem, 1)
                        if later(n):
                            e.wait_ge(va.sem, va.at(f"sn{u}", n - 1))
                        e.activation(qk[u][:, :, :].rearrange("p h d -> p (h d)"), pQ[:, :], ACT.Copy).then_inc(sa.sem, 1)

                def exps(g):
                    if B:
                        e.wait_ge(vb.sem, vb.at(f"su{g}", B[0]))
                        e.activation(E[g % 2][:, :], E[g % 2][:, :], ACT.Exp, scale=8.0).then_inc(sb_.sem, 1)

                def copy_b(g):
                    if B:
                        e.wait_ge(pb.sem, pb.at(f"pt{g}", B[0]))
                        e.activation(PT[g % 2][:, :], pT[:, :], ACT.Copy).then_inc(sb_.sem, 1)

                def copy_o(g):
                    if B:
                        e.wait_ge(pb.sem, pb.at(f"pv{g}", B[0]))
                        for i in range(2):
                            e.activation(oT[:, 2 * g:2 * g + 2, :].rearrange("p c (t k) -> p c t k", t=T)[:, :, :, KEYS * i:KEYS * (i + 1)],
                                         pOV[i], ACT.Copy).then_inc(sb_.sem, 1)

                def gelu(j):
                    if C:
                        e.wait_ge(pc.sem, pc.at(f"h{j}", C[0]))
                        e.activation(gl[:, j, :], pC[:, L:2 * L], ACT.Gelu, bias=vec[:, 2 + HC + j:3 + HC + j]).then_inc(sc.sem, 1)
                exps(0)
                squares(0)
                copy_m("v", 0)
                copy_b(0)
                if C:
                    e.wait_ge(pc.sem, pc.at("xt", C[0]))
                    e.activation(ys[0:HALF, 0:L], pC[0:HALF, 0:L], ACT.Copy).then_inc(sc.sem, 1)
                    e.activation(ys[HALF:P, 1:L + 1], pC[HALF:P, 0:L], ACT.Copy).then_inc(sc.sem, 1)
                squares(1)
                exps(1)
                copy_o(0)
                squares(2)
                copy_b(1)
                squares(3)
                exps(2)
                copy_o(1)
                copy_m("tr", 0)
                if C:
                    if C[3] is not None:
                        e.wait_ge(sem["mlp_loaded"], 64 * (C[3] + 1))
                    e.wait_ge(pc.sem, pc.at("xn", C[0]))
                    e.activation(xnT[:, :], pC[:, 0:L], ACT.Identity, bias=vec[:, 1:2], scale=vec[:, 0:1]).then_inc(sc.sem, 1)
                copy_b(2)
                gelu(0)
                exps(3)
                copy_m("v", 1)
                copy_o(2)
                copy_m("tr", 1)
                copy_b(3)
                gelu(1)
                copy_o(3)
                gelu(2)
                copy_m("tr", 2)
                copy_m("tr", 3)
                if nxt:
                    e.wait_ge(pa.sem, pa.at("xt", nxt[0]))
                    e.activation(xs[0:HALF, WIN:WIN + L], pM[0][0:HALF, 0:L], ACT.Copy).then_inc(sa.sem, 1)
                    e.activation(xs[HALF:P, WIN + 1:WIN + L + 1], pM[0][HALF:P, 0:L], ACT.Copy).then_inc(sa.sem, 1)
            passes(run, e)

        @block.tensor
        def _(e):
            e.wait_ge(sem["v_setup"], 3)
            e.wait_ge(sem["g_setup"], 6)
            before = {}
            prev = ["tr3a", "tr3b"]
            for name in ["xt"] + PM.split():
                i = 0 if name == "xt" or name[-1] == "a" else 1
                before[name] = prev[i]
                prev[i] = "xs" if name == "xt" else name

            def run(A, B, C, nxt):
                def bank_free(n, name):
                    back = before[name]
                    first = name == "xt" or name == "v0b"
                    if not first:
                        e.wait_ge(sa.sem, sa.at(back, n))
                    elif later(n):
                        e.wait_ge(sa.sem, sa.at(back, n - 1))

                def a_xt(A):
                    if not A:
                        return
                    n, s, par, l = A
                    e.wait_ge(ga.sem, ga.at("st", n))
                    bank_free(n, "xt")
                    for t in range(T):
                        m = e.transpose(pM[0][:, t * P:(t + 1) * P], xin[:, t * P:(t + 1) * P], ident[:, :])
                    m.then_inc(pa.sem, 1)

                def a_qk(u):
                    if not A:
                        return
                    n, s, par, l = A
                    t, w = u // 2, u % 2
                    if u == 0:
                        if l is not None:
                            e.wait_ge(sem["wqkv_loaded"], 16 * (l + 1))
                        e.wait_ge(sa.sem, sa.at("xs", n))
                    if u:
                        e.wait_ge(sa.sem, sa.at(f"cp{u - 1}", n))
                    for i in range(2):
                        m = e.matmul(pQ[:, i * 512:(i + 1) * 512], xs[:, WIN + t * P:WIN + (t + 1) * P],
                                     wqkv[:, w * N + i * 512:w * N + (i + 1) * 512], start=True, stop=True)
                    m.then_inc(pa.sem, 1)

                def a_v(u):
                    if not A:
                        return
                    n, s, par, l = A
                    o = WIN + u * P
                    for i, half in enumerate("ab"):
                        bank_free(n, f"v{u}{half}")
                        e.matmul(pM[i][:, :], xs[:, o:o + P], wqkv[:, 2 * N + i * 512:2 * N + (i + 1) * 512],
                                 start=True, stop=True).then_inc(pa.sem, 1)

                def a_tr(u):
                    if not A:
                        return
                    n, s, par, l = A
                    e.wait_ge(ga.sem, ga.at(f"ad{u}", n))
                    for i, half in enumerate("ab"):
                        bank_free(n, f"tr{u}{half}")
                        for c in range(4):
                            m = e.transpose(pM[i][:, c * P:(c + 1) * P], rot[u % 2][:, (4 * i + c) * P:(4 * i + c + 1) * P], ident[:, :])
                        m.then_inc(pa.sem, 1)

                def b_s(g):
                    if not B:
                        return
                    b, s, par, l = B
                    if g == 0:
                        e.wait_ge(sa.sem, sa.at("tr3b", b))
                        e.wait_ge(sem["v_shifted"], 48 * (b + 1))
                    if g or later(b):
                        e.wait_ge(vb.sem, vb.at(f"su{g - 1}", b) if g else vb.at("su3", b - 1))
                    e.matmul(pS[:, :], identb[:, :], maskb[:, :], start=True, stop=False, skip_group_check=True)
                    for i, w in enumerate(ORDER):
                        for j in range(4):
                            h = 4 * g + j
                            r = HD * (h % 2)
                            m = e.matmul(pS[32 * j:32 * j + 32, i * KEYS:(i + 1) * KEYS], qT[par][r:r + HD, h // 2, WIN * w:WIN * (w + 1)],
                                         kT[par][r:r + HD, h // 2, WIN * w:WIN * (w + 2)], start=False, stop=(i == NW - 1),
                                         skip_group_check=True, tile_position=(r, 32 * j))
                    m.then_inc(pb.sem, 1)

                def b_pt(g):
                    if not B:
                        return
                    b = B[0]
                    e.wait_ge(vb.sem, vb.at(f"no{g}", b))
                    if g:
                        e.wait_ge(sb_.sem, sb_.at(f"ov{g - 1}", b))
                    elif later(b):
                        e.wait_ge(vb.sem, vb.at("xa", b - 1))
                    for i in range(4):
                        m = e.transpose(pT[:, i * P:(i + 1) * P], E[g % 2][:, i * P:(i + 1) * P], ident[:, :])
                    m.then_inc(pb.sem, 1)

                def b_pv(g):
                    if not B:
                        return
                    b, s, par, l = B
                    e.wait_ge(sb_.sem, sb_.at(f"pt{g}", b))
                    at_rest(e)
                    for i, w in enumerate(ORDER):
                        r = KEYS * (i % 2)
                        for j in range(4):
                            h = 4 * g + j
                            c = HD * (j % 2)
                            m = e.matmul(pOV[i % 2][c:c + HD, j // 2, w // 4, WIN * (w % 2):WIN * (w % 2 + 1)], V[par][r:r + KEYS, w // 4, 1 - w % 2, h * HD:(h + 1) * HD],
                                         PT[g % 2][r:r + KEYS, (i // 2) * P + 32 * j:(i // 2) * P + 32 * j + 32],
                                         start=True, stop=True, tile_position=(r, c))
                    m.then_inc(pb.sem, 1)

                def b_wo():
                    if not B:
                        return
                    b, s, par, l = B
                    if l is not None:
                        e.wait_ge(sem["wo_loaded"], 16 * (l + 1))
                    e.wait_ge(sb_.sem, sb_.at("ov3", b))
                    for t in range(T):
                        for c in range(N // P):
                            m = e.matmul(pT[:, t * P:(t + 1) * P], oT[:, c, t * P:(t + 1) * P], wo[:, c, :], start=c == 0, stop=c == N // P - 1)
                    m.then_inc(pb.sem, 1)

                def c_xt():
                    if not C:
                        return
                    c, s, par, l = C
                    e.wait_ge(gc.sem, gc.at("st", c))
                    if later(c):
                        e.wait_ge(vc.sem, vc.at("add", c - 1))
                    for t in range(T):
                        m = e.transpose(pC[:, t * P:(t + 1) * P], yin[:, t * P:(t + 1) * P], ident[:, :])
                    m.then_inc(pc.sem, 1)

                def c_back():
                    if not C:
                        return
                    c = C[0]
                    e.wait_ge(sc.sem, sc.at("sh", c))
                    for t in range(T):
                        m = e.transpose(pC[:, L + t * P:L + (t + 1) * P], ys[:, t * P:(t + 1) * P], ident[:, :])
                    m.then_inc(pc.sem, 1)

                def c_xn():
                    if not C:
                        return
                    c = C[0]
                    e.wait_ge(vc.sem, vc.at("xh", c))
                    for t in range(T):
                        m = e.transpose(pC[:, t * P:(t + 1) * P], xh[:, t, :], ident[:, :])
                    m.then_inc(pc.sem, 1)

                def c_h(j):
                    if not C:
                        return
                    c, s, par, l = C
                    if j == 0:
                        if l is not None:
                            e.wait_ge(sem["mlp_loaded"], 64 * (l + 1))
                        e.wait_ge(sc.sem, sc.at("xn", c))
                    else:
                        e.wait_ge(vc.sem, vc.at(f"hid{j - 1}", c))
                    e.matmul(pC[:, 0:L], w1[:, j, :], xnT[:, :], start=True, stop=True)
                    e.matmul(pC[:, L:2 * L], w1[:, HC + j, :], xnT[:, :], start=True, stop=True).then_inc(pc.sem, 1)

                def c_w2():
                    if not C:
                        return
                    c = C[0]
                    e.wait_ge(vc.sem, vc.at("hid2", c))
                    for t in range(T):
                        for j in range(HC):
                            e.matmul(pC[:, t * P:(t + 1) * P], hh[:, j, t * P:(t + 1) * P], w2[:, j, :], start=j == 0, stop=False)
                        m = e.matmul(pC[:, t * P:(t + 1) * P], ones[:, :], b2[:, :], start=False, stop=True)
                    m.then_inc(pc.sem, 1)

                b_s(0)
                a_qk(0)
                a_v(0)
                c_xt()
                b_pt(0)
                a_qk(1)
                c_back()
                b_s(1)
                b_pv(0)
                a_qk(2)
                b_pt(1)
                b_s(2)
                a_qk(3)
                b_pv(1)
                a_tr(0)
                c_xn()
                b_pt(2)
                b_s(3)
                c_h(0)
                a_v(1)
                b_pv(2)
                a_tr(1)
                c_h(1)
                b_pt(3)
                b_pv(3)
                b_wo()
                c_h(2)
                a_tr(2)
                c_w2()
                a_tr(3)
                a_xt(nxt)
            passes(run, e)


def layout(i):
    f = np.float32

    def rows(a, inner=P):
        return a.reshape(a.shape[0] // inner, inner, *a.shape[1:]).swapaxes(0, 1)
    a = {}
    g = lambda k: np.asarray(i[k])
    a["x"] = g("L0_attn_x").reshape(NSEQ, T, P, D).transpose(2, 0, 1, 3)
    a["a_win"] = rows(g("L0_attn_W_in"))
    a["a_wxd"] = rows(np.concatenate([g("L0_attn_W_dt").T, g("L0_attn_W_x").T], 1))
    a["a_cw"] = rows(g("L0_attn_conv_w")[:, 0, :])
    a["a_bias_in"] = rows(np.stack([g("L0_attn_b_in"), g("L0_attn_conv_b")], 1))
    a["a_svec"] = np.stack([g("L0_attn_b_dt"), g("L0_attn_b_x"), g("L0_attn_A_log")], 1)
    a["a_dmt"] = rows(g("L0_attn_D_mat").T)
    a["a_wot"] = rows(g("L0_attn_W_out").T)
    a["a_bout"] = g("L0_attn_b_out")[None]
    a["b_wg"] = g("L0_ffn_w_gate").transpose(2, 0, 1)
    a["b_wu"] = g("L0_ffn_w_up").transpose(2, 0, 1)
    a["b_wd"] = rows(g("L0_ffn_w_down").transpose(2, 0, 1).reshape(FI, NE * D))
    a["b_rgu"] = np.concatenate([g("L0_ffn_router_gate").T, g("L0_ffn_router_up").T], 1)
    a["b_rd"] = rows(g("L0_ffn_router_down").T)
    a["c_winT"] = g("L1_attn_W_in").T
    a["c_winu"] = rows(g("L1_attn_W_in")[0:DI])
    a["c_cw"] = g("L1_attn_conv_w")[:, 0, :].T[None]
    a["c_cvb"] = g("L1_attn_conv_b").reshape(CI, P).T
    a["c_gb"] = np.stack([g("L1_attn_ln_gamma"), g("L1_attn_ln_beta")], 1)
    a["c_wot"] = rows(g("L1_attn_W_out").T)
    a["c_am"] = np.stack([g("L1_attn_A"), g("L1_attn_A").T], 1)
    a["c_bmT"] = rows(g("L1_attn_Bm").T)
    a["c_cm"] = g("L1_attn_Cm")
    a["wqkv"] = g("L1_ffn_Wqkv")
    a["wo"] = g("L1_ffn_Wo").reshape(DEPTH, HEADS * HD // P, P, D).transpose(0, 2, 1, 3)
    m = g("L1_ffn_W2").shape[1]
    w1 = np.zeros((DEPTH, D, 2, HC * P), f)
    w1[:, :, :, :m] = g("L1_ffn_W1").reshape(DEPTH, D, 2, m)
    a["w1"] = w1.reshape(DEPTH, D, 2 * HC, P)
    w2 = np.zeros((DEPTH, HC * P, D), f)
    w2[:, :m] = g("L1_ffn_W2")
    a["w2"] = w2.reshape(DEPTH, HC, P, D).transpose(0, 2, 1, 3)
    b1 = np.zeros((DEPTH, 2, HC * P), f)
    b1[:, :, :m] = g("L1_ffn_b1").reshape(DEPTH, 2, m)
    a["vec"] = np.concatenate([np.stack([g("L1_ffn_ln_g"), g("L1_ffn_ln_b")], 2),
                               b1.reshape(DEPTH, 2 * HC, P).transpose(0, 2, 1)], 2)
    a["b2"] = g("L1_ffn_b2")[:, None]
    q, k = g("L1_ffn_q_scale"), g("L1_ffn_k_scale")
    swap = lambda v: np.concatenate([v[:, HD // 2:], v[:, :HD // 2]], 1)
    a["rows"] = np.stack([q, swap(q), k, swap(k)], 1)[:, None]
    a["ident"] = np.eye(P, dtype=f)
    a["ones"] = np.ones((1, P), f)
    a["iota"] = np.tile(np.arange(NE, dtype=f), (P, 1))
    a["ind"] = np.stack([(np.arange(L) >= TAPS - 1 - t) for t in range(TAPS)] + [np.ones(L, bool)]).astype(f)
    half = np.arange(0, HD, 2, dtype=f)
    inv = (f(1) / f(10000) ** (half / f(HD))).astype(f)
    t = np.arange(L, dtype=f)
    fr = np.concatenate([t[:, None] * inv[None]] * 2, 1)
    base = (half + f(0.4 * HD)) / f(1.4 * HD)
    sc = base[None].astype(np.float64) ** ((t[:, None] - L // 2) / (WIN // 2))
    sc = np.concatenate([sc, sc], 1)
    sign = np.where(np.arange(HD) < HD // 2, -1.0, 1.0)
    co, si = np.cos(fr.astype(np.float64)), np.sin(fr.astype(np.float64)) * sign
    tab = np.stack([co * sc, si * sc, co / sc, si / sc], 1).astype(f)
    a["tab"] = tab.reshape(T, P, 4, HD).swapaxes(0, 1)
    qi, kj = np.arange(WIN)[:, None], np.arange(WIN)[None]
    pair = np.concatenate([np.where(qi > kj, -1e30, 0), np.where(qi < kj, -1e30, 0)], 1)
    mask = np.stack([pair] * NW, 1)
    mask[:, 4, 0:WIN] = -1e30
    a["mask"] = np.tile(mask.reshape(WIN, NW * KEYS), (4, 1)).astype(f)
    return {k: np.ascontiguousarray(v) for k, v in a.items()}


def kernel(**inputs):
    import concourse.bacc as _bacc
    from concourse.bass_utils import run_bass_kernel_spmd as _run

    nc = _bacc.Bacc("TRN2", target_bir_lowering=False, num_devices=1)
    arrays = layout(inputs)
    I = {k: nc.dram_tensor("in_" + k, v.shape, mybir.dt.from_np(v.dtype), kind="ExternalInput").ap() for k, v in arrays.items()}
    out = nc.dram_tensor("out", (P, NSEQ, T, D), F32, kind="ExternalOutput").ap()
    program(nc, I, out)
    r = _run(nc, [{"in_" + k: v for k, v in arrays.items()}], core_ids=[0])
    return r.results[0]["out"].transpose(1, 2, 0, 3).reshape(NSEQ, L, D)
```
